# Optimizing a Trainium2 kernel written in Bass

```python
import numpy as np
import jax
import jax.numpy as jnp

def _softmax(x, axis=-1):
    return jax.nn.softmax(x, axis=axis)

def _gelu(x):
    return jax.nn.gelu(x, approximate=True)

def _silu(x):
    return jax.nn.silu(x)

def _sigmoid(x):
    return jax.nn.sigmoid(x)

def _layernorm(x, axis=-1, eps=1e-05):
    m = jnp.mean(x, axis=axis, keepdims=True)
    v = jnp.var(x, axis=axis, keepdims=True)
    return (x - m) / jnp.sqrt(v + eps)

def _scatter_add(tgt, idx, src, axis=0):
    return tgt.at[idx].add(src)

def _segment_sum(src, seg, n):
    return jax.ops.segment_sum(src, seg, n)
kernel_name = 'mk_flamingo_gated_d2_seqx_r4_1937d4'

def setup_inputs(seed: int=0):
    np.random.seed(seed)
    _w = jnp.asarray

    def _rec_inputs():
        import jax
        import jax.numpy as jnp
        _rk = jax.random.key(seed)
        x = -0.0002928 + 1 * jax.random.normal(jax.random.fold_in(_rk, 1), (16, 256, 256), jnp.float32)
        _lenS = 256 - jax.random.randint(jax.random.fold_in(_rk, 7), (16,), 0, max(1, 256 // 4) + 1, jnp.int32)
        _lenS2 = 77 - jax.random.randint(jax.random.fold_in(_rk, 8), (16,), 0, max(1, 77 // 4) + 1, jnp.int32)
        _ctx_1024P = jax.random.normal(jax.random.fold_in(_rk, 11), (16, 16, 256), jnp.float32)
        _ctx_1024c = jax.random.dirichlet(jax.random.fold_in(_rk, 511), 0.3 * jnp.ones((16,), jnp.float32), (16, 77))
        _ctx_1024t = jnp.einsum('bsk,bkd->bsd', _ctx_1024c, _ctx_1024P)
        _ctx_1024t = _ctx_1024t * jax.lax.rsqrt(jnp.mean(jnp.square(_ctx_1024t)) + 1e-12) * 0.953939
        ctx_1024 = -1.39393e-06 + 0.999914 * (_ctx_1024t + 0.3 * jax.random.normal(jax.random.fold_in(_rk, 611), (16, 77, 256), jnp.float32))
        _validS = jnp.arange(256)[None, :] < _lenS[:, None]
        _validS2 = jnp.arange(77)[None, :] < _lenS2[:, None]
        _causal = jnp.tril(jnp.ones((256, 256), dtype=bool))
        mask_1x1xSxS2_fk0 = jnp.where(jnp.broadcast_to(_validS2[0:1, None, None, :], (1, 1, 256, 77)), 0.0, 1.0).astype(jnp.float32)
        mask_BxS2_bf0 = jnp.logical_not(jnp.ones((16, 77), dtype=bool))
        _g = jax.random.normal(jax.random.fold_in(_rk, 9001), (2, 2), jnp.float32)
        _g = jnp.sign(_g) * jnp.maximum(jnp.abs(_g), 1.0) + (_g == 0) * 1.0
        g_xattn = _g[0]
        g_ffn = _g[1]
        return (x, ctx_1024, mask_1x1xSxS2_fk0, mask_BxS2_bf0, g_xattn, g_ffn)
    x, ctx_1024, mask_1x1xSxS2_fk0, mask_BxS2_bf0, g_xattn, g_ffn = _rec_inputs()

    def _L0_xattn_setup():
        import jax, jax.numpy as jnp
        import numpy as np
        B, N, H, NH = (2, 512, 256, 16)
        D = H // NH

        def _split_heads(x):
            b, n, _ = x.shape
            return x.reshape(b, n, NH, D).transpose(0, 2, 1, 3)
        key = jax.random.key(seed)
        ks = jax.random.split(key, 12)
        s = 0.02
        inp = {'q': jax.random.normal(ks[0], (B, N, H), jnp.float32), 'k': jax.random.normal(ks[1], (B, N, H), jnp.float32), 'v': jax.random.normal(ks[2], (B, N, H), jnp.float32), 'mask': jnp.tril(jnp.ones((N, N), jnp.float32))[None, None], 'Wq': jax.random.normal(ks[3], (H, H), jnp.float32) * s, 'bq': jnp.zeros((H,), jnp.float32), 'Wk': jax.random.normal(ks[4], (H, H), jnp.float32) * s, 'bk': jnp.zeros((H,), jnp.float32), 'Wv': jax.random.normal(ks[5], (H, H), jnp.float32) * s, 'bv': jnp.zeros((H,), jnp.float32), 'Wp': jax.random.normal(ks[6], (H, H), jnp.float32) * s, 'bp': jnp.zeros((H,), jnp.float32)}
        return inp
    _L0_xattn_all = _L0_xattn_setup()
    _L0_xattn_in = {k: v for k, v in _L0_xattn_all.items() if k in ('Wq', 'bq', 'Wk', 'bk', 'Wv', 'bv', 'Wp', 'bp')}
    del _L0_xattn_all

    def _L0_ffn_setup():
        import jax, jax.numpy as jnp
        import numpy as np
        from jax import lax
        D_MODEL = 256
        INTER = 256
        N_EXPERTS = 8
        TOP_K = 2
        ROUTE_SCALE = 1.0
        B, S = (2, 1024)
        key = jax.random.key(seed)
        ks = jax.random.split(key, 16)
        sc_d = 1.0 / np.sqrt(D_MODEL)
        sc_f = 1.0 / np.sqrt(INTER)
        inp = {'x': jax.random.normal(ks[0], (B, S, D_MODEL), dtype=jnp.float32), 'gate_w': jax.random.normal(ks[1], (N_EXPERTS, D_MODEL), dtype=jnp.float32) * sc_d, 'w1': jax.random.normal(ks[2], (N_EXPERTS, D_MODEL, INTER), dtype=jnp.float32) * sc_d, 'b1': jnp.zeros((N_EXPERTS, INTER), dtype=jnp.float32), 'w2': jax.random.normal(ks[3], (N_EXPERTS, INTER, D_MODEL), dtype=jnp.float32) * sc_f, 'b2': jnp.zeros((N_EXPERTS, D_MODEL), dtype=jnp.float32), 'w3': jax.random.normal(ks[4], (N_EXPERTS, D_MODEL, INTER), dtype=jnp.float32) * sc_d, 'b3': jnp.zeros((N_EXPERTS, INTER), dtype=jnp.float32), 'sw1': jax.random.normal(ks[5], (D_MODEL, INTER), dtype=jnp.float32) * sc_d, 'sb1': jnp.zeros((INTER,), dtype=jnp.float32), 'sw2': jax.random.normal(ks[6], (INTER, D_MODEL), dtype=jnp.float32) * sc_f, 'sb2': jnp.zeros((D_MODEL,), dtype=jnp.float32), 'sw3': jax.random.normal(ks[7], (D_MODEL, INTER), dtype=jnp.float32) * sc_d, 'sb3': jnp.zeros((INTER,), dtype=jnp.float32)}
        return inp
    _L0_ffn_all = _L0_ffn_setup()
    _L0_ffn_in = {k: v for k, v in _L0_ffn_all.items() if k in ('gate_w', 'w1', 'b1', 'w2', 'b2', 'w3', 'b3', 'sw1', 'sb1', 'sw2', 'sb2', 'sw3', 'sb3')}
    del _L0_ffn_all

    def _L1_xattn_setup():
        import jax, jax.numpy as jnp
        import numpy as np
        D = 256
        H = 16
        HD = D // H
        DFF = 4 * D
        EPS = 1e-05

        def _layernorm(x, g, b):
            mu = jnp.mean(x, axis=-1, keepdims=True)
            var = jnp.var(x, axis=-1, keepdims=True)
            return (x - mu) * jax.lax.rsqrt(var + EPS) * g + b
        key = jax.random.key(seed)
        ks = jax.random.split(key, 16)
        B, SQ, SK = (4, 256, 512)
        s = 1.0 / np.sqrt(D)
        inp = {'query': jax.random.normal(ks[0], (B, SQ, D), jnp.float32), 'key_value': jax.random.normal(ks[1], (B, SK, D), jnp.float32), 'key_padding_mask': jnp.zeros((B, SK), jnp.bool_), 'Wq': jax.random.normal(ks[2], (D, D), jnp.float32) * s, 'bq': jnp.zeros((D,), jnp.float32), 'Wk': jax.random.normal(ks[3], (D, D), jnp.float32) * s, 'bk': jnp.zeros((D,), jnp.float32), 'Wv': jax.random.normal(ks[4], (D, D), jnp.float32) * s, 'bv': jnp.zeros((D,), jnp.float32), 'Wo': jax.random.normal(ks[5], (D, D), jnp.float32) * s, 'bo': jnp.zeros((D,), jnp.float32), 'ln1_g': jnp.ones((D,), jnp.float32), 'ln1_b': jnp.zeros((D,), jnp.float32), 'W1': jax.random.normal(ks[6], (D, DFF), jnp.float32) * s, 'b1': jnp.zeros((DFF,), jnp.float32), 'W2': jax.random.normal(ks[7], (DFF, D), jnp.float32) * (1.0 / np.sqrt(DFF)), 'b2': jnp.zeros((D,), jnp.float32), 'ln2_g': jnp.ones((D,), jnp.float32), 'ln2_b': jnp.zeros((D,), jnp.float32)}
        return inp
    _L1_xattn_all = _L1_xattn_setup()
    _L1_xattn_in = {k: v for k, v in _L1_xattn_all.items() if k in ('Wq', 'bq', 'Wk', 'bk', 'Wv', 'bv', 'Wo', 'bo', 'ln1_g', 'ln1_b', 'W1', 'b1', 'W2', 'b2', 'ln2_g', 'ln2_b')}
    del _L1_xattn_all

    def _L1_ffn_setup():
        import jax, jax.numpy as jnp
        import numpy as np
        LN_EPS = 1e-05

        def layer_norm(x, g, b):
            mu = jnp.mean(x, axis=-1, keepdims=True)
            var = jnp.mean(jnp.square(x - mu), axis=-1, keepdims=True)
            return (x - mu) * jax.lax.rsqrt(var + LN_EPS) * g + b

        def ternary_quant(w):
            scale = 1.0 / jnp.clip(jnp.mean(jnp.abs(w)), 1e-05)
            wq = jnp.clip(jnp.round(w * scale), -1.0, 1.0) / scale
            return w + jax.lax.stop_gradient(wq - w)
        key = jax.random.key(seed)
        ks = jax.random.split(key, 3)
        dim, hidden = (256, 1024)
        B, S = (8, 256)
        x = jax.random.normal(ks[0], (B, S, dim), dtype=jnp.float32)
        w1 = jax.random.normal(ks[1], (hidden, dim), dtype=jnp.float32) * 0.02
        w2 = jax.random.normal(ks[2], (dim, hidden), dtype=jnp.float32) * 0.02
        return {'x': x, 'ln1_g': jnp.ones((dim,), jnp.float32), 'ln1_b': jnp.zeros((dim,), jnp.float32), 'w1': w1, 'b1': jnp.zeros((hidden,), jnp.float32), 'ln2_g': jnp.ones((hidden,), jnp.float32), 'ln2_b': jnp.zeros((hidden,), jnp.float32), 'w2': w2, 'b2': jnp.zeros((dim,), jnp.float32)}
    _L1_ffn_all = _L1_ffn_setup()
    _L1_ffn_in = {k: v for k, v in _L1_ffn_all.items() if k in ('ln1_g', 'ln1_b', 'w1', 'b1', 'ln2_g', 'ln2_b', 'w2', 'b2')}
    del _L1_ffn_all
    return {'x': x, 'ctx_1024': ctx_1024, 'mask_1x1xSxS2_fk0': mask_1x1xSxS2_fk0, 'mask_BxS2_bf0': mask_BxS2_bf0, 'g_xattn': g_xattn, 'g_ffn': g_ffn, 'L0_xattn_Wq': _L0_xattn_in['Wq'], 'L0_xattn_bq': _L0_xattn_in['bq'], 'L0_xattn_Wk': _L0_xattn_in['Wk'], 'L0_xattn_bk': _L0_xattn_in['bk'], 'L0_xattn_Wv': _L0_xattn_in['Wv'], 'L0_xattn_bv': _L0_xattn_in['bv'], 'L0_xattn_Wp': _L0_xattn_in['Wp'], 'L0_xattn_bp': _L0_xattn_in['bp'], 'L0_ffn_gate_w': _L0_ffn_in['gate_w'], 'L0_ffn_w1': _L0_ffn_in['w1'], 'L0_ffn_b1': _L0_ffn_in['b1'], 'L0_ffn_w2': _L0_ffn_in['w2'], 'L0_ffn_b2': _L0_ffn_in['b2'], 'L0_ffn_w3': _L0_ffn_in['w3'], 'L0_ffn_b3': _L0_ffn_in['b3'], 'L0_ffn_sw1': _L0_ffn_in['sw1'], 'L0_ffn_sb1': _L0_ffn_in['sb1'], 'L0_ffn_sw2': _L0_ffn_in['sw2'], 'L0_ffn_sb2': _L0_ffn_in['sb2'], 'L0_ffn_sw3': _L0_ffn_in['sw3'], 'L0_ffn_sb3': _L0_ffn_in['sb3'], 'L1_xattn_Wq': _L1_xattn_in['Wq'], 'L1_xattn_bq': _L1_xattn_in['bq'], 'L1_xattn_Wk': _L1_xattn_in['Wk'], 'L1_xattn_bk': _L1_xattn_in['bk'], 'L1_xattn_Wv': _L1_xattn_in['Wv'], 'L1_xattn_bv': _L1_xattn_in['bv'], 'L1_xattn_Wo': _L1_xattn_in['Wo'], 'L1_xattn_bo': _L1_xattn_in['bo'], 'L1_xattn_ln1_g': _L1_xattn_in['ln1_g'], 'L1_xattn_ln1_b': _L1_xattn_in['ln1_b'], 'L1_xattn_W1': _L1_xattn_in['W1'], 'L1_xattn_b1': _L1_xattn_in['b1'], 'L1_xattn_W2': _L1_xattn_in['W2'], 'L1_xattn_b2': _L1_xattn_in['b2'], 'L1_xattn_ln2_g': _L1_xattn_in['ln2_g'], 'L1_xattn_ln2_b': _L1_xattn_in['ln2_b'], 'L1_ffn_ln1_g': _L1_ffn_in['ln1_g'], 'L1_ffn_ln1_b': _L1_ffn_in['ln1_b'], 'L1_ffn_w1': _L1_ffn_in['w1'], 'L1_ffn_b1': _L1_ffn_in['b1'], 'L1_ffn_ln2_g': _L1_ffn_in['ln2_g'], 'L1_ffn_ln2_b': _L1_ffn_in['ln2_b'], 'L1_ffn_w2': _L1_ffn_in['w2'], 'L1_ffn_b2': _L1_ffn_in['b2']}

def reference(x, ctx_1024, mask_1x1xSxS2_fk0, mask_BxS2_bf0, g_xattn, g_ffn, L0_xattn_Wq, L0_xattn_bq, L0_xattn_Wk, L0_xattn_bk, L0_xattn_Wv, L0_xattn_bv, L0_xattn_Wp, L0_xattn_bp, L0_ffn_gate_w, L0_ffn_w1, L0_ffn_b1, L0_ffn_w2, L0_ffn_b2, L0_ffn_w3, L0_ffn_b3, L0_ffn_sw1, L0_ffn_sb1, L0_ffn_sw2, L0_ffn_sb2, L0_ffn_sw3, L0_ffn_sb3, L1_xattn_Wq, L1_xattn_bq, L1_xattn_Wk, L1_xattn_bk, L1_xattn_Wv, L1_xattn_bv, L1_xattn_Wo, L1_xattn_bo, L1_xattn_ln1_g, L1_xattn_ln1_b, L1_xattn_W1, L1_xattn_b1, L1_xattn_W2, L1_xattn_b2, L1_xattn_ln2_g, L1_xattn_ln2_b, L1_ffn_ln1_g, L1_ffn_ln1_b, L1_ffn_w1, L1_ffn_b1, L1_ffn_ln2_g, L1_ffn_ln2_b, L1_ffn_w2, L1_ffn_b2):
    import jax
    import jax.numpy as jnp

    def _L0_xattn_ref(q, k, v, mask, Wq, bq, Wk, bk, Wv, bv, Wp, bp):
        import jax, jax.numpy as jnp
        import numpy as np
        B, N, H, NH = (2, 512, 256, 16)
        D = H // NH

        def _split_heads(x):
            b, n, _ = x.shape
            return x.reshape(b, n, NH, D).transpose(0, 2, 1, 3)
        Q = _split_heads(q @ Wq.T + bq)
        K = _split_heads(k @ Wk.T + bk)
        V = _split_heads(v @ Wv.T + bv)
        scores = jnp.einsum('bhnd,bhmd->bhnm', Q, K) / jnp.sqrt(jnp.float32(D))
        scores = jnp.where(mask == 0, -jnp.inf, scores)
        attn = jax.nn.softmax(scores, axis=-1)
        out = jnp.einsum('bhnm,bhmd->bhnd', attn, V)
        out = out.transpose(0, 2, 1, 3).reshape(q.shape[0], q.shape[1], H)
        return out @ Wp.T + bp

    def _L0_ffn_ref(x, gate_w, w1, b1, w2, b2, w3, b3, sw1, sb1, sw2, sb2, sw3, sb3):
        import jax, jax.numpy as jnp
        import numpy as np
        from jax import lax
        D_MODEL = 256
        INTER = 256
        N_EXPERTS = 8
        TOP_K = 2
        ROUTE_SCALE = 1.0
        B, S = (2, 1024)
        Bx, Sx, D = x.shape
        xt = x.reshape(-1, D)
        scores = jax.nn.softmax((xt @ gate_w.T).astype(jnp.float32), axis=-1)
        top_vals, top_idx = lax.top_k(scores, TOP_K)
        weights = (top_vals * ROUTE_SCALE).astype(x.dtype)
        combine = jnp.sum(jax.nn.one_hot(top_idx, N_EXPERTS, dtype=x.dtype) * weights[..., None], axis=1)

        def body(acc, p):
            W1, B1, W2, B2, W3, B3, c = p
            h = jax.nn.silu(xt @ W1 + B1) * (xt @ W3 + B3)
            return (acc + c[:, None] * (h @ W2 + B2), None)
        y, _ = lax.scan(body, jnp.zeros_like(xt), (w1, b1, w2, b2, w3, b3, combine.T))
        z = jax.nn.silu(xt @ sw1 + sb1) * (xt @ sw3 + sb3) @ sw2 + sb2
        return (y + z).reshape(Bx, Sx, D)

    def _L1_xattn_ref(query, key_value, key_padding_mask, Wq, bq, Wk, bk, Wv, bv, Wo, bo, ln1_g, ln1_b, W1, b1, W2, b2, ln2_g, ln2_b):
        import jax, jax.numpy as jnp
        import numpy as np
        D = 256
        H = 16
        HD = D // H
        DFF = 4 * D
        EPS = 1e-05

        def _layernorm(x, g, b):
            mu = jnp.mean(x, axis=-1, keepdims=True)
            var = jnp.var(x, axis=-1, keepdims=True)
            return (x - mu) * jax.lax.rsqrt(var + EPS) * g + b
        B, SQ, _ = query.shape
        SK = key_value.shape[1]
        scale = HD ** (-0.5)
        q = (query @ Wq + bq).reshape(B, SQ, H, HD).transpose(0, 2, 1, 3)
        k = (key_value @ Wk + bk).reshape(B, SK, H, HD).transpose(0, 2, 1, 3)
        v = (key_value @ Wv + bv).reshape(B, SK, H, HD).transpose(0, 2, 1, 3)
        scores = jnp.einsum('bhqd,bhkd->bhqk', q, k) * scale
        scores = jnp.where(key_padding_mask[:, None, None, :], -jnp.inf, scores)
        attn = jax.nn.softmax(scores, axis=-1)
        attn_out = jnp.einsum('bhqk,bhkd->bhqd', attn, v)
        attn_out = attn_out.transpose(0, 2, 1, 3).reshape(B, SQ, D)
        attn_out = attn_out @ Wo + bo
        x = _layernorm(query + attn_out, ln1_g, ln1_b)
        ffn = jax.nn.gelu(x @ W1 + b1, approximate=False) @ W2 + b2
        return _layernorm(x + ffn, ln2_g, ln2_b)

    def _L1_ffn_ref(x, ln1_g, ln1_b, w1, b1, ln2_g, ln2_b, w2, b2):
        import jax, jax.numpy as jnp
        import numpy as np
        LN_EPS = 1e-05

        def layer_norm(x, g, b):
            mu = jnp.mean(x, axis=-1, keepdims=True)
            var = jnp.mean(jnp.square(x - mu), axis=-1, keepdims=True)
            return (x - mu) * jax.lax.rsqrt(var + LN_EPS) * g + b

        def ternary_quant(w):
            scale = 1.0 / jnp.clip(jnp.mean(jnp.abs(w)), 1e-05)
            wq = jnp.clip(jnp.round(w * scale), -1.0, 1.0) / scale
            return w + jax.lax.stop_gradient(wq - w)
        h = layer_norm(x, ln1_g, ln1_b)
        h = jnp.einsum('bsd,hd->bsh', h, ternary_quant(w1)) + b1
        h = jax.nn.gelu(h, approximate=False)
        h = layer_norm(h, ln2_g, ln2_b)
        out = jnp.einsum('bsh,dh->bsd', h, ternary_quant(w2)) + b2
        return out
    x = x + jnp.tanh(g_xattn[0]) * _L0_xattn_ref(_layernorm(x, axis=-1), ctx_1024, ctx_1024, mask_1x1xSxS2_fk0, L0_xattn_Wq, L0_xattn_bq, L0_xattn_Wk, L0_xattn_bk, L0_xattn_Wv, L0_xattn_bv, L0_xattn_Wp, L0_xattn_bp)
    x = x + jnp.tanh(g_ffn[0]) * _L0_ffn_ref(_layernorm(x, axis=-1), L0_ffn_gate_w, L0_ffn_w1, L0_ffn_b1, L0_ffn_w2, L0_ffn_b2, L0_ffn_w3, L0_ffn_b3, L0_ffn_sw1, L0_ffn_sb1, L0_ffn_sw2, L0_ffn_sb2, L0_ffn_sw3, L0_ffn_sb3)
    x = x + jnp.tanh(g_xattn[1]) * _L1_xattn_ref(_layernorm(x, axis=-1), ctx_1024, mask_BxS2_bf0, L1_xattn_Wq, L1_xattn_bq, L1_xattn_Wk, L1_xattn_bk, L1_xattn_Wv, L1_xattn_bv, L1_xattn_Wo, L1_xattn_bo, L1_xattn_ln1_g, L1_xattn_ln1_b, L1_xattn_W1, L1_xattn_b1, L1_xattn_W2, L1_xattn_b2, L1_xattn_ln2_g, L1_xattn_ln2_b)
    x = x + jnp.tanh(g_ffn[1]) * _L1_ffn_ref(_layernorm(x, axis=-1), L1_ffn_ln1_g, L1_ffn_ln1_b, L1_ffn_w1, L1_ffn_b1, L1_ffn_ln2_g, L1_ffn_ln2_b, L1_ffn_w2, L1_ffn_b2)
    return x

_drawn_inputs = setup_inputs


def setup_inputs(seed=0):
    import zlib

    import numpy as np

    out = dict(_drawn_inputs(seed))
    spreads = {'g_ffn': (-1.0, 0.2),
     'L0_xattn_bq': (0.0, 2.0),
     'L0_xattn_bk': (0.0, 2.0),
     'L0_xattn_bv': (0.0, 0.299),
     'L0_xattn_bp': (0.0, 0.1),
     'L0_ffn_b1': (0.0, 0.515),
     'L0_ffn_b2': (0.0, 0.319),
     'L0_ffn_b3': (0.0, 0.537),
     'L0_ffn_sb1': (0.0, 0.1),
     'L0_ffn_sb2': (0.0, 0.1),
     'L0_ffn_sb3': (0.0, 0.1),
     'L1_xattn_bq': (0.0, 0.356),
     'L1_xattn_bk': (0.0, 2.0),
     'L1_xattn_bv': (0.0, 0.1),
     'L1_xattn_bo': (0.0, 0.1),
     'L1_xattn_ln1_g': (1.0, 0.2),
     'L1_xattn_ln1_b': (0.0, 0.1),
     'L1_xattn_b1': (0.0, 0.1),
     'L1_xattn_b2': (0.0, 0.1),
     'L1_xattn_ln2_g': (1.0, 0.2),
     'L1_xattn_ln2_b': (0.0, 0.1),
     'L1_ffn_ln1_g': (1.0, 0.2),
     'L1_ffn_ln1_b': (0.0, 0.1),
     'L1_ffn_b1': (0.0, 0.1),
     'L1_ffn_ln2_g': (1.0, 0.2),
     'L1_ffn_ln2_b': (0.0, 0.1),
     'L1_ffn_b2': (0.0, 0.1)}
    factors = {'L0_xattn_Wq': 8.0, 'L0_xattn_Wk': 8.0}
    for name, (base, spread) in spreads.items():
        noise = np.random.default_rng([zlib.crc32(name.encode()), seed]).standard_normal(out[name].shape)
        drawn = base * np.exp(spread * noise) if base else spread * noise
        out[name] = jnp.asarray(drawn.astype(out[name].dtype))
    for name, factor in factors.items():
        out[name] = (out[name] * factor).astype(out[name].dtype)
    return out
```

```python
import numpy as np
from contextlib import ExitStack

import concourse.bass as bass
from concourse import mybir
from concourse.alu_op_type import AluOpType as ALU

F32 = mybir.dt.float32
F32R = mybir.dt.float32r
U8 = mybir.dt.uint8
ACT = mybir.ActivationFunctionType
AX = mybir.AxisListType

P = 128
BATCH, SEQ, DIM = 16, 256, 256
CTX = 77
CTXP = CTX + 1
HEADS, HD = 16, 16
EXPERTS = 8
KC = DIM // P
TILES = BATCH * SEQ // P
BT = SEQ // P
HPC = P // HD
VW = HD + 2
UNITS = KC * BT
MT = 4
MB = TILES // MT
MN = MT * P
HID = 1024
HC = HID // P
EPS = 1e-5
MASKED = -1e30
MATRIX = KC * DIM
EARLY = 5
EXPERT_COLS = 3 * MATRIX
LATE = EXPERTS + 1 - EARLY
LATE_CHUNK = MATRIX
LATE_CHUNKS = 3 * LATE
MOE_CHUNK = EARLY * EXPERT_COLS // BATCH
FFN_COLS = 2 * KC * HID
FFN_CHUNK = FFN_COLS // BATCH
TER_COLS = KC * HID
ROUND = 1.5 * 2 ** 23

COL_BQ, COL_BK = (0, 4), (2, 6)
COL_B1 = 8
COL_B3 = COL_B1 + KC * (EXPERTS + 1)
COL_FB1 = COL_B3 + KC * (EXPERTS + 1)
COL_G1 = COL_FB1 + HC
COL_T1 = COL_G1 + KC
COL_G2 = COL_T1 + KC
COL_T2 = COL_G2 + HC
COLS = COL_T2 + HC


def after(engine, semaphore, value):
    if not (isinstance(value, int) and value <= 0):
        engine.wait_ge(semaphore, value)


class Block:

    def __init__(self, n, parity, half, base=0):
        self.n, self.z, self.half, self.base = n, parity, half, base
        self.count = n + base

    def next(self):
        return Block(self.n + 1, 1 - self.z, self.half + self.z, self.base)

    def last(self):
        return Block(self.n - 1, 1 - self.z, self.half - (1 - self.z), self.base)


def paired_blocks(engine, count, body, base=0):
    body(Block(0, 0, 0, base), False, True)
    with engine.Fori(0, (count - 2) // 2) as i:
        body(Block(2 * i + 1, 1, i, base), True, True)
        body(Block(2 * i + 2, 0, i + 1, base), True, True)
    body(Block(count - 1, 1, (count - 2) // 2, base), True, False)

def lay_out(i):
    def chunks(w):
        return w.reshape(-1, P, w.shape[1]).transpose(1, 0, 2)

    def flat(w):
        return chunks(w).reshape(P, -1)

    def col(b):
        return b.reshape(-1, P).T

    ctx = np.zeros((BATCH, P, KC, CTXP), np.float32)
    ctx[..., :CTX] = i["ctx_1024"].transpose(0, 2, 1).reshape(BATCH, KC, P, CTX).transpose(0, 2, 1, 3)
    moe = []
    for e in range(EXPERTS):
        moe += [flat(i[f"L0_ffn_w{n}"][e]) for n in (1, 3, 2)]
    moe += [flat(i[f"L0_ffn_sw{n}"]) for n in (1, 3, 2)]
    cols = [col(i[n]) for n in ("L0_xattn_bq", "L0_xattn_bk", "L1_xattn_bq", "L1_xattn_bk")]
    for n in (1, 3):
        cols += [col(i[f"L0_ffn_b{n}"].reshape(-1)), col(i[f"L0_ffn_sb{n}"])]
    cols += [col(i[n]) for n in ("L1_xattn_b1", "L1_ffn_ln1_g", "L1_ffn_ln1_b", "L1_ffn_ln2_g", "L1_ffn_ln2_b")]
    arrays = {
        "x": i["x"],
        "ctx": ctx,
        "mask_q": i["mask_1x1xSxS2_fk0"].reshape(SEQ, CTX),
        "mask_k": i["mask_BxS2_bf0"].reshape(1, BATCH, CTX),
        "wa0": np.stack([flat(i[f"L0_xattn_W{n}"].T) for n in "qkvp"], 1),
        "wa1": np.stack([flat(i[f"L1_xattn_W{n}"]) for n in "qkvo"], 1),
        "moe_w": np.concatenate(moe, 1),
        "moe_b2": np.concatenate([i["L0_ffn_b2"], i["L0_ffn_sb2"][None]]),
        "gate_w": flat(i["L0_ffn_gate_w"].T),
        "ffn_w": np.concatenate([flat(i["L1_xattn_W1"]), flat(i["L1_xattn_W2"])], 1),
        "ter_w1": flat(i["L1_ffn_w1"].T),
        "ter_w2": flat(i["L1_ffn_w2"].T),
        "ter_g2": i["L1_ffn_ln2_g"],
        "ter_b1": i["L1_ffn_b1"][None],
        "ter_b2": i["L1_ffn_b2"],
        "cols": np.concatenate(cols, 1),
        "bv": np.stack([i["L0_xattn_bv"], i["L1_xattn_bv"]]),
        "bias": np.stack([i[n] for n in ("L0_xattn_bp", "L1_xattn_bo", "L1_xattn_b2")]),
        "norms": np.stack([i[n] for n in ("L1_xattn_ln1_g", "L1_xattn_ln1_b", "L1_xattn_ln2_g", "L1_xattn_ln2_b")]),
        "gates": np.concatenate([i["g_xattn"], i["g_ffn"]]),
    }
    return {n: np.ascontiguousarray(a) for n, a in arrays.items()}


def flamingo_kernel(nc, d, out, stages=4):
    x_dram = d["x"].rearrange("b (t p) c -> p (b t) c", p=P)
    out_dram = out.rearrange("b (t p) c -> p (b t) c", p=P)
    ctx_dram = d["ctx"]
    root = ExitStack()
    with root:
        def sb(scope, name, shape, dt=F32):
            return scope.enter_context(nc.sbuf_tensor("s_" + name, shape, dt))

        def sem(name):
            return root.enter_context(nc.semaphore(name))

        x = sb(root, "x", [P, TILES, DIM])
        ident = sb(root, "ident", [P, P])
        ones_r = sb(root, "ones_r", [P, P], F32R)
        ones = sb(root, "ones", [P, P])
        headmask = sb(root, "headmask", [P, HPC])
        neghalf = sb(root, "neghalf", [P, 8])
        eps_tile = sb(root, "eps_tile", [P, 8])
        cols = sb(root, "cols", [P, COLS])
        gates_raw = sb(root, "gates_raw", [P, 4])
        gates = sb(root, "gates", [P, 4])

        PSUM = root.enter_context(nc.psum_tensor("PSUM", [P, 8, 512], F32))

        consts_in = sem("consts_in")
        consts_done = sem("consts_done")
        pool_const = sem("pool_const")
        gates_done = sem("gates_done")

        def one(shape):
            ap = ones[:, 0:1]
            for _ in shape[2:]:
                ap = ap.unsqueeze(1)
            return ap.broadcast_to(shape)

        class AttentionSignals:
            x_in = [sem(f"a_x_in{z}") for z in range(2)]
            ctx_in = [sem(f"a_ctx_in{z}") for z in range(2)]
            w_in = [sem(f"a_w_in{i}") for i in range(4)]
            small_in = sem("a_small_in")
            bias_round = sem("a_bias_round")
            bias_split = sem("a_bias_split")
            w_round = sem("a_w_round")
            w_split = sem("a_w_split")
            mask_in = sem("a_mask_in")
            mask_done = sem("a_mask_done")
            v_ones = sem("a_v_ones")
            ctx_round = sem("a_ctx_round")
            ctx_split = sem("a_ctx_split")
            bn_done = sem("a_bn_done")
            ln_stats = sem("a_ln_stats")
            ln_eps = sem("a_ln_eps")
            ln_rstd = sem("a_ln_rstd")
            ln_done = sem("a_ln_done")
            ln_kept = sem("a_ln_kept")
            xt_ps = sem("a_xt_ps")
            x_round = sem("a_x_round")
            x_split = sem("a_x_split")
            q_ps = sem("a_q_ps")
            q_round = sem("a_q_round")
            q_split = sem("a_q_split")
            kv_ps = sem("a_kv_ps")
            kv_done = sem("a_kv_done")
            k_rounded = sem("a_k_rounded")
            k_residue = sem("a_k_residue")
            kd_done = sem("a_kd_done")
            scores_ps = sem("a_scores_ps")
            max_done = sem("a_max_done")
            scores_read = sem("a_scores_read")
            exp_done = sem("a_exp_done")
            pt_ps = sem("a_pt_ps")
            pt_done = sem("a_pt_done")
            pv_ps = sem("a_pv_ps")
            sum_done = sem("a_sum_done")
            o_done = sem("a_o_done")
            ot_ps = sem("a_ot_ps")
            o_round = sem("a_o_round")
            o_split = sem("a_o_split")
            y_ps = sem("a_y_ps")
            y_done = sem("a_y_done")
            mask_zero = sem("a_mask_zero")
            mask_cast = sem("a_mask_cast")

        class Attention(AttentionSignals):

            def __init__(self, stage, scope):
                self.stage = stage
                self.base = BATCH * stage
                n = f"a{stage}_"
                two = range(2)
                self.w_raw = sb(scope, n + "w_raw", [P, 4, MATRIX])
                self.w_hi = sb(scope, n + "w_hi", [P, 4, KC, DIM], F32R)
                self.w_lo = sb(scope, n + "w_lo", [P, 4, KC, DIM], F32R)
                self.bv = sb(scope, n + "bv", [CTXP, DIM])
                self.bias_raw = sb(scope, n + "bias_raw", [1, DIM])
                self.bias_hi = sb(scope, n + "bias_hi", [1, DIM], F32R)
                self.bias_lo = sb(scope, n + "bias_lo", [1, DIM], F32R)
                self.bq, self.bk = COL_BQ[stage], COL_BK[stage]
                self.mv = sb(scope, n + "mv", [P, BT, 2])
                self.stats = sb(scope, n + "stats", [P, BT, 6])
                self.var_eps = sb(scope, n + "var_eps", [P, BT])
                self.rstd = sb(scope, n + "rstd", [P, BT])
                self.xn = sb(scope, n + "xn", [P, BT, DIM])
                self.x_hi = sb(scope, n + "x_hi", [P, KC, SEQ], F32R)
                self.x_lo = sb(scope, n + "x_lo", [P, KC, SEQ], F32R)
                self.q_hi = [sb(scope, n + f"q_hi{z}", [P, KC, SEQ], F32R) for z in two]
                self.q_lo = [sb(scope, n + f"q_lo{z}", [P, KC, SEQ], F32R) for z in two]
                self.ctx = [sb(scope, n + f"ctx{z}", [P, KC, CTXP]) for z in two]
                self.ctx_hi = [sb(scope, n + f"ctx_hi{z}", [P, KC, CTXP], F32R) for z in two]
                self.ctx_lo = [sb(scope, n + f"ctx_lo{z}", [P, KC, CTXP], F32R) for z in two]
                self.k = sb(scope, n + "k", [P, KC, CTXP])
                self.k_round = sb(scope, n + "k_round", [P, KC, CTXP], F32R)
                self.k_rest = sb(scope, n + "k_rest", [P, KC, CTXP])
                self.kd_hi = [sb(scope, n + f"kd_hi{z}", [P, KC, HPC, CTXP], F32R) for z in two]
                self.kd_lo = [sb(scope, n + f"kd_lo{z}", [P, KC, HPC, CTXP], F32R) for z in two]
                self.v = [sb(scope, n + f"v{z}", [CTXP, HEADS, VW]) for z in two]
                self.prob = [sb(scope, n + f"prob{z}", [P, HPC, CTXP]) for z in two]
                self.row_max = [sb(scope, n + f"row_max{z}", [P, HPC]) for z in two]
                self.prob_t = [sb(scope, n + f"prob_t{z}", [CTXP, HPC, P]) for z in two]
                self.row_sum = [sb(scope, n + f"row_sum{z}", [P, HPC, 1]) for z in two]
                self.o = [sb(scope, n + f"o{z}", [P, BT, DIM]) for z in two]
                self.o_hi = sb(scope, n + "o_hi", [P, KC, SEQ], F32R)
                self.o_lo = sb(scope, n + "o_lo", [P, KC, SEQ], F32R)
                if stage == 0:
                    self.mask_raw = sb(scope, n + "mask_raw", [P, BT, CTXP])
                    self.mask = sb(scope, n + "mask", [P, BT, CTXP], F32R)
                    self.ident = sb(scope, n + "ident", [P, P], F32R)
                else:
                    self.mask_u8 = sb(scope, n + "mask_u8", [1, BATCH, CTX], U8)
                    self.mask_raw = sb(scope, n + "mask_raw", [1, BATCH, CTXP])
                    self.mask = sb(scope, n + "mask", [1, BATCH, CTXP], F32R)
                self.scores = PSUM[:, 0:4, :].rearrange("p (b c) n -> p b c n", b=2)
                self.prob_t_ps = PSUM[:, 4:6, :].rearrange("p c (h n) -> p (c h) n", n=P)
                self.o_ps = PSUM[:, 6, 0:HPC * VW].rearrange("p (h n) -> p h n", n=VW)
                self.misc = PSUM[:, 7, :]

        def tiles(b):
            return x[:, bass.ds(BT * b.n, BT), :]

        def attention_on_vector(dve, a, z_kept):
            def ln_stats(b):
                if a.stage == 0:
                    dve.wait_ge(a.x_in[b.z], 16 * (b.half + 1))
                for t in range(BT):
                    last = dve.bn_stats(a.stats[:, t, :], x[:, bass.ds(BT * b.n + t, 1), :])
                last.then_inc(a.bn_done, 1)

            def ln_aggregate(b):
                if isinstance(b.n, int):
                    dve.wait_ge(a.bn_done, b.count + 1)
                for t in range(BT):
                    last = dve.bn_aggr(a.mv[:, t, :], a.stats[:, t, :])
                last.then_inc(a.ln_stats, 1)

            def ln_apply(b):
                dve.wait_ge(a.ln_rstd, b.count + 1)
                after(dve, a.xt_ps, b.count)
                if a.stage == 1:
                    after(dve, a.ln_kept, b.n)
                for t in range(BT):
                    last = dve.tensor_scalar(a.xn[:, t, :], x[:, bass.ds(BT * b.n + t, 1), :].rearrange("p o c -> p (o c)"),
                                             a.mv[:, t, 0:1], a.rstd[:, t:t + 1], ALU.subtract, ALU.mult)
                last.then_inc(a.ln_done, 1)

            def x_residue(b):
                dve.wait_ge(a.x_round, b.count + 1)
                dve.tensor_tensor(a.x_lo[:].rearrange("p k n -> p (k n)"), a.misc,
                                  a.x_hi[:].bitcast(F32).rearrange("p k n -> p (k n)"),
                                  ALU.subtract).then_inc(a.x_split, 1)

            def q_residue(b):
                dve.wait_ge(a.q_round, b.count + 1)
                for m in range(KC):
                    last = dve.scalar_tensor_tensor(a.q_lo[b.z][:, m, :], a.misc[:, m * SEQ:(m + 1) * SEQ],
                                                    cols[:, a.bq + m:a.bq + m + 1],
                                                    a.q_hi[b.z][:, m, :].bitcast(F32), ALU.add, ALU.subtract)
                last.then_inc(a.q_split, 1)

            def keys_values(b):
                dve.wait_ge(a.kv_ps, b.count + 1)
                after(dve, a.kd_done, b.count)
                dve.tensor_tensor(a.k[:], a.misc[:, 0:KC * CTXP].rearrange("p (k n) -> p k n", k=KC),
                                  cols[:, a.bk:a.bk + KC].unsqueeze(2).broadcast_to([P, KC, CTXP]), ALU.add)
                dve.tensor_tensor(a.v[b.z][:, :, 0:HD],
                                  a.misc[0:CTXP, DIM:2 * DIM].rearrange("p (h n) -> p h n", n=HD),
                                  a.bv[:].rearrange("p (h n) -> p h n", n=HD),
                                  ALU.add).then_inc(a.kv_done, 1)

            def score_max(b, j):
                u = UNITS * b.count + j
                s = a.scores[:, j % 2, :, 0:HPC // 2 * CTXP].rearrange("p c (h n) -> p c h n", n=CTXP)
                mx = a.row_max[j % 2][:].rearrange("p (c h) -> p c h", c=2)
                dve.wait_ge(a.scores_ps, u + 1)
                dve.tensor_reduce(mx, s, AX.X, ALU.max).then_inc(a.max_done, 1)
                dve.wait_ge(a.max_done, u + 1)
                after(dve, a.pt_ps, u - 1)
                dve.tensor_tensor(a.prob[j % 2][:].rearrange("p (c h) n -> p c h n", c=2), s,
                                  mx.unsqueeze(3).broadcast_to([P, 2, HPC // 2, CTXP]),
                                  ALU.subtract).then_inc(a.scores_read, 1)

            def normalise(b, j):
                u = UNITS * b.count + j
                m, qt = j // BT, j % BT
                dve.wait_ge(a.pv_ps, u + 1)
                dve.reciprocal(a.row_sum[j % 2][:], a.o_ps[:, :, HD:HD + 1]).then_inc(a.sum_done, 1)
                dve.wait_ge(a.sum_done, u + 1)
                dve.tensor_tensor(a.o[b.z][:, qt, m * P:(m + 1) * P].rearrange("p (h n) -> p h n", n=HD),
                                  a.o_ps[:, :, 0:HD], a.row_sum[j % 2][:].broadcast_to([P, HPC, HD]),
                                  ALU.mult).then_inc(a.o_done, 1)

            def o_residue(b):
                dve.wait_ge(a.o_round, b.count + 1)
                dve.tensor_tensor(a.o_lo[:].rearrange("p k n -> p (k n)"), a.misc,
                                  a.o_hi[:].bitcast(F32).rearrange("p k n -> p (k n)"),
                                  ALU.subtract).then_inc(a.o_split, 1)

            def residual(b):
                dve.wait_ge(a.y_ps, b.count + 1)
                y = a.misc.rearrange("p (t c) -> p t c", t=BT)
                if a.stage == 0:
                    dve.scalar_tensor_tensor(tiles(b), y, gates[:, 0:1], tiles(b), ALU.mult,
                                             ALU.add).then_inc(a.y_done, 1)
                else:
                    kept = z_kept[:, bass.ds(BT * b.n, BT), :]
                    dve.wait_ge(a.ln_kept, b.n + 1)
                    dve.tensor_tensor(kept, y, kept, ALU.add).then_inc(a.y_done, 1)

            dve.wait_ge(consts_done, 1)
            dve.wait_ge(gates_done, 1)
            dve.wait_ge(a.small_in, 32 * (a.stage + 1))
            first = Block(0, 0, 0, a.base)
            ln_stats(first)
            ln_aggregate(first)
            ln_apply(first)
            keys_values(first)
            x_residue(first)
            q_residue(first)

            def body(b, behind, ahead):
                if ahead:
                    ln_stats(b.next())
                score_max(b, 0)
                if ahead:
                    ln_aggregate(b.next())
                if behind:
                    normalise(b.last(), 2)
                if ahead:
                    ln_apply(b.next())
                score_max(b, 1)
                if behind:
                    normalise(b.last(), 3)
                if ahead:
                    keys_values(b.next())
                    x_residue(b.next())
                score_max(b, 2)
                normalise(b, 0)
                if ahead:
                    q_residue(b.next())
                if behind:
                    o_residue(b.last())
                score_max(b, 3)
                normalise(b, 1)
                if behind:
                    residual(b.last())

            paired_blocks(dve, BATCH, body, a.base)
            final = Block(BATCH - 1, 1, (BATCH - 2) // 2, a.base)
            normalise(final, 2)
            normalise(final, 3)
            o_residue(final)
            residual(final)

        def attention_on_scalar(act, a):
            def x_rounded(b):
                act.wait_ge(a.xt_ps, b.count + 1)
                after(act, a.q_ps, b.count)
                act.activation(a.x_hi[:].rearrange("p k n -> p (k n)"), a.misc, ACT.Copy).then_inc(a.x_round, 1)

            def q_rounded(b):
                act.wait_ge(a.q_ps, b.count + 1)
                for m in range(KC):
                    last = act.activation(a.q_hi[b.z][:, m, :], a.misc[:, m * SEQ:(m + 1) * SEQ], ACT.Identity,
                                          bias=cols[:, a.bq + m:a.bq + m + 1])
                last.then_inc(a.q_round, 1)

            def exponential(b, j):
                act.wait_ge(a.scores_read, UNITS * b.count + j + 1)
                act.activation(a.prob[j % 2][:], a.prob[j % 2][:], ACT.Exp,
                               scale=HD ** -0.5).then_inc(a.exp_done, 1)

            def transposed(b, j):
                u = UNITS * b.count + j
                act.wait_ge(a.pt_ps, u + 1)
                after(act, a.pv_ps, u - 1)
                act.activation(a.prob_t[j % 2][:], a.prob_t_ps[0:CTXP], ACT.Copy).then_inc(a.pt_done, 1)

            def o_rounded(b):
                act.wait_ge(a.ot_ps, b.count + 1)
                act.activation(a.o_hi[:].rearrange("p k n -> p (k n)"), a.misc, ACT.Copy).then_inc(a.o_round, 1)

            act.wait_ge(consts_done, 1)
            x_rounded(Block(0, 0, 0, a.base))
            q_rounded(Block(0, 0, 0, a.base))

            def body(b, behind, ahead):
                exponential(b, 0)
                if behind:
                    transposed(b.last(), 3)
                exponential(b, 1)
                transposed(b, 0)
                if ahead:
                    x_rounded(b.next())
                exponential(b, 2)
                transposed(b, 1)
                if ahead:
                    q_rounded(b.next())
                if behind:
                    o_rounded(b.last())
                exponential(b, 3)
                transposed(b, 2)

            paired_blocks(act, BATCH, body, a.base)
            final = Block(BATCH - 1, 1, (BATCH - 2) // 2, a.base)
            transposed(final, 3)
            o_rounded(final)

        def product(pe, ps, pairs, start=True, stop=True):
            n = len(pairs)
            for i, (lh, ll, rh, rl) in enumerate(pairs):
                pe.matmul(ps, lh, rh, start=start and i == 0, stop=False, skip_group_check=not start)
                pe.matmul(ps, ll, rh, start=False, stop=False, skip_group_check=not start)
                last = pe.matmul(ps, lh, rl, start=False, stop=stop and i == n - 1, skip_group_check=not start)
            return last

        def attention_on_tensor(pe, a):
            WQ, WK, WV, WP = range(4)

            def keys_values(b):
                pe.wait_ge(a.ctx_split, b.count + 1)
                if not isinstance(b.n, int) or b.n > 0:
                    pe.wait_ge(a.scores_read, UNITS * (b.count - 1) + 1)
                for m in range(KC):
                    product(pe, a.misc[:, m * CTXP:(m + 1) * CTXP],
                            [(a.w_hi[:, WK, k, m * P:(m + 1) * P], a.w_lo[:, WK, k, m * P:(m + 1) * P],
                              a.ctx_hi[b.z][:, k, :], a.ctx_lo[b.z][:, k, :]) for k in range(KC)])
                product(pe, a.misc[0:CTXP, DIM:2 * DIM],
                        [(a.ctx_hi[b.z][:, k, :], a.ctx_lo[b.z][:, k, :], a.w_hi[:, WV, k, :], a.w_lo[:, WV, k, :])
                         for k in range(KC)]).then_inc(a.kv_ps, 1)

            def transpose_x(b):
                pe.wait_ge(a.ln_done, b.count + 1)
                pe.wait_ge(a.kv_done, b.count + 1)
                for k in range(KC):
                    for t in range(BT):
                        last = pe.transpose(a.misc[:, k * SEQ + t * P:k * SEQ + (t + 1) * P],
                                            a.xn[:, t, k * P:(k + 1) * P], ident[:])
                last.then_inc(a.xt_ps, 1)

            def queries(b):
                pe.wait_ge(a.x_split, b.count + 1)
                for m in range(KC):
                    last = product(pe, a.misc[:, m * SEQ:(m + 1) * SEQ],
                                   [(a.w_hi[:, WQ, k, m * P:(m + 1) * P], a.w_lo[:, WQ, k, m * P:(m + 1) * P],
                                     a.x_hi[:, k, :], a.x_lo[:, k, :]) for k in range(KC)])
                last.then_inc(a.q_ps, 1)

            def score(b, j):
                u = UNITS * b.count + j
                m, qt = j // BT, j % BT
                pe.wait_ge(a.kd_done, b.count + 1)
                pe.wait_ge(a.q_split, b.count + 1)
                after(pe, a.scores_read, u - 1)
                q_hi = a.q_hi[b.z][:, m, qt * P:(qt + 1) * P]
                q_lo = a.q_lo[b.z][:, m, qt * P:(qt + 1) * P]
                for c in range(2):
                    heads = slice(c * HPC // 2, (c + 1) * HPC // 2)
                    ps = a.scores[:, j % 2, c, 0:HPC // 2 * CTXP].rearrange("p (h n) -> p h n", n=CTXP)
                    product(pe, ps, [(q_hi, q_lo, a.kd_hi[b.z][:, m, heads, :], a.kd_lo[b.z][:, m, heads, :])],
                            stop=False)
                    if a.stage == 0:
                        lhs, mask = a.ident[:], a.mask[:, qt, :].unsqueeze(1)
                    else:
                        lhs, mask = ones_r[0:1, :], a.mask[:, bass.ds(b.n, 1), :]
                    last = pe.matmul(ps, lhs, mask.broadcast_to([mask.shape[0], HPC // 2, CTXP]),
                                     start=False, stop=True)
                last.then_inc(a.scores_ps, 1)

            def transpose_prob(b, j):
                u = UNITS * b.count + j
                pe.wait_ge(a.exp_done, u + 1)
                after(pe, a.pt_done, u)
                for h in range(HPC):
                    last = pe.transpose(a.prob_t_ps[0:CTXP, h, :], a.prob[j % 2][:, h, :], ident[:])
                last.then_inc(a.pt_ps, 1)

            def weigh_values(b, j):
                u = UNITS * b.count + j
                pe.wait_ge(a.pt_done, u + 1)
                after(pe, a.o_done, u)
                for h in range(HPC):
                    last = pe.matmul(a.o_ps[:, h, :], a.prob_t[j % 2][:, h, :],
                                     a.v[b.z][:, (j // BT) * HPC + h, :], start=True, stop=True)
                last.then_inc(a.pv_ps, 1)

            def transpose_o(b, ahead):
                pe.wait_ge(a.o_done, UNITS * (b.count + 1))
                if ahead:
                    pe.wait_ge(a.q_split, b.count + 3)
                else:
                    pe.wait_ge(a.y_done, b.count)
                for k in range(KC):
                    for t in range(BT):
                        last = pe.transpose(a.misc[:, k * SEQ + t * P:k * SEQ + (t + 1) * P],
                                            a.o[b.z][:, t, k * P:(k + 1) * P], ident[:])
                last.then_inc(a.ot_ps, 1)

            def project(b):
                pe.wait_ge(a.o_split, b.count + 1)
                for t in range(BT):
                    ps = a.misc[:, t * DIM:(t + 1) * DIM]
                    product(pe, ps, [(a.o_hi[:, k, t * P:(t + 1) * P], a.o_lo[:, k, t * P:(t + 1) * P],
                                      a.w_hi[:, WP, k, :], a.w_lo[:, WP, k, :]) for k in range(KC)], stop=False)
                    pe.matmul(ps, ones_r[0:1, :], a.bias_hi[:], start=False, stop=False)
                    last = pe.matmul(ps, ones_r[0:1, :], a.bias_lo[:], start=False, stop=True)
                last.then_inc(a.y_ps, 1)

            pe.wait_ge(consts_done, 1)
            pe.wait_ge(a.bias_split, a.stage + 1)
            pe.wait_ge(a.mask_done, a.stage + 1)
            pe.wait_ge(a.v_ones, 2 * (a.stage + 1))
            pe.wait_ge(a.w_split, 4 * (a.stage + 1))
            first = Block(0, 0, 0, a.base)
            keys_values(first)
            transpose_x(first)
            queries(first)

            def body(b, behind, ahead):
                score(b, 0)
                if behind:
                    weigh_values(b.last(), 2)
                    transpose_prob(b.last(), 3)
                if ahead:
                    keys_values(b.next())
                score(b, 1)
                if behind:
                    weigh_values(b.last(), 3)
                transpose_prob(b, 0)
                if ahead:
                    transpose_x(b.next())
                score(b, 2)
                weigh_values(b, 0)
                transpose_prob(b, 1)
                if ahead:
                    queries(b.next())
                score(b, 3)
                if behind:
                    transpose_o(b.last(), ahead)
                weigh_values(b, 1)
                transpose_prob(b, 2)
                if behind:
                    project(b.last())

            paired_blocks(pe, BATCH, body, a.base)
            final = Block(BATCH - 1, 1, (BATCH - 2) // 2, a.base)
            weigh_values(final, 2)
            transpose_prob(final, 3)
            weigh_values(final, 3)
            transpose_o(final, False)
            project(final)

        def attention_on_gpsimd(pool, a, z_kept, side_job):
            def split_context(b):
                pool.wait_ge(a.ctx_in[b.z], 16 * (b.half + a.base // 2 + 1))
                after(pool, a.kv_ps, b.count - 1)
                pool.tensor_tensor(a.ctx_hi[b.z][:], a.ctx[b.z][:], one([P, KC, CTXP]), ALU.mult).then_inc(a.ctx_round, 1)
                pool.wait_ge(a.ctx_round, b.count + 1)
                pool.tensor_tensor(a.ctx_lo[b.z][:], a.ctx[b.z][:], a.ctx_hi[b.z][:].bitcast(F32),
                                   ALU.subtract).then_inc(a.ctx_split, 1)

            def inverse_std(b):
                pool.wait_ge(a.ln_stats, b.count + 1)
                after(pool, a.ln_done, b.count)
                pool.tensor_tensor(a.var_eps[:], a.mv[:, :, 1], eps_tile[:, 0:BT], ALU.add).then_inc(a.ln_eps, 1)
                pool.wait_ge(a.ln_eps, b.count + 1)
                pool.tensor_tensor(a.rstd[:], a.var_eps[:], neghalf[:, 0:BT], ALU.pow).then_inc(a.ln_rstd, 1)

            def keep_query(b):
                pool.wait_ge(a.ln_done, b.count + 1)
                pool.tensor_tensor(z_kept[:, bass.ds(BT * b.n, BT), :], a.xn[:], one([P, BT, DIM]),
                                   ALU.mult).then_inc(a.ln_kept, 1)

            def diagonal_keys(b):
                pool.wait_ge(a.kv_done, b.count + 1)
                pool.tensor_tensor(a.k_round[:], a.k[:], one([P, KC, CTXP]), ALU.mult).then_inc(a.k_rounded, 1)
                pool.wait_ge(a.k_rounded, b.count + 1)
                pool.tensor_tensor(a.k_rest[:], a.k[:], a.k_round[:].bitcast(F32),
                                   ALU.subtract).then_inc(a.k_residue, 1)
                pool.wait_ge(a.k_residue, b.count + 1)
                hm = headmask[:].unsqueeze(2).broadcast_to([P, HPC, CTXP])
                for part, kd in ((a.k, a.kd_hi), (a.k_rest, a.kd_lo)):
                    for m in range(KC):
                        last = pool.tensor_tensor(kd[b.z][:, m], part[:, m, :].unsqueeze(1).broadcast_to([P, HPC, CTXP]),
                                                  hm, ALU.mult)
                last.then_inc(a.kd_done, 1)

            pool.memset(a.v[0][:], 1.0).then_inc(a.v_ones, 1)
            pool.memset(a.v[1][:], 1.0).then_inc(a.v_ones, 1)
            first = Block(0, 0, 0, a.base)
            split_context(first)
            inverse_std(first)
            if a.stage == 1:
                keep_query(first)
            diagonal_keys(first)

            def body(b, behind, ahead):
                if ahead:
                    split_context(b.next())
                    inverse_std(b.next())
                    diagonal_keys(b.next())
                    if a.stage == 1:
                        keep_query(b.next())
                side_job(b)

            paired_blocks(pool, BATCH, body, a.base)

        class TokenSignals:
            bn_done = sem("t_bn_done")
            ln_stats = sem("t_ln_stats")
            ln_rstd = sem("t_ln_rstd")
            ln_done = sem("t_ln_done")
            xt_ps = sem("t_xt_ps")
            x_round = sem("t_x_round")
            x_split = sem("t_x_split")

        class Mixture(TokenSignals):

            def __init__(self, scope):
                two = range(2)
                self.late_hi = sb(scope, "late_hi", [P, LATE * EXPERT_COLS], F32R)
                self.late_lo = sb(scope, "late_lo", [P, LATE * EXPERT_COLS], F32R)
                self.raw = [sb(scope, f"late_raw{z}", [P, LATE_CHUNK]) for z in two]
                self.gate_raw = sb(scope, "gate_raw", [P, KC, EXPERTS])
                self.gate_hi = sb(scope, "gate_hi", [P, KC, EXPERTS], F32R)
                self.gate_lo = sb(scope, "gate_lo", [P, KC, EXPERTS], F32R)
                self.b2 = sb(scope, "moe_b2", [EXPERTS + 1, DIM])
                self.stats = sb(scope, "m_stats", [P, MT, 6])
                self.mv = sb(scope, "m_mv", [P, MT, 2])
                self.var_eps = sb(scope, "m_var_eps", [P, MT])
                self.rstd = sb(scope, "m_rstd", [P, MT])
                self.xn = sb(scope, "m_xn", [P, MT, DIM])
                self.x_hi = [sb(scope, f"m_x_hi{z}", [P, KC, MN], F32R) for z in two]
                self.x_lo = [sb(scope, f"m_x_lo{z}", [P, KC, MN], F32R) for z in two]
                self.h = [sb(scope, f"m_h{z}", [P, KC, MN]) for z in two]
                self.h_hi = [sb(scope, f"m_h_hi{z}", [P, KC, MN], F32R) for z in two]
                self.h_lo = [sb(scope, f"m_h_lo{z}", [P, KC, MN], F32R) for z in two]
                self.rank = sb(scope, "m_rank", [P, EXPERTS])
                self.p = sb(scope, "m_p", [P, MT, EXPERTS])
                self.pick = sb(scope, "m_pick", [P, MT, EXPERTS])
                self.pick2 = sb(scope, "m_pick2", [P, MT, EXPERTS])
                self.rest = sb(scope, "m_rest", [P, MT, EXPERTS])
                self.top = sb(scope, "m_top", [P, MT, 1])
                self.c = sb(scope, "m_c", [P, MT, EXPERTS + 1])
                self.cg = sb(scope, "m_cg", [P, MT, EXPERTS + 1])
                self.c_t = sb(scope, "m_c_t", [EXPERTS + 1, MN])
                self.up_ps = PSUM[:, 0:2, :]
                self.gate_ps = PSUM[:, 2:4, :]
                self.y_ps_bank = PSUM[:, 4:6, :].rearrange("p b (t c) -> p (b t) c", c=DIM)
                self.xt_bank = PSUM[:, 6:8, :]
                self.logits = PSUM[:, 6, 0:MT * EXPERTS].rearrange("p (t e) -> p t e", e=EXPERTS)
                self.ct_bank = PSUM[0:EXPERTS + 1, 7, :]
                self.raw_in = [sem(f"m_raw_in{z}") for z in two]
                self.small_in = sem("m_small_in")
                self.const_done = sem("m_const_done")
                self.gate_round = sem("m_gate_round")
                self.gate_split = sem("m_gate_split")
                self.late_round = sem("m_late_round")
                self.late_split = sem("m_late_split")
                self.ln_eps = sem("m_ln_eps")
                self.logits_ps = sem("m_logits_ps")
                self.logits_read = sem("m_logits_read")
                self.gate_exp = sem("m_gate_exp")
                self.route = sem("m_route")
                self.c_done = sem("m_c_done")
                self.cg_done = sem("m_cg_done")
                self.top_done = sem("m_top_done")
                self.ct_ps = sem("m_ct_ps")
                self.ct_done = sem("m_ct_done")
                self.up_done = sem("m_up_done")
                self.silu_done = sem("m_silu_done")
                self.gated = sem("m_gated")
                self.h_round = sem("m_h_round")
                self.h_split = sem("m_h_split")
                self.y_ps = sem("m_y_ps")
                self.y_added = sem("m_y_added")

            def weights(self, e):
                hi, lo = (moe_hi, moe_lo) if e < EARLY else (self.late_hi, self.late_lo)
                at = (e if e < EARLY else e - EARLY) * EXPERT_COLS

                def part(w, n):
                    return w[:, at + n * MATRIX:at + (n + 1) * MATRIX].rearrange("p (k c) -> p k c", k=KC)
                return [(part(hi, n), part(lo, n)) for n in range(3)]

        NE = EXPERTS + 1

        def mixture_on_sync(sp, m):
            sp.wait_ge(a0.y_done, BATCH)
            sp.wait_ge(side_split, BATCH)
            sp.dma_start(m.gate_raw[:].rearrange("p k e -> p (k e)"), d["gate_w"]).then_inc(m.small_in, 16)
            sp.dma_start(m.b2[:], d["moe_b2"]).then_inc(m.small_in, 16)
            for n in range(LATE_CHUNKS):
                if n >= 2:
                    sp.wait_ge(m.late_split, n - 1)
                at = EARLY * EXPERT_COLS + n * LATE_CHUNK
                sp.dma_start(m.raw[n % 2][:], d["moe_w"][:, at:at + LATE_CHUNK]).then_inc(m.raw_in[n % 2], 16)

        def mixture_on_gpsimd(pool, m):
            pool.wait_ge(a0.y_done, BATCH)
            for e in range(EXPERTS):
                last = pool.memset(m.rank[:, e:e + 1], float(EXPERTS - e))
            last.then_inc(m.const_done, 1)
            pool.memset(m.c[:], 1.0).then_inc(m.const_done, 1)

            def inverse_std(b):
                pool.wait_ge(m.ln_stats, b.n + 1)
                after(pool, m.ln_done, b.n)
                pool.tensor_tensor(m.var_eps[:], m.mv[:, :, 1], eps_tile[:, 0:MT], ALU.add).then_inc(m.ln_eps, 1)
                pool.wait_ge(m.ln_eps, b.n + 1)
                pool.tensor_tensor(m.rstd[:], m.var_eps[:], neghalf[:, 0:MT], ALU.pow).then_inc(m.ln_rstd, 1)

            def hidden_residue(b, e):
                for k in range(KC):
                    n = KC * (NE * b.n + e) + k + 1
                    z = (b.z + e) % 2
                    pool.wait_ge(m.h_round, n)
                    pool.tensor_tensor(m.h_lo[z][:, k], m.h[z][:, k], m.h_hi[z][:, k].bitcast(F32),
                                       ALU.subtract).then_inc(m.h_split, 1)

            inverse_std(Block(0, 0, 0))

            def body(b, behind, ahead):
                for e in range(NE):
                    hidden_residue(b, e)
                    if e == 3 and ahead:
                        inverse_std(b.next())

            paired_blocks(pool, MB, body)

        def mixture_on_scalar(act, m):
            act.wait_ge(a0.y_done, BATCH)
            act.wait_ge(m.small_in, 32)
            act.activation(m.gate_hi[:], m.gate_raw[:], ACT.Copy).then_inc(m.gate_round, 1)

            def x_rounded(b):
                act.wait_ge(m.xt_ps, b.n + 1)
                act.activation(m.x_hi[b.z][:], m.xt_bank, ACT.Copy).then_inc(m.x_round, 1)

            def late_rounded(n):
                act.wait_ge(m.raw_in[n % 2], 16 * (n // 2 + 1))
                act.activation(m.late_hi[:, n * LATE_CHUNK:(n + 1) * LATE_CHUNK], m.raw[n % 2][:],
                               ACT.Copy).then_inc(m.late_round, 1)

            def activate(b, e):
                z = (b.z + e) % 2
                at = NE * b.n + e
                for k in range(KC):
                    act.wait_ge(m.up_done, KC * at + k + 1)
                    after(act, m.h_split, KC * (at - 2) + k + 1)
                    col = COL_B1 + KC * e + k
                    act.activation(m.h[z][:, k], m.up_ps[:, k], ACT.Silu,
                                   bias=cols[:, col:col + 1]).then_inc(m.silu_done, 1)
                for k in range(KC):
                    act.wait_ge(m.gated, KC * at + k + 1)
                    after(act, m.y_ps, at - 1)
                    act.activation(m.h_hi[z][:, k], m.h[z][:, k], ACT.Copy).then_inc(m.h_round, 1)

            x_rounded(Block(0, 0, 0))

            def body(b, behind, ahead):
                act.wait_ge(m.logits_read, b.n + 1)
                act.activation(m.p[:], m.p[:], ACT.Exp).then_inc(m.gate_exp, 1)
                for e in range(NE):
                    activate(b, e)
                    if e == 1:
                        act.wait_ge(m.ct_ps, b.n + 1)
                        after(act, m.y_ps, NE * b.n)
                        act.activation(m.c_t[:], m.ct_bank, ACT.Copy).then_inc(m.ct_done, 1)
                    if not behind and 0 < e <= LATE:
                        for n in range(3):
                            late_rounded(3 * (e - 1) + n)
                if ahead:
                    x_rounded(b.next())

            paired_blocks(act, MB, body)

        def mixture_on_vector(dve, m):
            def ln_stats(b):
                for t in range(MT):
                    last = dve.bn_stats(m.stats[:, t, :], x[:, bass.ds(MT * b.n + t, 1), :])
                last.then_inc(m.bn_done, 1)

            def ln_aggregate(b):
                if isinstance(b.n, int):
                    dve.wait_ge(m.bn_done, b.n + 1)
                for t in range(MT):
                    last = dve.bn_aggr(m.mv[:, t, :], m.stats[:, t, :])
                last.then_inc(m.ln_stats, 1)

            def ln_apply(b):
                dve.wait_ge(m.ln_rstd, b.n + 1)
                after(dve, m.xt_ps, b.n)
                for t in range(MT):
                    last = dve.tensor_scalar(m.xn[:, t, :], x[:, bass.ds(MT * b.n + t, 1), :].rearrange("p o c -> p (o c)"),
                                             m.mv[:, t, 0:1], m.rstd[:, t:t + 1], ALU.subtract, ALU.mult)
                last.then_inc(m.ln_done, 1)

            def x_residue(b):
                dve.wait_ge(m.x_round, b.n + 1)
                dve.tensor_tensor(m.x_lo[b.z][:], m.xt_bank, m.x_hi[b.z][:].bitcast(F32),
                                  ALU.subtract).then_inc(m.x_split, 1)

            def late_residue(n):
                dve.wait_ge(m.late_round, n + 1)
                part = slice(n * LATE_CHUNK, (n + 1) * LATE_CHUNK)
                dve.tensor_tensor(m.late_lo[:, part], m.raw[n % 2][:], m.late_hi[:, part].bitcast(F32),
                                  ALU.subtract).then_inc(m.late_split, 1)

            ROUTE_STEPS = 15

            def route(b):
                wide = [P, MT, EXPERTS]
                top = m.top[:].broadcast_to(wide)
                rank = m.rank[:].unsqueeze(1).broadcast_to(wide)
                count = [0]

                def step(instruction):
                    count[0] += 1
                    instruction.then_inc(m.route, 1)
                    dve.wait_ge(m.route, ROUTE_STEPS * b.n + count[0])

                def largest(pick, values):
                    step(dve.tensor_reduce(m.top[:, :, 0], values, AX.X, ALU.max))
                    step(dve.tensor_tensor(pick[:], values, top, ALU.is_ge))
                    step(dve.tensor_tensor(pick[:], pick[:], rank, ALU.mult))
                    step(dve.tensor_reduce(m.top[:, :, 0], pick[:], AX.X, ALU.max))
                    step(dve.tensor_tensor(pick[:], pick[:], top, ALU.is_equal))

                step(dve.tensor_reduce(m.top[:, :, 0], m.p[:], AX.X, ALU.add))
                step(dve.reciprocal(m.top[:], m.top[:]))
                step(dve.tensor_tensor(m.p[:], m.p[:], top, ALU.mult))
                largest(m.pick, m.p[:])
                step(dve.scalar_tensor_tensor(m.rest[:], m.pick[:], -2.0, m.p[:], ALU.mult, ALU.add))
                largest(m.pick2, m.rest[:])
                assert count[0] == ROUTE_STEPS - 1
                step(dve.tensor_tensor(m.pick[:], m.pick[:], m.pick2[:], ALU.add))
                dve.tensor_tensor(m.c[:, :, 0:EXPERTS], m.p[:], m.pick[:], ALU.mult).then_inc(m.c_done, 1)
                dve.wait_ge(m.c_done, b.n + 1)
                after(dve, m.y_added, NE * b.n)
                dve.tensor_scalar(m.cg[:], m.c[:], gates[:, 2:3], None, ALU.mult).then_inc(m.cg_done, 1)

            def gate(b, e):
                z = (b.z + e) % 2
                for k in range(KC):
                    n = KC * (NE * b.n + e) + k + 1
                    dve.wait_ge(m.silu_done, n)
                    col = COL_B3 + KC * e + k
                    dve.scalar_tensor_tensor(m.h[z][:, k], m.gate_ps[:, k], cols[:, col:col + 1], m.h[z][:, k],
                                             ALU.add, ALU.mult).then_inc(m.gated, 1)

            def add(b, e):
                dve.wait_ge(m.y_ps, NE * b.n + e + 1)
                after(dve, m.y_added, NE * b.n + e)
                if e == 0:
                    dve.wait_ge(m.cg_done, b.n + 1)
                for t in range(MT):
                    xt = x[:, bass.ds(MT * b.n + t, 1), :].rearrange("p o c -> p (o c)")
                    last = dve.scalar_tensor_tensor(xt, m.y_ps_bank[:, t], m.cg[:, t, e:e + 1], xt, ALU.mult, ALU.add)
                last.then_inc(m.y_added, 1)

            dve.wait_ge(a0.y_done, BATCH)
            dve.wait_ge(m.gate_round, 1)
            dve.tensor_tensor(m.gate_lo[:], m.gate_raw[:], m.gate_hi[:].bitcast(F32), ALU.subtract).then_inc(m.gate_split, 1)
            dve.wait_ge(m.const_done, 2)
            first = Block(0, 0, 0)
            ln_stats(first)
            ln_aggregate(first)
            ln_apply(first)
            x_residue(first)

            def body(b, behind, ahead):
                if behind:
                    add(b.last(), NE - 1)
                dve.wait_ge(m.logits_ps, b.n + 1)
                if behind:
                    dve.wait_ge(m.ct_done, b.n)
                dve.tensor_reduce(m.top[:, :, 0], m.logits, AX.X, ALU.max).then_inc(m.top_done, 1)
                dve.wait_ge(m.top_done, b.n + 1)
                dve.tensor_tensor(m.p[:], m.logits, m.top[:].broadcast_to([P, MT, EXPERTS]),
                                  ALU.subtract).then_inc(m.logits_read, 1)
                gate(b, 0)
                dve.wait_ge(m.gate_exp, b.n + 1)
                route(b)
                for e in range(1, NE):
                    gate(b, e)
                    if e == 2 and ahead:
                        ln_stats(b.next())
                    add(b, e - 1)
                    if not behind and e <= LATE:
                        for n in range(3):
                            late_residue(3 * (e - 1) + n)
                    if e == 3 and ahead:
                        ln_aggregate(b.next())
                    if e == 5 and ahead:
                        ln_apply(b.next())
                if ahead:
                    x_residue(b.next())

            paired_blocks(dve, MB, body)
            final = Block(MB - 1, 1, (MB - 2) // 2)
            add(final, NE - 1)

        def mixture_on_tensor(pe, m):
            def transpose_x(b):
                pe.wait_ge(m.ln_done, b.n + 1)
                after(pe, m.ct_done, b.n)
                for k in range(KC):
                    for t in range(MT):
                        last = pe.transpose(m.xt_bank[:, k, t * P:(t + 1) * P], m.xn[:, t, k * P:(k + 1) * P], ident[:])
                last.then_inc(m.xt_ps, 1)

            def logits(b):
                pe.wait_ge(m.x_split, b.n + 1)
                for t in range(MT):
                    part = slice(t * P, (t + 1) * P)
                    last = product(pe, m.logits[:, t, :], [(m.x_hi[b.z][:, k, part], m.x_lo[b.z][:, k, part],
                                                            m.gate_hi[:, k], m.gate_lo[:, k]) for k in range(KC)])
                last.then_inc(m.logits_ps, 1)

            def up(b, e):
                (w1h, w1l), (w3h, w3l), _ = m.weights(e)
                xs = [(m.x_hi[b.z][:, k], m.x_lo[b.z][:, k]) for k in range(KC)]
                for o in range(KC):
                    part = slice(o * P, (o + 1) * P)
                    after(pe, m.gated, KC * (NE * b.n + e - 1) + o + 1)
                    product(pe, m.up_ps[:, o], [(w1h[:, k, part], w1l[:, k, part], *xs[k]) for k in range(KC)])
                    product(pe, m.gate_ps[:, o], [(w3h[:, k, part], w3l[:, k, part], *xs[k])
                                                  for k in range(KC)]).then_inc(m.up_done, 1)

            def down(b, e):
                _, _, (w2h, w2l) = m.weights(e)
                at = NE * b.n + e
                z = (b.z + e) % 2
                pe.wait_ge(m.h_split, KC * (at + 1))
                after(pe, m.y_added, at)
                for t in range(MT):
                    part = slice(t * P, (t + 1) * P)
                    shared = e == NE - 1
                    last = product(pe, m.y_ps_bank[:, t], [(m.h_hi[z][:, k, part], m.h_lo[z][:, k, part], w2h[:, k], w2l[:, k])
                                                           for k in range(KC)], stop=not shared)
                    if shared:
                        last = pe.matmul(m.y_ps_bank[:, t], m.c_t[:, part], m.b2[:], start=False, stop=True)
                last.then_inc(m.y_ps, 1)

            pe.wait_ge(m.gate_split, 1)
            transpose_x(Block(0, 0, 0))

            def body(b, behind, ahead):
                logits(b)
                up(b, 0)
                for e in range(1, NE):
                    if not behind and e >= EARLY:
                        pe.wait_ge(m.late_split, 3 * (e - EARLY + 1))
                    up(b, e)
                    if e == 1:
                        pe.wait_ge(m.c_done, b.n + 1)
                        for t in range(MT):
                            last = pe.transpose(m.ct_bank[:, t * P:(t + 1) * P], m.c[:, t, :], ident[:])
                        last.then_inc(m.ct_ps, 1)
                    if e == NE - 1:
                        down(b, e - 1)
                        if ahead:
                            transpose_x(b.next())
                    else:
                        down(b, e - 1)
                pe.wait_ge(m.ct_done, b.n + 1)
                down(b, NE - 1)

            paired_blocks(pe, MB, body)

        class FeedForward(TokenSignals):

            def __init__(self, scope):
                two, four = range(2), range(4)
                self.norms = sb(scope, "f_norms", [P, 4, DIM])
                self.out_g = sb(scope, "f_out_g", [P, DIM])
                self.out_b = sb(scope, "f_out_b", [P, DIM])
                self.bias_raw = sb(scope, "f_bias_raw", [1, DIM])
                self.bias_hi = sb(scope, "f_bias_hi", [1, DIM], F32R)
                self.bias_lo = sb(scope, "f_bias_lo", [1, DIM], F32R)
                self.stats1 = sb(scope, "f_stats1", [P, MT, 6])
                self.stats2 = sb(scope, "f_stats2", [P, MT, 6])
                self.mv1 = sb(scope, "f_mv1", [P, MT, 2])
                self.mv2 = sb(scope, "f_mv2", [P, MT, 2])
                self.var1 = sb(scope, "f_var1", [P, MT])
                self.var2 = sb(scope, "f_var2", [P, MT])
                self.rstd1 = sb(scope, "f_rstd1", [P, MT])
                self.rstd2 = sb(scope, "f_rstd2", [P, MT])
                self.x1 = [sb(scope, f"f_x1{z}", [P, MT, DIM]) for z in two]
                self.y = sb(scope, "f_y", [P, MT, DIM])
                self.x_hi = [sb(scope, f"f_x_hi{z}", [P, KC, MN], F32R) for z in two]
                self.x_lo = [sb(scope, f"f_x_lo{z}", [P, KC, MN], F32R) for z in two]
                self.h = [sb(scope, f"f_h{z}", [P, MN]) for z in four]
                self.h_hi = [sb(scope, f"f_h_hi{z}", [P, MN], F32R) for z in four]
                self.h_lo = [sb(scope, f"f_h_lo{z}", [P, MN], F32R) for z in four]
                self.up_ps = PSUM[:, 0:4, :]
                self.y_ps_bank = PSUM[:, 4:6, :]
                self.xt_bank = PSUM[:, 6:8, :]
                self.base = MB
                self.small_in = sem("f_small_in")
                self.const_done = sem("f_const_done")
                self.bias_round = sem("f_bias_round")
                self.bias_split = sem("f_bias_split")
                self.y_sum = sem("f_y_sum")
                self.bn2_done = sem("f_bn2_done")
                self.agg2_done = sem("f_agg2_done")
                self.ln2_stats = sem("f_ln2_stats")
                self.agg1_done = sem("f_agg1_done")
                self.ln2_rstd = sem("f_ln2_rstd")
                self.ln2_done = sem("f_ln2_done")
                self.out_scaled = sem("f_out_scaled")
                self.out_ready = sem("f_out_ready")
                self.x_done = sem("f_x_done")
                self.x1_scaled = sem("f_x1_scaled")
                self.x1_done = sem("f_x1_done")
                self.up_done = sem("f_up_done")
                self.gelu_done = sem("f_gelu_done")
                self.h_round = sem("f_h_round")
                self.h_split = sem("f_h_split")
                self.y_ps = sem("f_y_ps")

        def ffn_on_scalar(act, f):
            act.wait_ge(a1.y_done, 2 * BATCH)
            act.wait_ge(side_split, 2 * BATCH)
            act.dma_start(f.norms[:].rearrange("p r c -> p (r c)"),
                          d["norms"].rearrange("r c -> (r c)").partition_broadcast(P)).then_inc(f.small_in, 16)
            act.dma_start(f.bias_raw[:], d["bias"][2:3]).then_inc(f.small_in, 16)
            act.wait_ge(f.small_in, 32)
            act.activation(f.bias_hi[:], f.bias_raw[:], ACT.Copy).then_inc(f.bias_round, 1)
            act.activation(f.out_g[:], f.norms[:, 2], ACT.Copy, scale=gates[:, 1:2])
            act.activation(f.out_b[:], f.norms[:, 3], ACT.Copy, scale=gates[:, 1:2]).then_inc(f.const_done, 1)

            def x_rounded(b):
                act.wait_ge(f.xt_ps, b.count + 1)
                act.activation(f.x_hi[b.z][:], f.xt_bank, ACT.Copy).then_inc(f.x_round, 1)

            x_rounded(Block(0, 0, 0, f.base))

            def body(b, behind, ahead):
                for m in range(HC):
                    at = HC * b.n + m
                    act.wait_ge(f.up_done, at + 1)
                    after(act, f.h_split, at - 3)
                    act.activation(f.h[m % 4][:], f.up_ps[:, m % 4], ACT.Gelu,
                                   bias=cols[:, COL_FB1 + m:COL_FB1 + m + 1]).then_inc(f.gelu_done, 1)
                    act.wait_ge(f.gelu_done, at + 1)
                    act.activation(f.h_hi[m % 4][:], f.h[m % 4][:], ACT.Copy).then_inc(f.h_round, 1)
                    if m == HC - 1 and ahead:
                        x_rounded(b.next())
                if not ahead:
                    ternary_rows_on_scalar(act, w)

            paired_blocks(act, MB, body, f.base)

        def ffn_on_gpsimd(pool, f):
            pool.wait_ge(f.const_done, 1)

            def norm_1(b):
                pool.wait_ge(f.ln_stats, b.count + 1)
                pool.tensor_tensor(f.rstd1[:], f.var1[:], neghalf[:, 0:MT], ALU.pow).then_inc(f.ln_rstd, 1)

            def affine_1(b):
                pool.wait_ge(f.ln_done, b.count + 1)
                pool.tensor_tensor(f.x1[b.z][:], f.x1[b.z][:], f.norms[:, 0:1].broadcast_to([P, MT, DIM]),
                                   ALU.mult).then_inc(f.x1_scaled, 1)
                pool.wait_ge(f.x1_scaled, b.n + 1)
                pool.tensor_tensor(f.x1[b.z][:], f.x1[b.z][:], f.norms[:, 1:2].broadcast_to([P, MT, DIM]),
                                   ALU.add).then_inc(f.x1_done, 1)

            def norm_2(b):
                pool.wait_ge(f.ln2_stats, b.n + 1)
                pool.tensor_tensor(f.rstd2[:], f.var2[:], neghalf[:, 0:MT], ALU.pow).then_inc(f.ln2_rstd, 1)

            def affine_2(b):
                pool.wait_ge(f.ln2_done, b.n + 1)
                pool.tensor_tensor(f.y[:], f.y[:], f.out_g[:].unsqueeze(1).broadcast_to([P, MT, DIM]),
                                   ALU.mult).then_inc(f.out_scaled, 1)
                pool.wait_ge(f.out_scaled, b.n + 1)
                pool.tensor_tensor(f.y[:], f.y[:], f.out_b[:].unsqueeze(1).broadcast_to([P, MT, DIM]),
                                   ALU.add).then_inc(f.out_ready, 1)

            norm_1(Block(0, 0, 0, f.base))
            affine_1(Block(0, 0, 0, f.base))

            def body(b, behind, ahead):
                for m in range(HC):
                    at = HC * b.n + m
                    if m == 1 and behind:
                        norm_2(b.last())
                    if m == 1 and ahead:
                        norm_1(b.next())
                    if m == 2 and ahead:
                        affine_1(b.next())
                    if m == 4 and behind:
                        affine_2(b.last())
                    pool.wait_ge(f.h_round, at + 1)
                    pool.tensor_tensor(f.h_lo[m % 4][:], f.h[m % 4][:], f.h_hi[m % 4][:].bitcast(F32),
                                       ALU.subtract).then_inc(f.h_split, 1)

            paired_blocks(pool, MB, body, f.base)
            final = Block(MB - 1, 1, (MB - 2) // 2, f.base)
            norm_2(final)
            affine_2(final)

        def ffn_on_vector(dve, f):
            def stats_1(b):
                for t in range(MT):
                    last = dve.bn_stats(f.stats1[:, t, :], z_sum[:, bass.ds(MT * b.n + t, 1), :])
                last.then_inc(f.bn_done, 1)

            def aggregate_1(b):
                if isinstance(b.n, int):
                    dve.wait_ge(f.bn_done, b.count + 1)
                for t in range(MT):
                    last = dve.bn_aggr(f.mv1[:, t, :], f.stats1[:, t, :])
                last.then_inc(f.agg1_done, 1)
                dve.wait_ge(f.agg1_done, b.n + 1)
                dve.tensor_scalar(f.var1[:], f.mv1[:, :, 1], EPS, None, ALU.add).then_inc(f.ln_stats, 1)

            def apply_1(b):
                dve.wait_ge(f.ln_rstd, b.count + 1)
                after(dve, f.y_sum, b.n - 1)
                for t in range(MT):
                    last = dve.tensor_scalar(f.x1[b.z][:, t, :], z_sum[:, bass.ds(MT * b.n + t, 1), :].rearrange("p o c -> p (o c)"),
                                             f.mv1[:, t, 0:1], f.rstd1[:, t:t + 1], ALU.subtract, ALU.mult)
                last.then_inc(f.ln_done, 1)

            def x_residue(b):
                dve.wait_ge(f.x_round, b.count + 1)
                dve.tensor_tensor(f.x_lo[b.z][:], f.xt_bank, f.x_hi[b.z][:].bitcast(F32),
                                  ALU.subtract).then_inc(f.x_split, 1)

            def sums(b):
                dve.wait_ge(f.y_ps, b.n + 1)
                if isinstance(b.n, int):
                    after(dve, f.x_done, b.n)
                else:
                    dve.wait_ge(f.x_split, b.count + 2)
                dve.tensor_tensor(f.y[:].rearrange("p t c -> p (t c)"), f.y_ps_bank.rearrange("p b n -> p (b n)"),
                                  f.x1[b.z][:].rearrange("p t c -> p (t c)"), ALU.add).then_inc(f.y_sum, 1)
                dve.wait_ge(f.y_sum, b.n + 1)
                for t in range(MT):
                    last = dve.bn_stats(f.stats2[:, t, :], f.y[:, t])
                last.then_inc(f.bn2_done, 1)

            def aggregate_2(b, covered):
                if not covered:
                    dve.wait_ge(f.bn2_done, b.n + 1)
                for t in range(MT):
                    last = dve.bn_aggr(f.mv2[:, t, :], f.stats2[:, t, :])
                last.then_inc(f.agg2_done, 1)
                dve.wait_ge(f.agg2_done, b.n + 1)
                dve.tensor_scalar(f.var2[:], f.mv2[:, :, 1], EPS, None, ALU.add).then_inc(f.ln2_stats, 1)

            def apply_2(b):
                dve.wait_ge(f.ln2_rstd, b.n + 1)
                for t in range(MT):
                    last = dve.tensor_scalar(f.y[:, t], f.y[:, t], f.mv2[:, t, 0:1], f.rstd2[:, t:t + 1],
                                             ALU.subtract, ALU.mult)
                last.then_inc(f.ln2_done, 1)

            def residual(b):
                dve.wait_ge(f.out_ready, b.n + 1)
                xb = x[:, bass.ds(MT * b.n, MT), :]
                dve.tensor_tensor(xb, xb, f.y[:], ALU.add).then_inc(f.x_done, 1)

            dve.wait_ge(f.bias_round, 1)
            dve.tensor_tensor(f.bias_lo[:], f.bias_raw[:], f.bias_hi[:].bitcast(F32), ALU.subtract).then_inc(f.bias_split, 1)
            dve.wait_ge(a1.y_done, 2 * BATCH)
            first = Block(0, 0, 0, f.base)
            stats_1(first)
            aggregate_1(first)
            apply_1(first)
            x_residue(first)

            def body(b, behind, ahead):
                if behind:
                    sums(b.last())
                if ahead:
                    if behind:
                        dve.wait_ge(f.bn2_done, b.n)
                    stats_1(b.next())
                if behind:
                    aggregate_2(b.last(), ahead)
                if ahead:
                    aggregate_1(b.next())
                    apply_1(b.next())
                if behind:
                    apply_2(b.last())
                    residual(b.last())
                if not behind:
                    ternary_weights_on_vector(dve, w)
                if ahead:
                    x_residue(b.next())
                else:
                    ternary_rows_on_vector(dve, w)

            paired_blocks(dve, MB, body, f.base)
            final = Block(MB - 1, 1, (MB - 2) // 2, f.base)
            sums(final)
            aggregate_2(final, False)
            apply_2(final)
            residual(final)

        def ffn_on_tensor(pe, f):
            w1 = [both[:, 0:KC * HID].rearrange("p (k n) -> p k n", k=KC) for both in (ffn_hi, ffn_lo)]
            w2 = [both[:, KC * HID:].rearrange("p (k n) -> p k n", k=HC) for both in (ffn_hi, ffn_lo)]

            def transpose_x(b):
                pe.wait_ge(f.x1_done, b.n + 1)
                after(pe, f.x_split, b.count)
                for k in range(KC):
                    for t in range(MT):
                        last = pe.transpose(f.xt_bank[:, k, t * P:(t + 1) * P], f.x1[b.z][:, t, k * P:(k + 1) * P], ident[:])
                last.then_inc(f.xt_ps, 1)

            def up(b, m):
                part = slice(m * P, (m + 1) * P)
                pe.wait_ge(f.x_split, b.count + 1)
                after(pe, f.gelu_done, HC * b.n + m - 3)
                product(pe, f.up_ps[:, m % 4], [(w1[0][:, k, part], w1[1][:, k, part], f.x_hi[b.z][:, k], f.x_lo[b.z][:, k])
                                                for k in range(KC)]).then_inc(f.up_done, 1)

            def down(b, m):
                if m == 0:
                    after(pe, f.y_sum, b.n)
                    for half in range(2):
                        for n, part in enumerate((f.bias_hi, f.bias_lo)):
                            pe.matmul(f.y_ps_bank[:, half].rearrange("p (t c) -> p t c", c=DIM), ones_r[0:1, :],
                                      part[:].unsqueeze(1).broadcast_to([1, 2, DIM]), start=n == 0, stop=False,
                                      skip_group_check=True)
                pe.wait_ge(f.h_split, HC * b.n + m + 1)
                for t in range(MT):
                    part = slice(t * P, (t + 1) * P)
                    last = product(pe, f.y_ps_bank[:, t // 2, t % 2 * DIM:(t % 2 + 1) * DIM],
                                   [(f.h_hi[m % 4][:, part], f.h_lo[m % 4][:, part], w2[0][:, m], w2[1][:, m])],
                                   start=False, stop=m == HC - 1)
                if m == HC - 1:
                    last.then_inc(f.y_ps, 1)

            pe.wait_ge(side_split, 2 * BATCH)
            pe.wait_ge(f.bias_split, 1)
            transpose_x(Block(0, 0, 0, f.base))

            def body(b, behind, ahead):
                up(b, 0)
                up(b, 1)
                for m in range(2, HC):
                    up(b, m)
                    down(b, m - 2)
                if not behind:
                    ternary_weights_on_tensor(pe, w)
                    pe.wait_ge(w.size_done, 1)
                if ahead:
                    transpose_x(b.next())
                down(b, HC - 2)
                down(b, HC - 1)

            paired_blocks(pe, MB, body, f.base)

        class Ternary(TokenSignals):

            def __init__(self, scope):
                self.raw = sb(scope, "t_raw", [P, 2, TER_COLS])
                self.code = sb(scope, "t_code", [P, 2, TER_COLS], F32R)
                self.rows_hi = sb(scope, "t_rows_hi", [P, 2, HC, P], F32R)
                self.rows_lo = sb(scope, "t_rows_lo", [P, 2, HC, P], F32R)
                self.sums = sb(scope, "t_sums", [P, 2])
                self.size = sb(scope, "t_size", [P, 2])
                self.scale = sb(scope, "t_scale", [P, 2])
                self.gate = sb(scope, "t_gate", [P, 1])
                self.neg_gate = sb(scope, "t_neg_gate", [P, 1])
                self.base = 2 * MB
                self.raw_in = sem("r_raw_in")
                self.small_in = sem("r_small_in")
                self.sums_done = sem("r_sums_done")
                self.total_ps = sem("r_total_ps")
                self.size_done = sem("r_size_done")
                self.code_done = sem("r_code_done")
                self.scale_done = sem("r_scale_done")
                self.bias_scaled = sem("r_bias_scaled")
                self.bias_round = sem("r_bias_round")
                self.bias_split = sem("r_bias_split")
                self.rows_round = sem("r_rows_round")
                self.rows_split = sem("r_rows_split")
                self.rows_ps = sem("r_rows_ps")
                self.rows_done = sem("r_rows_done")
                self.agg1_done = sem("r_agg1_done")
                self.xk_ps = sem("r_xk_ps")
                self.x_affine = sem("r_x_affine")
                self.up_done = sem("r_up_done")
                self.gelu_done = sem("r_gelu_done")
                self.gh_done = sem("r_gh_done")
                self.bn2_done = sem("r_bn2_done")
                self.agg2_done = sem("r_agg2_done")
                self.norm_step = sem("r_norm_step")
                self.rg_done = sem("r_rg_done")
                self.ht_ps = sem("r_ht_ps")
                self.h_round = sem("r_h_round")
                self.h_split = sem("r_h_split")
                self.y_ps = sem("r_y_ps")
                self.centred = sem("r_centred")
                self.x_shift = sem("r_x_shift")
                self.x_done = sem("r_x_done")

            def work_buffers(self, work):
                two, four = range(2), range(4)
                self.b1 = sb(work, "t_b1", [1, HID])
                self.b1_hi = sb(work, "t_b1_hi", [1, HID], F32R)
                self.b1_lo = sb(work, "t_b1_lo", [1, HID], F32R)
                self.b2 = sb(work, "t_b2", [P, DIM])
                self.g2 = sb(work, "t_g2", [P, HID])
                self.mean_row = sb(work, "t_mean_row", [P, DIM])
                self.shift_row = sb(work, "t_shift_row", [P, DIM])
                self.stats1 = sb(work, "t_stats1", [P, MT, 6])
                self.mv1 = sb(work, "t_mv1", [P, MT, 2])
                self.var1 = sb(work, "t_var1", [P, MT])
                self.rstd1 = sb(work, "t_rstd1", [P, MT])
                self.xn = sb(work, "t_xn", [P, MT, DIM])
                self.xa = sb(work, "t_xa", [P, KC, MN])
                self.x_hi = [sb(work, f"t_x_hi{z}", [P, KC, MN], F32R) for z in two]
                self.x_lo = [sb(work, f"t_x_lo{z}", [P, KC, MN], F32R) for z in two]
                self.h = [sb(work, f"t_h{z}", [P, HID]) for z in two]
                self.gh = [sb(work, f"t_gh{z}", [P, HID]) for z in two]
                self.stats2 = [sb(work, f"t_stats2{z}", [P, 2, 6]) for z in four]
                self.mv2 = [sb(work, f"t_mv2{z}", [P, 2]) for z in four]
                self.var2 = [sb(work, f"t_var2{z}", [P, 1]) for z in four]
                self.rstd2 = [sb(work, f"t_rstd2{z}", [P, 1]) for z in four]
                self.rg = [sb(work, f"t_rg{z}", [P, 1]) for z in four]
                self.h_hi = [sb(work, f"t_h_hi{z}", [P, HC, P], F32R) for z in two]
                self.h_lo = [sb(work, f"t_h_lo{z}", [P, HC, P], F32R) for z in two]
                self.y = sb(work, "t_y", [P, DIM])
                self.up_ps = PSUM[:, 0:4, :].rearrange("p (z b) n -> p z b n", z=2)
                self.ht_bank = PSUM[:, 4:6, :]
                self.y_bank = PSUM[:, 6, 0:DIM]
                self.xt_bank = PSUM[:, 7, :]
                self.rows_ps_bank = PSUM[:, 6:8, 0:DIM]
                self.total = PSUM[:, 7, 0:2]

        def ternary_weights_on_tensor(pe, w):
            pe.wait_ge(w.sums_done, 1)
            pe.matmul(w.total, ones[:], w.sums[:], start=True, stop=True).then_inc(w.total_ps, 1)

        def ternary_weights_on_vector(dve, w):
            count = [0]

            def step(instruction):
                count[0] += 1
                instruction.then_inc(w.code_done, 1)
                dve.wait_ge(w.code_done, count[0])

            dve.wait_ge(w.raw_in, 32)
            for n in range(2):
                last = dve.tensor_reduce(w.sums[:, n:n + 1], w.raw[:, n], AX.X, ALU.add, apply_absolute_value=True)
            last.then_inc(w.sums_done, 1)
            dve.wait_ge(w.total_ps, 1)
            dve.tensor_scalar(w.size[:], w.total, 1.0 / (HID * DIM), 1e-5, ALU.mult, ALU.max).then_inc(w.size_done, 1)
            dve.wait_ge(w.size_done, 1)
            step(dve.reciprocal(w.scale[:], w.size[:]))
            for n in range(2):
                step(dve.tensor_scalar(w.raw[:, n], w.raw[:, n], w.scale[:, n:n + 1], -1.0, ALU.mult, ALU.max))
                step(dve.tensor_scalar(w.raw[:, n], w.raw[:, n], 1.0, ROUND, ALU.min, ALU.add))
                step(dve.tensor_scalar(w.code[:, n], w.raw[:, n], ROUND, None, ALU.subtract))
            step(dve.reciprocal(w.size[:], w.scale[:]))
            step(dve.tensor_scalar(w.gate[:], w.size[:, 1:2], gates[:, 3:4], None, ALU.mult))
            dve.tensor_scalar(w.neg_gate[:], w.gate[:], -1.0, None, ALU.mult).then_inc(w.scale_done, 1)

        def ternary_rows_on_scalar(act, w):
            for n, col in enumerate((COL_G2, COL_T2)):
                last = act.activation(w.rows_hi[:, n], cols[:, col:col + HC].unsqueeze(2).broadcast_to([P, HC, P]), ACT.Copy)
            last.then_inc(w.rows_round, 1)

        def ternary_rows_on_vector(dve, w):
            dve.wait_ge(w.rows_round, 1)
            for n, col in enumerate((COL_G2, COL_T2)):
                last = dve.tensor_tensor(w.rows_lo[:, n], cols[:, col:col + HC].unsqueeze(2).broadcast_to([P, HC, P]),
                                         w.rows_hi[:, n].bitcast(F32), ALU.subtract)
            last.then_inc(w.rows_split, 1)

        def ternary_on_scalar(act, w):
            act.wait_ge(f.x_done, MB)
            for dst, src in ((w.b1[:], d["ter_b1"]), (w.b2[:], d["ter_b2"].partition_broadcast(P)),
                             (w.g2[:], d["ter_g2"].partition_broadcast(P))):
                act.dma_start(dst, src).then_inc(w.small_in, 16)
            act.wait_ge(w.bias_scaled, 1)
            act.activation(w.b1_hi[:], w.b1[:], ACT.Copy).then_inc(w.bias_round, 1)

            def x_affine(b, k):
                act.wait_ge(w.xk_ps, KC * b.n + k + 1)
                if k == 0:
                    after(act, w.x_split, b.count)
                act.activation(w.xa[:, k], w.xt_bank, ACT.Identity, scale=cols[:, COL_G1 + k:COL_G1 + k + 1],
                               bias=cols[:, COL_T1 + k:COL_T1 + k + 1]).then_inc(w.x_affine, 1)

            def x_rounded(b):
                act.wait_ge(w.x_affine, KC * (b.n + 1))
                act.activation(w.x_hi[b.z][:], w.xa[:], ACT.Copy).then_inc(w.x_round, 1)

            def gelu(b, t):
                at = MT * b.n + t
                act.wait_ge(w.up_done, at + 1)
                after(act, w.gh_done, at - 1)
                after(act, w.bn2_done, at - 1)
                act.activation(w.h[t % 2][:], w.up_ps[:, t % 2].rearrange("p b n -> p (b n)"), ACT.Gelu,
                               scale=w.size[:, 0:1]).then_inc(w.gelu_done, 1)

            def rounded(b, t):
                at = MT * b.n + t
                act.wait_ge(w.ht_ps, at + 1)
                after(act, w.y_ps, at - 1)
                act.activation(w.h_hi[t % 2][:], w.ht_bank.rearrange("p b (k n) -> p (b k) n", n=P),
                               ACT.Copy).then_inc(w.h_round, 1)

            first = Block(0, 0, 0, w.base)
            for k in range(KC):
                x_affine(first, k)
            x_rounded(first)

            def body(b, behind, ahead):
                for t in range(MT):
                    if t == 3 and ahead:
                        x_affine(b.next(), 1)
                        x_rounded(b.next())
                    gelu(b, t)
                    if t >= 1:
                        rounded(b, t - 1)
                    elif behind:
                        rounded(b.last(), MT - 1)
                    if t == 2 and ahead:
                        x_affine(b.next(), 0)

            paired_blocks(act, MB, body, w.base)
            rounded(Block(MB - 1, 1, (MB - 2) // 2, w.base), MT - 1)

        def ternary_on_gpsimd(pool, w):
            pool.wait_ge(f.x_done, MB)

            def inverse_std(b):
                pool.wait_ge(w.ln_stats, b.count + 1)
                pool.tensor_tensor(w.rstd1[:], w.var1[:], neghalf[:, 0:MT], ALU.pow).then_inc(w.ln_rstd, 1)

            def scale_h(b, t):
                at = MT * b.n + t
                pool.wait_ge(w.gelu_done, at + 1)
                after(pool, w.ht_ps, at - 1)
                pool.tensor_tensor(w.gh[t % 2][:], w.h[t % 2][:], w.g2[:], ALU.mult).then_inc(w.gh_done, 1)

            def norm_2(b, t):
                at = MT * b.n + t
                pool.wait_ge(w.agg2_done, at + 1)
                pool.tensor_tensor(w.var2[t][:], w.mv2[t][:, 1:2], eps_tile[:, 0:1], ALU.add).then_inc(w.norm_step, 1)
                pool.wait_ge(w.norm_step, 2 * at + 1)
                pool.tensor_tensor(w.rstd2[t][:], w.var2[t][:], neghalf[:, 0:1], ALU.pow).then_inc(w.norm_step, 1)
                pool.wait_ge(w.norm_step, 2 * at + 2)
                pool.tensor_tensor(w.rg[t][:], w.rstd2[t][:], w.neg_gate[:], ALU.mult).then_inc(w.rg_done, 1)

            def shift(b):
                pool.wait_ge(w.ln_done, b.count + 1)
                xb = x[:, bass.ds(MT * b.n, MT), :]
                pool.tensor_tensor(xb, xb, w.shift_row[:].unsqueeze(1).broadcast_to([P, MT, DIM]),
                                   ALU.add).then_inc(w.x_shift, 1)

            inverse_std(Block(0, 0, 0, w.base))
            pool.wait_ge(w.small_in, 48)
            pool.wait_ge(w.rows_done, 2)

            def body(b, behind, ahead):
                for t in range(MT):
                    scale_h(b, t)
                    if t == 1 and ahead:
                        inverse_std(b.next())
                    norm_2(b, t)
                    if t == 0:
                        shift(b)

            paired_blocks(pool, MB, body, w.base)

        def ternary_on_vector(dve, w):
            def stats_1(b):
                for t in range(MT):
                    last = dve.bn_stats(w.stats1[:, t, :], x[:, bass.ds(MT * b.n + t, 1), :])
                last.then_inc(w.bn_done, 1)

            def aggregate_1(b):
                if isinstance(b.n, int):
                    dve.wait_ge(w.bn_done, b.count + 1)
                for t in range(MT):
                    last = dve.bn_aggr(w.mv1[:, t, :], w.stats1[:, t, :])
                last.then_inc(w.agg1_done, 1)
                dve.wait_ge(w.agg1_done, b.n + 1)
                dve.tensor_scalar(w.var1[:], w.mv1[:, :, 1], 1.0 + EPS, EPS * EPS, ALU.mult, ALU.add).then_inc(w.ln_stats, 1)

            def apply_1(b):
                dve.wait_ge(w.ln_rstd, b.count + 1)
                after(dve, w.xk_ps, KC * b.n)
                for t in range(MT):
                    last = dve.tensor_scalar(w.xn[:, t, :], x[:, bass.ds(MT * b.n + t, 1), :].rearrange("p o c -> p (o c)"),
                                             w.mv1[:, t, 0:1], w.rstd1[:, t:t + 1], ALU.subtract, ALU.mult)
                last.then_inc(w.ln_done, 1)

            def x_residue(b):
                dve.wait_ge(w.x_round, b.count + 1)
                dve.tensor_tensor(w.x_lo[b.z][:], w.xa[:], w.x_hi[b.z][:].bitcast(F32), ALU.subtract).then_inc(w.x_split, 1)

            def stats_2(b, t):
                at = MT * b.n + t
                dve.wait_ge(w.gelu_done, at + 1)
                for c in range(2):
                    last = dve.bn_stats(w.stats2[t][:, c], w.h[t % 2][:, c * 512:(c + 1) * 512])
                last.then_inc(w.bn2_done, 1)

            def aggregate_2(b, t):
                if isinstance(b.n, int):
                    dve.wait_ge(w.bn2_done, MT * b.n + t + 1)
                dve.bn_aggr(w.mv2[t][:], w.stats2[t][:].rearrange("p c s -> p (c s)")).then_inc(w.agg2_done, 1)

            def residue(b, t):
                dve.wait_ge(w.h_round, MT * b.n + t + 1)
                dve.tensor_tensor(w.h_lo[t % 2][:], w.ht_bank.rearrange("p b (k n) -> p (b k) n", n=P),
                                  w.h_hi[t % 2][:].bitcast(F32), ALU.subtract).then_inc(w.h_split, 1)

            def residual(b, t):
                at = MT * b.n + t
                dve.wait_ge(w.y_ps, at + 1)
                dve.wait_ge(w.rg_done, at + 1)
                after(dve, w.x_done, at)
                dve.scalar_tensor_tensor(w.y[:], w.mean_row[:], w.mv2[t][:, 0:1], w.y_bank, ALU.mult,
                                         ALU.subtract).then_inc(w.centred, 1)
                dve.wait_ge(w.centred, at + 1)
                if t == 0:
                    dve.wait_ge(w.x_shift, b.n + 1)
                xt = x[:, bass.ds(at, 1), :].rearrange("p o c -> p (o c)")
                dve.scalar_tensor_tensor(xt, w.y[:], w.rg[t][:], xt, ALU.mult, ALU.add).then_inc(w.x_done, 1)

            dve.wait_ge(f.x_done, MB)
            first = Block(0, 0, 0, w.base)
            stats_1(first)
            aggregate_1(first)
            dve.wait_ge(w.small_in, 48)
            dve.wait_ge(w.scale_done, 1)
            dve.tensor_scalar(w.b1[:], w.b1[:], w.scale[0:1, 0:1], None, ALU.mult).then_inc(w.bias_scaled, 1)
            dve.wait_ge(w.rows_ps, 1)
            dve.tensor_copy(w.mean_row[:], w.rows_ps_bank[:, 0])
            dve.tensor_scalar(w.shift_row[:], w.b2[:], gates[:, 3:4], None, ALU.mult).then_inc(w.rows_done, 1)
            apply_1(first)
            dve.wait_ge(w.rows_done, 1)
            dve.scalar_tensor_tensor(w.shift_row[:], w.rows_ps_bank[:, 1], w.gate[:], w.shift_row[:], ALU.mult,
                                     ALU.add).then_inc(w.rows_done, 1)
            dve.wait_ge(w.bias_round, 1)
            dve.tensor_tensor(w.b1_lo[:], w.b1[:], w.b1_hi[:].bitcast(F32), ALU.subtract).then_inc(w.bias_split, 1)
            x_residue(first)

            def body(b, behind, ahead):
                for t in range(MT):
                    if t == 2 and ahead:
                        apply_1(b.next())
                    if t == 3 and ahead:
                        x_residue(b.next())
                    stats_2(b, t)
                    if t == 0 and ahead:
                        stats_1(b.next())
                    if t >= 1:
                        residue(b, t - 1)
                    elif behind:
                        residue(b.last(), MT - 1)
                    if t >= 2:
                        residual(b, t - 2)
                    elif behind:
                        residual(b.last(), t - 2 + MT)
                    aggregate_2(b, t)
                    if t == 0 and ahead:
                        aggregate_1(b.next())

            paired_blocks(dve, MB, body, w.base)
            final = Block(MB - 1, 1, (MB - 2) // 2, w.base)
            residue(final, MT - 1)
            residual(final, MT - 2)
            residual(final, MT - 1)

        def ternary_on_tensor(pe, w):
            w1 = w.code[:, 0].rearrange("p (k n) -> p k n", k=KC)
            w2 = w.code[:, 1].rearrange("p (k n) -> p k n", k=HC)

            def transpose_x(b, k):
                if k == 0:
                    pe.wait_ge(w.ln_done, b.count + 1)
                after(pe, w.x_affine, KC * b.n + k)
                for t in range(MT):
                    last = pe.transpose(w.xt_bank[:, t * P:(t + 1) * P], w.xn[:, t, k * P:(k + 1) * P], ident[:])
                last.then_inc(w.xk_ps, 1)

            def up(b, t):
                part = slice(t * P, (t + 1) * P)
                pe.wait_ge(w.x_split, b.count + 1)
                after(pe, w.gelu_done, MT * b.n + t - 1)
                for c in range(2):
                    n = slice(c * 512, (c + 1) * 512)
                    ps = w.up_ps[:, t % 2, c]
                    pe.matmul(ps, ones_r[0:1, :], w.b1_hi[:, n], start=True, stop=False)
                    pe.matmul(ps, ones_r[0:1, :], w.b1_lo[:, n], start=False, stop=False)
                    for k in range(KC):
                        pe.matmul(ps, w.x_hi[b.z][:, k, part], w1[:, k, n], start=False, stop=False)
                        last = pe.matmul(ps, w.x_lo[b.z][:, k, part], w1[:, k, n], start=False, stop=k == KC - 1)
                last.then_inc(w.up_done, 1)

            def transpose_h(b, t):
                at = MT * b.n + t
                pe.wait_ge(w.gh_done, at + 1)
                after(pe, w.h_split, at)
                for k in range(HC):
                    last = pe.transpose(w.ht_bank[:, k // 4, k % 4 * P:(k % 4 + 1) * P], w.gh[t % 2][:, k * P:(k + 1) * P], ident[:])
                last.then_inc(w.ht_ps, 1)

            def down(b, t):
                at = MT * b.n + t
                pe.wait_ge(w.h_split, at + 1)
                after(pe, w.x_done, at)
                for k in range(HC):
                    pe.matmul(w.y_bank, w.h_hi[t % 2][:, k], w2[:, k], start=k == 0, stop=False)
                    last = pe.matmul(w.y_bank, w.h_lo[t % 2][:, k], w2[:, k], start=False, stop=k == HC - 1)
                last.then_inc(w.y_ps, 1)

            pe.wait_ge(w.rows_split, 1)
            pe.wait_ge(w.scale_done, 1)
            for n in range(2):
                for k in range(HC):
                    pe.matmul(w.rows_ps_bank[:, n], w.rows_hi[:, n, k], w2[:, k], start=k == 0, stop=False)
                    last = pe.matmul(w.rows_ps_bank[:, n], w.rows_lo[:, n, k], w2[:, k], start=False, stop=k == HC - 1)
            last.then_inc(w.rows_ps, 1)
            pe.wait_ge(w.rows_done, 2)
            for k in range(KC):
                transpose_x(Block(0, 0, 0, w.base), k)
            pe.wait_ge(w.bias_split, 1)

            def body(b, behind, ahead):
                for t in range(MT):
                    if t == 3 and ahead:
                        transpose_x(b.next(), 1)
                    up(b, t)
                    if t >= 1:
                        transpose_h(b, t - 1)
                    elif behind:
                        transpose_h(b.last(), MT - 1)
                    if t == 2 and ahead:
                        transpose_x(b.next(), 0)
                    if t >= 2:
                        down(b, t - 2)
                    elif behind:
                        down(b.last(), t - 2 + MT)

            paired_blocks(pe, MB, body, w.base)
            final = Block(MB - 1, 1, (MB - 2) // 2, w.base)
            transpose_h(final, MT - 1)
            down(final, MT - 2)
            down(final, MT - 1)

        moe_scope = root.enter_context(ExitStack())
        moe_hi = sb(moe_scope, "moe_hi", [P, EARLY * EXPERT_COLS], F32R)
        moe_lo = sb(moe_scope, "moe_lo", [P, EARLY * EXPERT_COLS], F32R)
        att0_scope = moe_scope.enter_context(ExitStack())
        moe_raw = [sb(att0_scope, f"moe_raw{z}", [P, MOE_CHUNK]) for z in range(2)]
        a0 = Attention(0, att0_scope)
        att0_scope.close()
        mix_scope = moe_scope.enter_context(ExitStack())
        mix = Mixture(mix_scope)
        mix_scope.close()
        moe_scope.close()

        layer1_scope = root.enter_context(ExitStack())
        z_sum = sb(layer1_scope, "z_sum", [P, TILES, DIM])
        ffn_hi = sb(layer1_scope, "ffn_hi", [P, FFN_COLS], F32R)
        ffn_lo = sb(layer1_scope, "ffn_lo", [P, FFN_COLS], F32R)
        att1_scope = layer1_scope.enter_context(ExitStack())
        ffn_raw = [sb(att1_scope, f"ffn_raw{z}", [P, FFN_CHUNK]) for z in range(2)]
        a1 = Attention(1, att1_scope)
        att1_scope.close()
        f = FeedForward(layer1_scope)
        w = Ternary(layer1_scope)
        layer1_scope.close()
        w.work_buffers(root)

        side_in = [sem(f"side_in{z}") for z in range(2)]
        side_round = sem("side_round")
        side_split = sem("side_split")
        out_done = sem("out_done")
        WA_ORDER = (1, 2, 0, 3)

        block = root.enter_context(nc.Block())

        @block.sync
        def _(sp):
            def load(a, b):
                if a.stage == 0:
                    after(sp, a.x_in[b.z], 16 * b.half)
                    sp.dma_start(tiles(b), x_dram[:, bass.ds(BT * b.n, BT), :]).then_inc(a.x_in[b.z], 16)
                after(sp, a.ctx_split, b.count - 1)
                sp.dma_start(a.ctx[b.z][:], ctx_dram[bass.ds(b.n, 1)].rearrange("o p k n -> p (o k) n")).then_inc(a.ctx_in[b.z], 16)

            def load_moe(b):
                after(sp, side_split, b.count - 1)
                sp.dma_start(moe_raw[b.z][:], d["moe_w"][:, bass.ds(b.n * MOE_CHUNK, MOE_CHUNK)]).then_inc(side_in[b.z], 16)

            load(a0, Block(0, 0, 0))
            load_moe(Block(0, 0, 0))

            def body(b, behind, ahead):
                if ahead:
                    load(a0, b.next())
                    load_moe(b.next())

            paired_blocks(sp, BATCH, body)
            if stages > 1:
                mixture_on_sync(sp, mix)
            if stages > 2:
                sp.wait_ge(mix.y_added, NE * MB)
                def load_ffn(b):
                    after(sp, side_split, b.count - 1)
                    sp.dma_start(ffn_raw[b.z][:], d["ffn_w"][:, bass.ds(b.n * FFN_CHUNK, FFN_CHUNK)]).then_inc(side_in[b.z], 16)

                load(a1, Block(0, 0, 0, a1.base))
                load_ffn(Block(0, 0, 0, a1.base))

                def body(b, behind, ahead):
                    if ahead:
                        load(a1, b.next())
                        load_ffn(b.next())

                paired_blocks(sp, BATCH, body, a1.base)
            if stages > 3:
                sp.wait_ge(a1.y_done, 2 * BATCH)
                sp.wait_ge(side_split, 2 * BATCH)
                for n, name in enumerate(("ter_w1", "ter_w2")):
                    sp.dma_start(w.raw[:, n], d[name]).then_inc(w.raw_in, 16)
            for b in range(BATCH):
                if stages == 1:
                    sp.wait_ge(a0.y_done, b + 1)
                elif stages == 2:
                    sp.wait_ge(mix.y_added, (EXPERTS + 1) * MB)
                elif stages == 3:
                    sp.wait_ge(a1.y_done, BATCH + b + 1)
                    sp.dma_start(out_dram[:, BT * b:BT * (b + 1), :], z_sum[:, BT * b:BT * (b + 1), :]).then_inc(out_done, 16)
                    continue
                elif stages == 5:
                    sp.wait_ge(f.x_done, b // 2 + 1)
                else:
                    sp.wait_ge(w.x_done, BT * (b + 1))
                sp.dma_start(out_dram[:, BT * b:BT * (b + 1), :], x[:, BT * b:BT * (b + 1), :]).then_inc(out_done, 16)
            sp.wait_ge(out_done, 16 * BATCH)

        @block.gpsimd
        def _(pool):
            pool.memset(ident[:], 0.0).then_inc(pool_const, 1)
            pool.memset(headmask[:], 1.0).then_inc(pool_const, 1)
            pool.memset(ones[:], 1.0).then_inc(pool_const, 1)
            pool.memset(neghalf[:], -0.5)
            pool.memset(eps_tile[:], EPS).then_inc(pool_const, 1)
            pool.memset(a0.mask_raw[:], 0.0).then_inc(pool_const, 1)
            pool.wait_ge(pool_const, 5)
            pool.affine_select(out=ident[:], in_=ident[:], compare_op=ALU.not_equal, fill=1.0, base=0,
                               pattern=[[-1, P]], channel_multiplier=1).then_inc(pool_const, 1)
            pool.affine_select(out=headmask[:], in_=headmask[:], compare_op=ALU.is_ge, fill=0.0, base=0,
                               pattern=[[-HD, HPC]], channel_multiplier=1).then_inc(pool_const, 1)
            pool.wait_ge(pool_const, 7)
            pool.affine_select(out=headmask[:], in_=headmask[:], compare_op=ALU.is_ge, fill=0.0, base=HD - 1,
                               pattern=[[HD, HPC]], channel_multiplier=-1).then_inc(pool_const, 1)
            pool.wait_ge(pool_const, 8)

            def split_moe(b):
                part = bass.ds(b.n * MOE_CHUNK, MOE_CHUNK)
                pool.wait_ge(side_in[b.z], 16 * (b.half + b.base // 2 + 1))
                pool.tensor_tensor(moe_hi[:, part], moe_raw[b.z][:], one([P, MOE_CHUNK]), ALU.mult).then_inc(side_round, 1)
                pool.wait_ge(side_round, b.count + 1)
                pool.tensor_tensor(moe_lo[:, part], moe_raw[b.z][:], moe_hi[:, part].bitcast(F32),
                                   ALU.subtract).then_inc(side_split, 1)

            attention_on_gpsimd(pool, a0, None, split_moe)
            if stages > 1:
                mixture_on_gpsimd(pool, mix)

            def split_ffn(b):
                part = bass.ds(b.n * FFN_CHUNK, FFN_CHUNK)
                pool.wait_ge(side_in[b.z], 16 * (b.half + b.base // 2 + 1))
                pool.tensor_tensor(ffn_hi[:, part], ffn_raw[b.z][:], one([P, FFN_CHUNK]), ALU.mult).then_inc(side_round, 1)
                pool.wait_ge(side_round, b.count + 1)
                pool.tensor_tensor(ffn_lo[:, part], ffn_raw[b.z][:], ffn_hi[:, part].bitcast(F32),
                                   ALU.subtract).then_inc(side_split, 1)

            if stages > 2:
                pool.wait_ge(mix.y_added, NE * MB)
                pool.memset(a1.mask_raw[:], 1.0).then_inc(a1.mask_zero, 1)
                attention_on_gpsimd(pool, a1, z_sum, split_ffn)
            if stages > 3:
                ffn_on_gpsimd(pool, f)
            if stages == 4:
                ternary_on_gpsimd(pool, w)

        @block.scalar
        def _(act):
            act.dma_start(a0.w_raw[:, 1], d["wa0"][:, 1]).then_inc(a0.w_in[1], 16)
            act.dma_start(a0.w_raw[:, 2], d["wa0"][:, 2]).then_inc(a0.w_in[2], 16)
            act.dma_start(cols[:], d["cols"]).then_inc(consts_in, 16)
            act.dma_start(a0.bv[:], d["bv"][0].partition_broadcast(CTXP)).then_inc(a0.small_in, 16)
            act.dma_start(a0.w_raw[:, 0], d["wa0"][:, 0]).then_inc(a0.w_in[0], 16)
            act.dma_start(a0.bias_raw[:], d["bias"][0:1]).then_inc(a0.small_in, 16)
            act.dma_start(gates_raw[:], d["gates"].partition_broadcast(P)).then_inc(consts_in, 16)
            act.wait_ge(pool_const, 5)
            act.dma_start(a0.mask_raw[:, :, 0:CTX], d["mask_q"].rearrange("(t p) n -> p t n", p=P)).then_inc(a0.mask_in, 16)
            act.dma_start(a0.w_raw[:, 3], d["wa0"][:, 3]).then_inc(a0.w_in[3], 16)
            for n, i in enumerate(WA_ORDER):
                act.wait_ge(a0.w_in[i], 16)
                act.activation(a0.w_hi[:, i].rearrange("p k n -> p (k n)"), a0.w_raw[:, i], ACT.Copy).then_inc(a0.w_round, 1)
                if n == 0:
                    act.wait_ge(consts_in, 32)
                    act.wait_ge(a0.small_in, 32)
                    act.activation(a0.bias_hi[:], a0.bias_raw[:], ACT.Copy).then_inc(a0.bias_round, 1)
                    act.activation(gates[:], gates_raw[:], ACT.Tanh).then_inc(gates_done, 1)
            attention_on_scalar(act, a0)
            if stages > 1:
                mixture_on_scalar(act, mix)
            if stages > 2:
                act.wait_ge(mix.y_added, NE * MB)
                for i in WA_ORDER:
                    act.dma_start(a1.w_raw[:, i], d["wa1"][:, i]).then_inc(a1.w_in[i], 16)
                act.dma_start(a1.bv[:], d["bv"][1].partition_broadcast(CTXP)).then_inc(a1.small_in, 16)
                act.dma_start(a1.bias_raw[:], d["bias"][1:2]).then_inc(a1.small_in, 16)
                act.dma_start(a1.mask_u8[:], d["mask_k"]).then_inc(a1.mask_in, 16)
                for n, i in enumerate(WA_ORDER):
                    act.wait_ge(a1.w_in[i], 32)
                    act.activation(a1.w_hi[:, i].rearrange("p k n -> p (k n)"), a1.w_raw[:, i], ACT.Copy).then_inc(a1.w_round, 1)
                    if n == 0:
                        act.wait_ge(a1.small_in, 64)
                        act.activation(a1.bias_hi[:], a1.bias_raw[:], ACT.Copy).then_inc(a1.bias_round, 1)
                attention_on_scalar(act, a1)
            if stages > 3:
                ffn_on_scalar(act, f)
            if stages == 4:
                ternary_on_scalar(act, w)

        @block.vector
        def _(dve):
            dve.wait_ge(pool_const, 8)
            dve.tensor_copy(a0.ident[:], ident[:])
            dve.tensor_copy(ones_r[:], ones[:]).then_inc(consts_done, 1)
            dve.wait_ge(a0.bias_round, 1)
            dve.tensor_tensor(a0.bias_lo[:], a0.bias_raw[:], a0.bias_hi[:].bitcast(F32), ALU.subtract).then_inc(a0.bias_split, 1)
            for n, i in enumerate(WA_ORDER):
                dve.wait_ge(a0.w_round, n + 1)
                dve.tensor_tensor(a0.w_lo[:, i].rearrange("p k n -> p (k n)"), a0.w_raw[:, i],
                                  a0.w_hi[:, i].bitcast(F32).rearrange("p k n -> p (k n)"), ALU.subtract).then_inc(a0.w_split, 1)
            dve.wait_ge(a0.mask_in, 16)
            dve.tensor_scalar(a0.mask[:], a0.mask_raw[:], 0.0, MASKED, ALU.is_equal, ALU.mult).then_inc(a0.mask_done, 1)
            attention_on_vector(dve, a0, None)
            if stages > 1:
                mixture_on_vector(dve, mix)
            if stages > 2:
                dve.wait_ge(mix.y_added, NE * MB)
                dve.wait_ge(a1.bias_round, 2)
                dve.tensor_tensor(a1.bias_lo[:], a1.bias_raw[:], a1.bias_hi[:].bitcast(F32), ALU.subtract).then_inc(a1.bias_split, 1)
                for n, i in enumerate(WA_ORDER):
                    dve.wait_ge(a1.w_round, 4 + n + 1)
                    dve.tensor_tensor(a1.w_lo[:, i].rearrange("p k n -> p (k n)"), a1.w_raw[:, i],
                                      a1.w_hi[:, i].bitcast(F32).rearrange("p k n -> p (k n)"), ALU.subtract).then_inc(a1.w_split, 1)
                dve.wait_ge(a1.mask_in, 32)
                dve.wait_ge(a1.mask_zero, 1)
                dve.tensor_copy(a1.mask_raw[:, :, 0:CTX], a1.mask_u8[:]).then_inc(a1.mask_cast, 1)
                dve.wait_ge(a1.mask_cast, 1)
                dve.tensor_scalar(a1.mask[:], a1.mask_raw[:], MASKED, None, ALU.mult).then_inc(a1.mask_done, 1)
                attention_on_vector(dve, a1, z_sum)
            if stages > 3:
                ffn_on_vector(dve, f)
            if stages == 4:
                ternary_on_vector(dve, w)

        @block.tensor
        def _(pe):
            attention_on_tensor(pe, a0)
            if stages > 1:
                mixture_on_tensor(pe, mix)
            if stages > 2:
                attention_on_tensor(pe, a1)
            if stages > 3:
                ffn_on_tensor(pe, f)
            if stages == 4:
                ternary_on_tensor(pe, w)


_SHAPE = (BATCH, SEQ, DIM)


def kernel(**inputs):
    import concourse.bacc as bacc
    from concourse.bass_utils import run_bass_kernel_spmd

    nc = bacc.Bacc("TRN2", target_bir_lowering=False, num_devices=1)
    arrays = lay_out({k: np.asarray(v) for k, v in inputs.items()})
    d = {n: nc.dram_tensor(n, a.shape, mybir.dt.from_np(a.dtype), kind="ExternalInput").ap() for n, a in arrays.items()}
    out = nc.dram_tensor("y", _SHAPE, F32, kind="ExternalOutput").ap()
    flamingo_kernel(nc, d, out)
    r = run_bass_kernel_spmd(nc, [arrays], core_ids=[0])
    return r.results[0]["y"]
```

```python
import numpy as np
from contextlib import ExitStack

import concourse.bass as bass
from concourse import mybir
from concourse.alu_op_type import AluOpType as ALU

F32 = mybir.dt.float32
F32R = mybir.dt.float32r
U8 = mybir.dt.uint8
U32 = mybir.dt.uint32
I32 = mybir.dt.int32
ACT = mybir.ActivationFunctionType
AX = mybir.AxisListType

P = 128
BATCH, SEQ, DIM = 16, 256, 256
CTX = 77
CTXP = CTX + 1
HEADS, HD = 16, 16
EXPERTS = 8
KC = DIM // P
TILES = BATCH * SEQ // P
BT = SEQ // P
HPC = P // HD
VW = HD + 2
UNITS = KC * BT
PAIRS = HPC * CTXP
PC = -(-PAIRS // P)
MT = 4
MB = TILES // MT
MN = MT * P
HID = 1024
HC = HID // P
EPS = 1e-5
MASKED = -1e30
MATRIX = KC * DIM
MOE_CHUNK = 2 * DIM
EXPERT_COLS = 3 * 2 * MOE_CHUNK
EARLY_CHUNKS = BATCH
LATE_PART = MOE_CHUNK // 2
SORTED = 2 * TILES + EXPERTS
GROUP = 4
GROUPS = SORTED // GROUP
ZERO_TILES = SORTED // BATCH
FFN_COLS = 2 * KC * HID
FFN_CHUNK = FFN_COLS // BATCH
TER_COLS = KC * HID
ROUND = 1.5 * 2 ** 23

COL_BQ, COL_BK = (0, 4), (2, 6)
COL_B1 = 8
COL_B3 = COL_B1 + KC
COL_FB1 = COL_B3 + KC
COL_G1 = COL_FB1 + HC
COL_T1 = COL_G1 + KC
COL_G2 = COL_T1 + KC
COL_T2 = COL_G2 + HC
COLS = COL_T2 + HC


def heads_of(chunk):
    if chunk == 0:
        return 0, HPC
    first = chunk * P // CTXP
    return first, (min((chunk + 1) * P, PAIRS) - 1) // CTXP - first + 1


def column_of(chunk):
    return sum(heads_of(c)[1] for c in range(chunk)) * VW


def value_pieces():
    for h in range(HPC):
        pair, end = h * CTXP, (h + 1) * CTXP
        while pair < end:
            stop = min(end, (pair // P + 1) * P)
            yield h, pair - h * CTXP, stop - pair, pair // P, pair % P
            pair = stop


PIECES = len(list(value_pieces()))


def after(engine, semaphore, value):
    if not (isinstance(value, int) and value <= 0):
        engine.wait_ge(semaphore, value)


class Block:

    def __init__(self, n, parity, half, base=0):
        self.n, self.z, self.half, self.base = n, parity, half, base
        self.count = n + base

    def next(self):
        return Block(self.n + 1, 1 - self.z, self.half + self.z, self.base)

    def last(self):
        return Block(self.n - 1, 1 - self.z, self.half - (1 - self.z), self.base)


def paired_blocks(engine, count, body, base=0, reach=1):
    body(Block(0, 0, 0, base), False, reach)
    with engine.Fori(0, (count - 1 - reach) // 2) as i:
        body(Block(2 * i + 1, 1, i, base), True, reach)
        body(Block(2 * i + 2, 0, i + 1, base), True, reach)
    for n in range(count - reach, count):
        body(Block(n, n % 2, n // 2, base), True, count - 1 - n)

def lay_out(i):
    def chunks(w):
        return w.reshape(-1, P, w.shape[1]).transpose(1, 0, 2)

    def flat(w):
        return chunks(w).reshape(P, -1)

    def col(b):
        return b.reshape(-1, P).T

    ctx = np.zeros((BATCH, P, KC, CTXP), np.float32)
    ctx[..., :CTX] = i["ctx_1024"].transpose(0, 2, 1).reshape(BATCH, KC, P, CTX).transpose(0, 2, 1, 3)
    moe = []
    for w1, w3, w2 in [[i[f"L0_ffn_w{n}"][e] for n in (1, 3, 2)] for e in range(EXPERTS)] + [[i[f"L0_ffn_sw{n}"] for n in (1, 3, 2)]]:
        moe += [chunks(np.concatenate([w1, w3], 1)).reshape(P, -1), flat(w2)]
    cols = [col(i[n]) for n in ("L0_xattn_bq", "L0_xattn_bk", "L1_xattn_bq", "L1_xattn_bk")]
    cols += [col(i["L0_ffn_sb1"]), col(i["L0_ffn_sb3"])]
    cols += [col(i[n]) for n in ("L1_xattn_b1", "L1_ffn_ln1_g", "L1_ffn_ln1_b", "L1_ffn_ln2_g", "L1_ffn_ln2_b")]
    arrays = {
        "x": i["x"],
        "ctx": ctx,
        "mask_q": i["mask_1x1xSxS2_fk0"].reshape(SEQ, CTX),
        "mask_k": i["mask_BxS2_bf0"].reshape(1, BATCH, CTX),
        "wa0": np.stack([flat(i[f"L0_xattn_W{n}"].T) for n in "qkvp"], 1),
        "wa1": np.stack([flat(i[f"L1_xattn_W{n}"]) for n in "qkvo"], 1),
        "moe_w": np.concatenate(moe, 1),
        "moe_b2": np.concatenate([i["L0_ffn_b2"], i["L0_ffn_sb2"][None]]),
        "moe_b13": np.repeat(np.concatenate([i["L0_ffn_b1"], i["L0_ffn_b3"]], 1), 2, 0),
        "tile_numbers": np.tile(np.arange(SORTED, dtype=np.float32), (2 * EXPERTS, 1)),
        "row_of": np.array([[r // 2, 1 - r % 2, r % 2] for r in range(2 * EXPERTS)], np.float32),
        "gate_w": flat(i["L0_ffn_gate_w"].T),
        "ffn_w": np.concatenate([flat(i["L1_xattn_W1"]), flat(i["L1_xattn_W2"])], 1),
        "ter_w1": flat(i["L1_ffn_w1"].T),
        "ter_w2": flat(i["L1_ffn_w2"].T),
        "ter_g2": i["L1_ffn_ln2_g"],
        "ter_b1": i["L1_ffn_b1"][None],
        "ter_b2": i["L1_ffn_b2"],
        "cols": np.concatenate(cols, 1),
        "bv": np.stack([i["L0_xattn_bv"], i["L1_xattn_bv"]]),
        "bias": np.stack([i[n] for n in ("L0_xattn_bp", "L1_xattn_bo", "L1_xattn_b2")]),
        "norms": np.stack([i[n] for n in ("L1_xattn_ln1_g", "L1_xattn_ln1_b", "L1_xattn_ln2_g", "L1_xattn_ln2_b")]),
        "gates": np.concatenate([i["g_xattn"], i["g_ffn"]]),
    }
    return {n: np.ascontiguousarray(a) for n, a in arrays.items()}


def flamingo_kernel(nc, d, out, stages=4):
    x_dram = d["x"].rearrange("b (t p) c -> p (b t) c", p=P)
    out_dram = out.rearrange("b (t p) c -> p (b t) c", p=P)
    ctx_dram = d["ctx"]
    d = {**d, **{n: nc.dram_tensor(n, (SORTED * P, DIM), F32, kind="Internal").ap() for n in ("sorted_x", "sorted_y")}}
    root = ExitStack()
    with root:
        def sb(scope, name, shape, dt=F32):
            return scope.enter_context(nc.sbuf_tensor("s_" + name, shape, dt))

        def sem(name):
            return root.enter_context(nc.semaphore(name))

        x = sb(root, "x", [P, TILES, DIM])
        ident = sb(root, "ident", [P, P])
        ones_r = sb(root, "ones_r", [P, P], F32R)
        ones = sb(root, "ones", [P, P])
        headmask = sb(root, "headmask", [P, HPC])
        neghalf = sb(root, "neghalf", [P, 8])
        eps_tile = sb(root, "eps_tile", [P, 8])
        cols = sb(root, "cols", [P, COLS])
        gates_raw = sb(root, "gates_raw", [P, 4])
        gates = sb(root, "gates", [P, 4])
        slots = sb(root, "slots", [P, TILES, 2], U32)
        weight = sb(root, "weight", [P, TILES, 2])

        PSUM = root.enter_context(nc.psum_tensor("PSUM", [P, 8, 512], F32))

        consts_in = sem("consts_in")
        consts_done = sem("consts_done")
        pool_const = sem("pool_const")
        gates_done = sem("gates_done")

        def one(shape):
            ap = ones[:, 0:1]
            for _ in shape[2:]:
                ap = ap.unsqueeze(1)
            return ap.broadcast_to(shape)

        class AttentionSignals:
            x_in = [sem(f"a_x_in{z}") for z in range(2)]
            rows_in = [sem(f"a_rows_in{z}") for z in range(2)]
            ctx_in = [sem(f"a_ctx_in{z}") for z in range(2)]
            w_in = [sem(f"a_w_in{i}") for i in range(4)]
            small_in = sem("a_small_in")
            bias_round = sem("a_bias_round")
            bias_split = sem("a_bias_split")
            w_round = sem("a_w_round")
            w_split = sem("a_w_split")
            mask_in = sem("a_mask_in")
            mask_done = sem("a_mask_done")
            v_ones = sem("a_v_ones")
            v_spread = [sem(f"a_v_spread{z}") for z in range(2)]
            ctx_round = sem("a_ctx_round")
            ctx_split = sem("a_ctx_split")
            bn_done = sem("a_bn_done")
            ln_stats = sem("a_ln_stats")
            ln_eps = sem("a_ln_eps")
            ln_rstd = sem("a_ln_rstd")
            ln_done = sem("a_ln_done")
            ln_kept = sem("a_ln_kept")
            xt_ps = sem("a_xt_ps")
            x_round = sem("a_x_round")
            x_split = sem("a_x_split")
            q_ps = sem("a_q_ps")
            q_round = sem("a_q_round")
            q_split = sem("a_q_split")
            kv_ps = sem("a_kv_ps")
            kv_done = sem("a_kv_done")
            k_rounded = sem("a_k_rounded")
            k_residue = sem("a_k_residue")
            kd_done = sem("a_kd_done")
            scores_ps = sem("a_scores_ps")
            max_done = sem("a_max_done")
            scores_read = sem("a_scores_read")
            exp_done = sem("a_exp_done")
            pt_ps = sem("a_pt_ps")
            pt_done = sem("a_pt_done")
            pv_ps = sem("a_pv_ps")
            sum_done = sem("a_sum_done")
            o_done = sem("a_o_done")
            ot_ps = sem("a_ot_ps")
            o_round = sem("a_o_round")
            o_split = sem("a_o_split")
            y_ps = sem("a_y_ps")
            y_done = sem("a_y_done")
            mixed = sem("a_mixed")
            slot_copied = sem("a_slot_copied")
            mask_cast = sem("a_mask_cast")

        class Attention(AttentionSignals):

            def __init__(self, stage, scope, sums=None):
                self.stage = stage
                self.base = BATCH * stage
                n = f"a{stage}_"
                two = range(2)
                self.w_raw = sb(scope, n + "w_raw", [P, 4, MATRIX])
                self.w_hi = sb(scope, n + "w_hi", [P, 4, KC, DIM], F32R)
                self.w_lo = sb(scope, n + "w_lo", [P, 4, KC, DIM], F32R)
                self.bv = sb(scope, n + "bv", [CTXP, DIM])
                self.bias_raw = sb(scope, n + "bias_raw", [1, DIM])
                self.bias_hi = sb(scope, n + "bias_hi", [1, DIM], F32R)
                self.bias_lo = sb(scope, n + "bias_lo", [1, DIM], F32R)
                self.bq, self.bk = COL_BQ[stage], COL_BK[stage]
                self.mv = sb(scope, n + "mv", [P, BT, 2])
                self.stats = sb(scope, n + "stats", [P, BT, 6])
                self.var_eps = sb(scope, n + "var_eps", [P, BT])
                self.rstd = sb(scope, n + "rstd", [P, BT])
                self.xn = sb(scope, n + "xn", [P, BT, DIM])
                self.x_hi = sb(scope, n + "x_hi", [P, KC, SEQ], F32R)
                self.x_lo = sb(scope, n + "x_lo", [P, KC, SEQ], F32R)
                self.q_hi = [sb(scope, n + f"q_hi{z}", [P, KC, SEQ], F32R) for z in two]
                self.q_lo = [sb(scope, n + f"q_lo{z}", [P, KC, SEQ], F32R) for z in two]
                self.ctx = [sb(scope, n + f"ctx{z}", [P, KC, CTXP]) for z in two]
                self.ctx_hi = [sb(scope, n + f"ctx_hi{z}", [P, KC, CTXP], F32R) for z in two]
                self.ctx_lo = [sb(scope, n + f"ctx_lo{z}", [P, KC, CTXP], F32R) for z in two]
                self.k = sb(scope, n + "k", [P, KC, CTXP])
                self.k_round = sb(scope, n + "k_round", [P, KC, CTXP], F32R)
                self.k_rest = sb(scope, n + "k_rest", [P, KC, CTXP])
                self.kd_hi = [sb(scope, n + f"kd_hi{z}", [P, KC, HPC, CTXP], F32R) for z in two]
                self.kd_lo = [sb(scope, n + f"kd_lo{z}", [P, KC, HPC, CTXP], F32R) for z in two]
                self.v = [sb(scope, n + f"v{z}", [CTXP, HEADS, VW]) for z in two]
                self.v_diagonal = [sb(scope, n + f"v_diagonal{z}", [P, KC, column_of(PC)]) for z in two]
                self.pairs = [sb(scope, n + f"prob{z}", [P, PC, P]) for z in two]
                self.prob = [t[:].rearrange("p c n -> p (c n)")[:, 0:PAIRS].rearrange("p (h n) -> p h n", n=CTXP) for t in self.pairs]
                self.row_max = [sb(scope, n + f"row_max{z}", [P, HPC]) for z in two]
                self.prob_t = [sb(scope, n + f"prob_t{z}", [P, PC, P]) for z in two]
                self.row_sum = [sb(scope, n + f"row_sum{z}", [P, HPC, 1]) for z in two]
                self.o = [sb(scope, n + f"o{z}", [P, BT, DIM]) for z in two]
                self.o_hi = sb(scope, n + "o_hi", [P, KC, SEQ], F32R)
                self.o_lo = sb(scope, n + "o_lo", [P, KC, SEQ], F32R)
                if stage == 0:
                    self.mask_raw = sb(scope, n + "mask_raw", [P, BT, CTXP])
                    self.mask = sb(scope, n + "mask", [P, BT, CTXP], F32R)
                    self.ident = sb(scope, n + "ident", [P, P], F32R)
                else:
                    self.slot = [sb(scope, n + f"slot{z}", [P, BT, 2], U32) for z in two]
                    self.rows = [sb(scope, n + f"rows{z}", [P, BT, 2, DIM]) for z in two]
                    self.mask_u8 = sb(scope, n + "mask_u8", [1, BATCH, CTX], U8)
                    late_sums = sums[0:1, TILES // 2:, :].rearrange("p t c -> p (t c)")
                    self.mask_raw = late_sums[:, 0:BATCH * CTXP].rearrange("p (b n) -> p b n", n=CTXP)
                    self.mask = sb(scope, n + "mask", [1, BATCH, CTXP], F32R)
                self.scores = PSUM[:, 0:4, :].rearrange("p (b c) n -> p b c n", b=2)
                self.prob_t_ps = PSUM[:, 4:6, :].rearrange("p c (h n) -> p (c h) n", n=P)[:, 0:PC]
                self.o_ps = PSUM[:, 6, 0:HPC * VW].rearrange("p (h n) -> p h n", n=VW)
                self.o_t_bank = PSUM[:, 6, :]
                self.misc = PSUM[:, 7, :]

        def tiles(b):
            return x[:, bass.ds(BT * b.n, BT), :]

        def attention_on_vector(dve, a, z_kept):
            def mixed(b):
                dve.wait_ge(a.rows_in[b.z], 16 * 2 * BT * (b.half + 1))
                for s in range(2):
                    if s == 1:
                        dve.wait_ge(a.mixed, 2 * b.n + 1)
                    for t in range(BT):
                        xt = x[:, bass.ds(BT * b.n + t, 1), :].rearrange("p o c -> p (o c)")
                        last = dve.scalar_tensor_tensor(xt, a.rows[b.z][:, t, s, :],
                                                        weight[:, bass.ds(BT * b.n + t, 1), s:s + 1].rearrange("p o c -> p (o c)"),
                                                        xt, ALU.mult, ALU.add)
                    last.then_inc(a.mixed, 1)
                dve.wait_ge(a.mixed, 2 * b.n + 2)

            def ln_stats(b):
                if a.stage == 0:
                    dve.wait_ge(a.x_in[b.z], 16 * (b.half + 1))
                for t in range(BT):
                    last = dve.bn_stats(a.stats[:, t, :], x[:, bass.ds(BT * b.n + t, 1), :])
                last.then_inc(a.bn_done, 1)

            def ln_aggregate(b):
                if isinstance(b.n, int):
                    dve.wait_ge(a.bn_done, b.count + 1)
                for t in range(BT):
                    last = dve.bn_aggr(a.mv[:, t, :], a.stats[:, t, :])
                last.then_inc(a.ln_stats, 1)

            def ln_apply(b):
                dve.wait_ge(a.ln_rstd, b.count + 1)
                after(dve, a.xt_ps, b.count)
                if a.stage == 1:
                    after(dve, a.ln_kept, b.n)
                for t in range(BT):
                    last = dve.tensor_scalar(a.xn[:, t, :], x[:, bass.ds(BT * b.n + t, 1), :].rearrange("p o c -> p (o c)"),
                                             a.mv[:, t, 0:1], a.rstd[:, t:t + 1], ALU.subtract, ALU.mult)
                last.then_inc(a.ln_done, 1)

            def x_residue(b):
                dve.wait_ge(a.x_round, b.count + 1)
                dve.tensor_tensor(a.x_lo[:].rearrange("p k n -> p (k n)"), a.misc,
                                  a.x_hi[:].bitcast(F32).rearrange("p k n -> p (k n)"),
                                  ALU.subtract).then_inc(a.x_split, 1)

            def q_residue(b):
                dve.wait_ge(a.q_round, b.count + 1)
                for m in range(KC):
                    last = dve.scalar_tensor_tensor(a.q_lo[b.z][:, m, :], a.misc[:, m * SEQ:(m + 1) * SEQ],
                                                    cols[:, a.bq + m:a.bq + m + 1],
                                                    a.q_hi[b.z][:, m, :].bitcast(F32), ALU.add, ALU.subtract)
                last.then_inc(a.q_split, 1)

            def keys_values(b):
                dve.wait_ge(a.kv_ps, b.count + 1)
                after(dve, a.kd_done, b.count)
                after(dve, a.v_spread[b.z], 16 * PIECES * (b.half + a.base // 2))
                dve.tensor_tensor(a.k[:], a.misc[:, 0:KC * CTXP].rearrange("p (k n) -> p k n", k=KC),
                                  cols[:, a.bk:a.bk + KC].unsqueeze(2).broadcast_to([P, KC, CTXP]), ALU.add)
                dve.tensor_tensor(a.v[b.z][:, :, 0:HD],
                                  a.misc[0:CTXP, DIM:2 * DIM].rearrange("p (h n) -> p h n", n=HD),
                                  a.bv[:].rearrange("p (h n) -> p h n", n=HD),
                                  ALU.add).then_inc(a.kv_done, 1)

            def score_max(b, j):
                u = UNITS * b.count + j
                s = a.scores[:, j % 2, :, 0:HPC // 2 * CTXP].rearrange("p c (h n) -> p c h n", n=CTXP)
                mx = a.row_max[j % 2][:].rearrange("p (c h) -> p c h", c=2)
                dve.wait_ge(a.scores_ps, u + 1)
                dve.tensor_reduce(mx, s, AX.X, ALU.max).then_inc(a.max_done, 1)
                dve.wait_ge(a.max_done, u + 1)
                after(dve, a.pt_ps, u - 1)
                dve.tensor_tensor(a.prob[j % 2].rearrange("p (c h) n -> p c h n", c=2), s,
                                  mx.unsqueeze(3).broadcast_to([P, 2, HPC // 2, CTXP]),
                                  ALU.subtract).then_inc(a.scores_read, 1)

            def normalise(b, j):
                u = UNITS * b.count + j
                m, qt = j // BT, j % BT
                dve.wait_ge(a.pv_ps, u + 1)
                dve.reciprocal(a.row_sum[j % 2][:], a.o_ps[:, :, HD:HD + 1]).then_inc(a.sum_done, 1)
                dve.wait_ge(a.sum_done, u + 1)
                dve.tensor_tensor(a.o[b.z][:, qt, m * P:(m + 1) * P].rearrange("p (h n) -> p h n", n=HD),
                                  a.o_ps[:, :, 0:HD], a.row_sum[j % 2][:].broadcast_to([P, HPC, HD]),
                                  ALU.mult).then_inc(a.o_done, 1)

            def o_residue(b):
                dve.wait_ge(a.o_round, b.count + 1)
                dve.tensor_tensor(a.o_lo[:].rearrange("p k n -> p (k n)"), a.o_t_bank,
                                  a.o_hi[:].bitcast(F32).rearrange("p k n -> p (k n)"),
                                  ALU.subtract).then_inc(a.o_split, 1)

            def residual(b):
                dve.wait_ge(a.y_ps, b.count + 1)
                y = a.misc.rearrange("p (t c) -> p t c", t=BT)
                if a.stage == 0:
                    dve.scalar_tensor_tensor(tiles(b), y, gates[:, 0:1], tiles(b), ALU.mult,
                                             ALU.add).then_inc(a.y_done, 1)
                else:
                    kept = z_kept[:, bass.ds(BT * b.n, BT), :]
                    dve.wait_ge(a.ln_kept, b.n + 1)
                    dve.tensor_tensor(kept, y, kept, ALU.add).then_inc(a.y_done, 1)

            dve.wait_ge(consts_done, 1)
            dve.wait_ge(gates_done, 1)
            dve.wait_ge(a.small_in, 32 * (a.stage + 1))
            first = Block(0, 0, 0, a.base)
            if a.stage == 1:
                mixed(first)
            ln_stats(first)
            ln_aggregate(first)
            ln_apply(first)
            keys_values(first)
            x_residue(first)
            q_residue(first)

            def body(b, behind, ahead):
                if ahead and a.stage == 1:
                    mixed(b.next())
                score_max(b, 0)
                if ahead:
                    ln_stats(b.next())
                if behind:
                    normalise(b.last(), 2)
                if ahead:
                    ln_aggregate(b.next())
                    ln_apply(b.next())
                score_max(b, 1)
                if ahead:
                    keys_values(b.next())
                if behind:
                    normalise(b.last(), 3)
                if ahead:
                    x_residue(b.next())
                score_max(b, 2)
                normalise(b, 0)
                if behind:
                    o_residue(b.last())
                if ahead:
                    q_residue(b.next())
                score_max(b, 3)
                normalise(b, 1)
                if behind:
                    residual(b.last())

            paired_blocks(dve, BATCH, body, a.base)
            final = Block(BATCH - 1, 1, (BATCH - 2) // 2, a.base)
            normalise(final, 2)
            normalise(final, 3)
            o_residue(final)
            residual(final)

        def attention_on_scalar(act, a):
            def x_rounded(b):
                act.wait_ge(a.xt_ps, b.count + 1)
                after(act, a.q_ps, b.count)
                act.activation(a.x_hi[:].rearrange("p k n -> p (k n)"), a.misc, ACT.Copy).then_inc(a.x_round, 1)

            def q_rounded(b):
                act.wait_ge(a.q_ps, b.count + 1)
                for m in range(KC):
                    last = act.activation(a.q_hi[b.z][:, m, :], a.misc[:, m * SEQ:(m + 1) * SEQ], ACT.Identity,
                                          bias=cols[:, a.bq + m:a.bq + m + 1])
                last.then_inc(a.q_round, 1)

            def exponential(b, j):
                act.wait_ge(a.scores_read, UNITS * b.count + j + 1)
                act.activation(a.prob[j % 2], a.prob[j % 2], ACT.Exp,
                               scale=HD ** -0.5).then_inc(a.exp_done, 1)

            def transposed(b, j):
                u = UNITS * b.count + j
                act.wait_ge(a.pt_ps, u + 1)
                after(act, a.pv_ps, u - 1)
                act.activation(a.prob_t[j % 2][:], a.prob_t_ps, ACT.Copy).then_inc(a.pt_done, 1)

            def o_rounded(b):
                act.wait_ge(a.ot_ps, b.count + 1)
                act.activation(a.o_hi[:].rearrange("p k n -> p (k n)"), a.o_t_bank, ACT.Copy).then_inc(a.o_round, 1)

            act.wait_ge(consts_done, 1)
            x_rounded(Block(0, 0, 0, a.base))
            q_rounded(Block(0, 0, 0, a.base))

            def body(b, behind, ahead):
                exponential(b, 0)
                if behind:
                    transposed(b.last(), 3)
                exponential(b, 1)
                transposed(b, 0)
                if ahead:
                    x_rounded(b.next())
                exponential(b, 2)
                transposed(b, 1)
                if behind:
                    o_rounded(b.last())
                if ahead:
                    q_rounded(b.next())
                exponential(b, 3)
                transposed(b, 2)

            paired_blocks(act, BATCH, body, a.base)
            final = Block(BATCH - 1, 1, (BATCH - 2) // 2, a.base)
            transposed(final, 3)
            o_rounded(final)

        def product(pe, ps, pairs, start=True, stop=True):
            n = len(pairs)
            for i, (lh, ll, rh, rl) in enumerate(pairs):
                pe.matmul(ps, lh, rh, start=start and i == 0, stop=False, skip_group_check=not start)
                pe.matmul(ps, ll, rh, start=False, stop=False, skip_group_check=not start)
                last = pe.matmul(ps, lh, rl, start=False, stop=stop and i == n - 1, skip_group_check=not start)
            return last

        def attention_on_tensor(pe, a):
            WQ, WK, WV, WP = range(4)

            def keys_values(b):
                pe.wait_ge(a.ctx_split, b.count + 1)
                if not isinstance(b.n, int) or b.n > 0:
                    pe.wait_ge(a.scores_read, UNITS * (b.count - 1) + 1)
                for m in range(KC):
                    product(pe, a.misc[:, m * CTXP:(m + 1) * CTXP],
                            [(a.w_hi[:, WK, k, m * P:(m + 1) * P], a.w_lo[:, WK, k, m * P:(m + 1) * P],
                              a.ctx_hi[b.z][:, k, :], a.ctx_lo[b.z][:, k, :]) for k in range(KC)])
                product(pe, a.misc[0:CTXP, DIM:2 * DIM],
                        [(a.ctx_hi[b.z][:, k, :], a.ctx_lo[b.z][:, k, :], a.w_hi[:, WV, k, :], a.w_lo[:, WV, k, :])
                         for k in range(KC)]).then_inc(a.kv_ps, 1)

            def transpose_x(b):
                pe.wait_ge(a.ln_done, b.count + 1)
                pe.wait_ge(a.kv_done, b.count + 1)
                for k in range(KC):
                    for t in range(BT):
                        last = pe.transpose(a.misc[:, k * SEQ + t * P:k * SEQ + (t + 1) * P],
                                            a.xn[:, t, k * P:(k + 1) * P], ident[:])
                last.then_inc(a.xt_ps, 1)

            def queries(b):
                pe.wait_ge(a.x_split, b.count + 1)
                for m in range(KC):
                    last = product(pe, a.misc[:, m * SEQ:(m + 1) * SEQ],
                                   [(a.w_hi[:, WQ, k, m * P:(m + 1) * P], a.w_lo[:, WQ, k, m * P:(m + 1) * P],
                                     a.x_hi[:, k, :], a.x_lo[:, k, :]) for k in range(KC)])
                last.then_inc(a.q_ps, 1)

            def score(b, j):
                u = UNITS * b.count + j
                m, qt = j // BT, j % BT
                pe.wait_ge(a.kd_done, b.count + 1)
                pe.wait_ge(a.q_split, b.count + 1)
                after(pe, a.scores_read, u - 1)
                q_hi = a.q_hi[b.z][:, m, qt * P:(qt + 1) * P]
                q_lo = a.q_lo[b.z][:, m, qt * P:(qt + 1) * P]
                for c in range(2):
                    heads = slice(c * HPC // 2, (c + 1) * HPC // 2)
                    ps = a.scores[:, j % 2, c, 0:HPC // 2 * CTXP].rearrange("p (h n) -> p h n", n=CTXP)
                    product(pe, ps, [(q_hi, q_lo, a.kd_hi[b.z][:, m, heads, :], a.kd_lo[b.z][:, m, heads, :])],
                            stop=False)
                    if a.stage == 0:
                        lhs, mask = a.ident[:], a.mask[:, qt, :].unsqueeze(1)
                    else:
                        lhs, mask = ones_r[0:1, :], a.mask[:, bass.ds(b.n, 1), :]
                    last = pe.matmul(ps, lhs, mask.broadcast_to([mask.shape[0], HPC // 2, CTXP]),
                                     start=False, stop=True)
                last.then_inc(a.scores_ps, 1)

            def transpose_prob(b, j):
                u = UNITS * b.count + j
                pe.wait_ge(a.exp_done, u + 1)
                after(pe, a.pt_done, u)
                for c in range(PC):
                    last = pe.transpose(a.prob_t_ps[:, c, :], a.pairs[j % 2][:, c, :], ident[:])
                last.then_inc(a.pt_ps, 1)

            def weigh_values(b, j):
                u = UNITS * b.count + j
                pe.wait_ge(a.pt_done, u + 1)
                after(pe, a.o_done, u)
                if j == 1:
                    after(pe, a.o_split, b.count)
                if j == 0:
                    pe.wait_ge(a.v_spread[b.z], 16 * PIECES * (b.half + a.base // 2 + 1))
                for c in range(PC):
                    first, heads = heads_of(c)
                    at = column_of(c)
                    last = pe.matmul(a.o_ps[:, first:first + heads, :], a.prob_t[j % 2][:, c, :],
                                     a.v_diagonal[b.z][:, j // BT, at:at + heads * VW].rearrange("p (h n) -> p h n", n=VW),
                                     start=c == 0, stop=c == PC - 1, skip_group_check=True)
                last.then_inc(a.pv_ps, 1)

            def transpose_o(b, later):
                pe.wait_ge(a.o_done, UNITS * (b.count + 1) + later)
                for k in range(KC):
                    for t in range(BT):
                        last = pe.transpose(a.o_t_bank[:, k * SEQ + t * P:k * SEQ + (t + 1) * P],
                                            a.o[b.z][:, t, k * P:(k + 1) * P], ident[:])
                last.then_inc(a.ot_ps, 1)

            def project(b, ahead):
                pe.wait_ge(a.o_split, b.count + 1)
                if ahead:
                    pe.wait_ge(a.q_split, b.count + 3)
                else:
                    pe.wait_ge(a.y_done, b.count)
                for t in range(BT):
                    ps = a.misc[:, t * DIM:(t + 1) * DIM]
                    product(pe, ps, [(a.o_hi[:, k, t * P:(t + 1) * P], a.o_lo[:, k, t * P:(t + 1) * P],
                                      a.w_hi[:, WP, k, :], a.w_lo[:, WP, k, :]) for k in range(KC)], stop=False)
                    pe.matmul(ps, ones_r[0:1, :], a.bias_hi[:], start=False, stop=False)
                    last = pe.matmul(ps, ones_r[0:1, :], a.bias_lo[:], start=False, stop=True)
                last.then_inc(a.y_ps, 1)

            pe.wait_ge(consts_done, 1)
            pe.wait_ge(a.bias_split, a.stage + 1)
            pe.wait_ge(a.mask_done, a.stage + 1)
            pe.wait_ge(a.v_ones, 2 * (a.stage + 1))
            pe.wait_ge(a.w_split, 4 * (a.stage + 1))
            first = Block(0, 0, 0, a.base)
            keys_values(first)
            transpose_x(first)
            queries(first)

            def body(b, behind, ahead):
                score(b, 0)
                if behind:
                    weigh_values(b.last(), 2)
                    transpose_prob(b.last(), 3)
                score(b, 1)
                if ahead:
                    keys_values(b.next())
                if behind:
                    weigh_values(b.last(), 3)
                transpose_prob(b, 0)
                if ahead:
                    transpose_x(b.next())
                score(b, 2)
                weigh_values(b, 0)
                transpose_prob(b, 1)
                score(b, 3)
                if behind:
                    transpose_o(b.last(), 1)
                if ahead:
                    queries(b.next())
                weigh_values(b, 1)
                transpose_prob(b, 2)
                if behind:
                    project(b.last(), ahead)

            paired_blocks(pe, BATCH, body, a.base)
            final = Block(BATCH - 1, 1, (BATCH - 2) // 2, a.base)
            weigh_values(final, 2)
            transpose_prob(final, 3)
            weigh_values(final, 3)
            transpose_o(final, 0)
            project(final, False)

        def attention_on_gpsimd(pool, a, z_kept, side_job):
            def split_context(b):
                pool.wait_ge(a.ctx_in[b.z], 16 * (b.half + a.base // 2 + 1))
                after(pool, a.kv_ps, b.count - 1)
                pool.tensor_tensor(a.ctx_hi[b.z][:], a.ctx[b.z][:], one([P, KC, CTXP]), ALU.mult).then_inc(a.ctx_round, 1)
                pool.wait_ge(a.ctx_round, b.count + 1)
                pool.tensor_tensor(a.ctx_lo[b.z][:], a.ctx[b.z][:], a.ctx_hi[b.z][:].bitcast(F32),
                                   ALU.subtract).then_inc(a.ctx_split, 1)

            def inverse_std(b):
                pool.wait_ge(a.ln_stats, b.count + 1)
                after(pool, a.ln_done, b.count)
                pool.tensor_tensor(a.var_eps[:], a.mv[:, :, 1], eps_tile[:, 0:BT], ALU.add).then_inc(a.ln_eps, 1)
                pool.wait_ge(a.ln_eps, b.count + 1)
                pool.tensor_tensor(a.rstd[:], a.var_eps[:], neghalf[:, 0:BT], ALU.pow).then_inc(a.ln_rstd, 1)

            def keep_query(b):
                pool.wait_ge(a.ln_done, b.count + 1)
                pool.tensor_tensor(z_kept[:, bass.ds(BT * b.n, BT), :], a.xn[:], one([P, BT, DIM]),
                                   ALU.mult).then_inc(a.ln_kept, 1)

            def diagonal_keys(b):
                pool.wait_ge(a.kv_done, b.count + 1)
                pool.tensor_tensor(a.k_round[:], a.k[:], one([P, KC, CTXP]), ALU.mult).then_inc(a.k_rounded, 1)
                pool.wait_ge(a.k_rounded, b.count + 1)
                pool.tensor_tensor(a.k_rest[:], a.k[:], a.k_round[:].bitcast(F32),
                                   ALU.subtract).then_inc(a.k_residue, 1)
                pool.wait_ge(a.k_residue, b.count + 1)
                hm = headmask[:].unsqueeze(2).broadcast_to([P, HPC, CTXP])
                for part, kd in ((a.k, a.kd_hi), (a.k_rest, a.kd_lo)):
                    for m in range(KC):
                        last = pool.tensor_tensor(kd[b.z][:, m], part[:, m, :].unsqueeze(1).broadcast_to([P, HPC, CTXP]),
                                                  hm, ALU.mult)
                last.then_inc(a.kd_done, 1)

            def slots_of(b):
                after(pool, a.mixed, 2 * (b.n - 1))
                pool.tensor_copy(a.slot[b.z][:], slots[:, bass.ds(BT * b.n, BT), :]).then_inc(a.slot_copied, 1)
                pool.wait_ge(a.slot_copied, b.n + 1)

            def fetch(b):
                for t in range(BT):
                    for s in range(2):
                        pool.indirect_dma_start(a.rows[b.z][:, t, s, :], None, d["sorted_y"],
                                                bass.IndirectOffsetOnAxis(ap=a.slot[b.z][:, t, s:s + 1], axis=0)).then_inc(a.rows_in[b.z], 16)

            first = Block(0, 0, 0, a.base)
            if a.stage == 1:
                for b in (first, first.next()):
                    slots_of(b)
                    fetch(b)
            for z in range(2):
                pool.memset(a.v[z][:], 1.0)
                pool.memset(a.pairs[z][:], 0.0)
                pool.memset(a.v_diagonal[z][:], 0.0).then_inc(a.v_ones, 1)
            split_context(first)
            inverse_std(first)
            if a.stage == 1:
                keep_query(first)
            diagonal_keys(first)
            split_context(first.next())

            def body(b, behind, ahead):
                if ahead:
                    inverse_std(b.next())
                    diagonal_keys(b.next())
                if ahead > 1:
                    if a.stage == 1:
                        slots_of(b.next().next())
                if ahead and a.stage == 1:
                    keep_query(b.next())
                if ahead > 1:
                    if a.stage == 1:
                        fetch(b.next().next())
                    split_context(b.next().next())
                side_job(b)

            paired_blocks(pool, BATCH, body, a.base, 3)

        class TokenSignals:
            bn_done = sem("t_bn_done")
            ln_stats = sem("t_ln_stats")
            ln_rstd = sem("t_ln_rstd")
            ln_done = sem("t_ln_done")
            xt_ps = sem("t_xt_ps")
            x_round = sem("t_x_round")
            x_split = sem("t_x_split")

        class Mixture(TokenSignals):

            def __init__(self, scope):
                two = range(2)
                sb(scope, "moe_w_place", [P, (EXPERTS + 1) * EXPERT_COLS], F32R)
                self.w = moe_w
                self.raw = [sb(scope, f"late_raw{z}", [P, LATE_PART]) for z in two]
                self.gate_raw = sb(scope, "gate_raw", [P, KC, EXPERTS])
                self.gate_hi = sb(scope, "gate_hi", [P, KC, EXPERTS], F32R)
                self.gate_lo = sb(scope, "gate_lo", [P, KC, EXPERTS], F32R)
                self.b2 = sb(scope, "moe_b2", [EXPERTS + 1, DIM])
                self.b13 = sb(scope, "moe_b13", [2 * EXPERTS, 2 * DIM])
                self.b13_parts = sb(scope, "moe_b13_parts", [2 * EXPERTS, 2 * DIM], F32R)
                self.row_of = sb(scope, "m_row_of", [2 * EXPERTS, 3])
                self.chosen = sb(scope, "m_chosen", [2 * EXPERTS, SORTED])
                self.choice = [sb(scope, f"m_choice{z}", [2 * EXPERTS, P], F32R) for z in two]
                self.stats = sb(scope, "m_stats", [P, MT, 6])
                self.mv = sb(scope, "m_mv", [P, MT, 2])
                self.var_eps = sb(scope, "m_var_eps", [P, MT])
                self.rstd = sb(scope, "m_rstd", [P, MT])
                self.xn = sb(scope, "m_xn", [P, TILES, DIM])
                self.x_hi = [sb(scope, f"m_x_hi{z}", [P, KC, SEQ], F32R) for z in two]
                self.x_lo = [sb(scope, f"m_x_lo{z}", [P, KC, SEQ], F32R) for z in two]
                self.h = [sb(scope, f"m_h{z}", [P, KC, SEQ]) for z in two]
                self.h_hi = [sb(scope, f"m_h_hi{z}", [P, KC, SEQ], F32R) for z in two]
                self.h_lo = [sb(scope, f"m_h_lo{z}", [P, KC, SEQ], F32R) for z in two]
                self.coef_t = [sb(scope, f"m_coef_t{z}", [P, SEQ]) for z in two]
                self.c_t = [t[0:EXPERTS + 1, :] for t in self.coef_t]
                self.tile_x = [self.xn[:, z * GROUP:(z + 1) * GROUP, :] for z in two]
                self.tile_y = [self.xn[:, (2 + z) * GROUP:(3 + z) * GROUP, :] for z in two]

                def by_expert(buffer):
                    return buffer.rearrange("p (t e) -> p t e", e=EXPERTS)
                self.p, self.rest = (by_expert(self.h[0][:, n, :]) for n in two)
                self.count = [by_expert(self.h[1][:, n, :]) for n in two]
                self.pick = [by_expert(t[:]) for t in self.coef_t]
                self.both = by_expert(self.h_hi[0][:, 0, :])
                self.earlier = self.h[1][:, 1, 0:P]
                self.rank = sb(scope, "m_rank", [P, EXPERTS])
                self.top = sb(scope, "m_top", [P, TILES, 1])
                self.c = sb(scope, "m_c", [P, TILES, EXPERTS + 1])
                self.ends = [sb(scope, f"m_ends{n}", [P, EXPERTS]) for n in two]
                self.tiles_of = sb(scope, "m_tiles_of", [P, EXPERTS])
                self.number = sb(scope, "m_number", [2 * EXPERTS, SORTED])
                self.expert_f = sb(scope, "m_expert_f", [2 * EXPERTS, SORTED])
                self.expert = sb(scope, "m_expert", [1, SORTED], I32)
                self.earlier_r = sb(scope, "m_earlier_r", [P, P], F32R)
                self.up_ps = PSUM[:, 0:2, :].rearrange("p g (o n) -> p g o n", o=KC)
                self.tile_up_ps = PSUM[:, 0:2, :]
                self.xt_bank = PSUM[:, 2, :].rearrange("p (k n) -> p k n", k=KC)
                self.ht_bank = PSUM[:, 3, 0:DIM].rearrange("p (k n) -> p k n", k=KC)
                self.ct_bank = PSUM[0:EXPERTS + 1, 3, 0:SEQ]
                self.y_ps_bank = PSUM[:, 4, :].rearrange("p (t c) -> p t c", c=DIM)
                self.logits = PSUM[:, 5, 0:TILES * EXPERTS].rearrange("p (t e) -> p t e", e=EXPERTS)
                self.norm_bank = [PSUM[:, 6 + z, :].rearrange("p (k n) -> p k n", k=KC) for z in two]
                self.rank_ps = PSUM[:, 6, 0:TILES * EXPERTS]
                self.total_ps = PSUM[:, 7, 0:TILES * EXPERTS]
                self.late_in = [sem(f"m_late_in{z}") for z in two]
                self.tile_in = [sem(f"m_tile_in{z}") for z in two]
                self.tile_out = [sem(f"m_tile_out{z}") for z in two]
                self.small_in = sem("m_small_in")
                self.const_done = sem("m_const_done")
                self.small_round = sem("m_small_round")
                self.gate_split = sem("m_gate_split")
                self.late_round = sem("m_late_round")
                self.late_split = sem("m_late_split")
                self.bias_split = sem("m_bias_split")
                self.ln_eps = sem("m_ln_eps")
                self.logits_ps = sem("m_logits_ps")
                self.logits_read = sem("m_logits_read")
                self.gate_exp = sem("m_gate_exp")
                self.route = sem("m_route")
                self.picks_done = sem("m_picks_done")
                self.ranks_ps = sem("m_ranks_ps")
                self.slots_done = sem("m_slots_done")
                self.chosen_done = sem("m_chosen_done")
                self.scattered = sem("m_scattered")
                self.t_ps = sem("m_t_ps")
                self.t_round = sem("m_t_round")
                self.t_split = sem("m_t_split")
                self.c_copied = sem("m_c_copied")
                self.up_done = sem("m_up_done")
                self.silu_done = sem("m_silu_done")
                self.gated = sem("m_gated")
                self.ht_ps = sem("m_ht_ps")
                self.h_round = sem("m_h_round")
                self.h_split = sem("m_h_split")
                self.y_ps = sem("m_y_ps")
                self.y_done = sem("m_y_done")

            def chunk(self, n):
                return tuple(self.w[:, bass.ds((2 * n + part) * MOE_CHUNK, MOE_CHUNK)] for part in range(2))

        SHARED = BATCH
        LATE = [(n, half) for n in (*range(EXPERTS * 3, EXPERTS * 3 + 3), *range(EARLY_CHUNKS, EXPERTS * 3)) for half in range(2)]
        SHARED_PARTS = 3 * 2

        AHEAD = 2
        final_group = Block(GROUPS - 1, 1, (GROUPS - 2) // 2)

        def at(g, j, behind, ahead, step):
            if j < 0:
                if behind:
                    step(g.last(), j + GROUP)
            elif j < GROUP:
                step(g, j)
            elif ahead:
                step(g.next(), j - GROUP)

        def mixture_on_sync(sp, m):
            sp.wait_ge(a0.y_done, BATCH)
            sp.wait_ge(side_split, EARLY_CHUNKS)
            for dst, name in ((m.gate_raw[:].rearrange("p k e -> p (k e)"), "gate_w"), (m.b2[:], "moe_b2"),
                              (m.b13[:], "moe_b13"), (m.number[:], "tile_numbers"), (m.row_of[:], "row_of")):
                sp.dma_start(dst, d[name]).then_inc(m.small_in, 16)
            for n, (chunk, half) in enumerate(LATE):
                if n >= 2:
                    sp.wait_ge(m.late_split, n - 1)
                at = chunk * MOE_CHUNK + half * LATE_PART
                sp.dma_start(m.raw[n % 2][:], d["moe_w"][:, at:at + LATE_PART]).then_inc(m.late_in[n % 2], 16)
            sp.wait_ge(m.scattered, 16 * 2 * TILES)

            sorted_x, sorted_y = (d[n].rearrange("(t p) c -> p t c", p=P) for n in ("sorted_x", "sorted_y"))

            def load(g):
                after(sp, m.t_ps, SHARED + GROUP * (g.n - 1))
                sp.dma_start(m.tile_x[g.z], sorted_x[:, bass.ds(GROUP * g.n, GROUP), :]).then_inc(m.tile_in[g.z], 16)

            def store(g):
                sp.wait_ge(m.y_done, SHARED + GROUP * (g.n + 1))
                sp.dma_start(sorted_y[:, bass.ds(GROUP * g.n, GROUP), :], m.tile_y[g.z]).then_inc(m.tile_out[g.z], 16)

            sp.wait_ge(m.t_ps, SHARED)
            load(Block(0, 0, 0))

            def body(g, behind, ahead):
                if ahead:
                    load(g.next())
                if behind:
                    store(g.last())

            paired_blocks(sp, GROUPS, body)
            store(Block(GROUPS - 1, 1, (GROUPS - 2) // 2))

        def mixture_on_gpsimd(pool, m):
            pool.wait_ge(a0.y_done, BATCH)
            for e in range(EXPERTS):
                last = pool.memset(m.rank[:, e:e + 1], float(EXPERTS - e))
            last.then_inc(m.const_done, 1)
            pool.memset(m.c[:], 1.0).then_inc(m.const_done, 1)
            pool.memset(m.earlier, 1.0).then_inc(m.const_done, 1)
            pool.wait_ge(m.const_done, 3)
            pool.affine_select(out=m.earlier, in_=m.earlier, compare_op=ALU.is_ge, fill=0.0, base=-1,
                               pattern=[[1, P]], channel_multiplier=-1).then_inc(m.const_done, 1)

            def inverse_std(b):
                pool.wait_ge(m.ln_stats, 2 * (b.n + 1))
                after(pool, m.ln_done, 2 * b.n)
                pool.tensor_tensor(m.var_eps[:], m.mv[:, :, 1], eps_tile[:, 0:MT], ALU.add).then_inc(m.ln_eps, 1)
                pool.wait_ge(m.ln_eps, b.n + 1)
                pool.tensor_tensor(m.rstd[:], m.var_eps[:], neghalf[:, 0:MT], ALU.pow).then_inc(m.ln_rstd, 2)

            inverse_std(Block(0, 0, 0))

            def body(b, behind, ahead):
                if ahead:
                    inverse_std(b.next())

            paired_blocks(pool, MB, body)
            for n, (chunk, half) in enumerate(LATE):
                hi, lo = (w[:, half * LATE_PART:(half + 1) * LATE_PART] for w in m.chunk(chunk))
                pool.wait_ge(m.late_in[n % 2], 16 * (n // 2 + 1))
                pool.tensor_tensor(hi, m.raw[n % 2][:], one([P, LATE_PART]), ALU.mult).then_inc(m.late_round, 1)
                pool.wait_ge(m.late_round, n + 1)
                pool.tensor_tensor(lo, m.raw[n % 2][:], hi.bitcast(F32), ALU.subtract).then_inc(m.late_split, 1)
                if n == SHARED_PARTS - 1:
                    pool.wait_ge(m.slots_done, 1)
                    pool.wait_ge(zeros_out, 16 * (BATCH + 1))
                    for t in range(TILES):
                        for s in range(2):
                            pool.indirect_dma_start(d["sorted_x"], bass.IndirectOffsetOnAxis(ap=slots[:, t, s:s + 1], axis=0),
                                                    m.xn[:, t, :], None).then_inc(m.scattered, 16)
            pool.wait_ge(m.slots_done, 2)

            def choose(g, behind, ahead):
                for j in range(GROUP):
                    n = GROUP * g.n + j
                    after(pool, m.up_done, SHARED + n - 1)
                    column = m.chosen[:, bass.ds(n, 1)].broadcast_to([2 * EXPERTS, P])
                    pool.tensor_tensor(m.choice[j % 2][:], column, ones[0:2 * EXPERTS, :], ALU.mult).then_inc(m.chosen_done, 1)

            paired_blocks(pool, GROUPS, choose)

        def mixture_on_scalar(act, m):
            act.wait_ge(a0.y_done, BATCH)
            act.wait_ge(m.small_in, 80)
            act.activation(m.gate_hi[:], m.gate_raw[:], ACT.Copy).then_inc(m.small_round, 1)
            act.activation(m.b13_parts[:], m.b13[:], ACT.Copy).then_inc(m.small_round, 1)

            def norm_rounded(b):
                act.wait_ge(m.xt_ps, b.n + 1)
                act.activation(m.x_hi[b.z][:], m.norm_bank[b.z], ACT.Copy).then_inc(m.x_round, 1)

            paired_blocks(act, BATCH, lambda b, behind, ahead: norm_rounded(b))
            act.wait_ge(m.logits_read, 1)
            act.activation(m.p, m.p, ACT.Exp).then_inc(m.gate_exp, 1)

            def shared_rounded(b):
                act.wait_ge(m.t_ps, b.n + 1)
                act.activation(m.x_hi[b.z][:], m.xt_bank, ACT.Copy).then_inc(m.t_round, 1)

            def coefficients(b):
                act.wait_ge(m.t_ps, b.n + 1)
                after(act, m.y_ps, b.n - 1)
                act.activation(m.c_t[b.z][:], m.ct_bank, ACT.Copy).then_inc(m.c_copied, 1)

            shared_rounded(Block(0, 0, 0))
            coefficients(Block(0, 0, 0))

            def shared(b, behind, ahead):
                act.wait_ge(m.up_done, b.n + 1)
                after(act, m.h_split, b.n - 1)
                for o in range(KC):
                    last = act.activation(m.h[b.z][:, o], m.up_ps[:, 0, o], ACT.Silu, bias=cols[:, COL_B1 + o:COL_B1 + o + 1])
                last.then_inc(m.silu_done, 1)
                if ahead:
                    shared_rounded(b.next())
                act.wait_ge(m.gated, b.n + 1)
                after(act, m.y_ps, b.n - 1)
                act.activation(m.h_hi[b.z][:], m.h[b.z][:], ACT.Copy).then_inc(m.h_round, 1)
                if ahead:
                    coefficients(b.next())

            paired_blocks(act, BATCH, shared)

            def x_rounded(g, j):
                act.wait_ge(m.t_ps, SHARED + GROUP * g.n + j + 1)
                act.activation(m.x_hi[j % 2][:, :, 0:P], m.xt_bank[:, :, 0:P], ACT.Copy).then_inc(m.t_round, 1)

            def activate(g, j):
                act.wait_ge(m.up_done, SHARED + GROUP * g.n + j + 1)
                act.activation(m.h[j % 2][:, 0], m.tile_up_ps[:, j % 2, 0:DIM], ACT.Silu).then_inc(m.silu_done, 1)

            def h_rounded(g, j):
                act.wait_ge(m.ht_ps, GROUP * g.n + j + 1)
                act.activation(m.h_hi[j % 2][:, :, 0:P], m.ht_bank, ACT.Copy).then_inc(m.h_round, 1)

            def output(g, j):
                act.wait_ge(m.y_ps, SHARED + GROUP * g.n + j + 1)
                if j == 0:
                    after(act, m.tile_out[g.z], 16 * g.half)
                act.activation(m.tile_y[g.z][:, j, :], m.y_ps_bank[:, 0], ACT.Copy).then_inc(m.y_done, 1)

            act.wait_ge(m.y_ps, SHARED)
            act.wait_ge(m.scattered, 16 * 2 * TILES)
            for j in range(AHEAD):
                x_rounded(Block(0, 0, 0), j)

            def tiles_of(g, behind, ahead):
                for j in range(GROUP):
                    activate(g, j)
                    at(g, j - 1, behind, ahead, h_rounded)
                    at(g, j + AHEAD, behind, ahead, x_rounded)
                    at(g, j - 2, behind, ahead, output)

            paired_blocks(act, GROUPS, tiles_of)
            h_rounded(final_group, GROUP - 1)
            output(final_group, GROUP - 2)
            output(final_group, GROUP - 1)

        def mixture_on_vector(dve, m):
            def ln_stats(b):
                for t in range(MT):
                    last = dve.bn_stats(m.stats[:, t, :], x[:, bass.ds(MT * b.n + t, 1), :])
                last.then_inc(m.bn_done, 2)

            def ln_aggregate(b):
                for t in range(MT):
                    last = dve.bn_aggr(m.mv[:, t, :], m.stats[:, t, :])
                last.then_inc(m.ln_stats, 2)

            def ln_apply(b):
                dve.wait_ge(m.ln_rstd, 2 * (b.n + 1))
                for t in range(MT):
                    xt = x[:, bass.ds(MT * b.n + t, 1), :].rearrange("p o c -> p (o c)")
                    last = dve.tensor_scalar(m.xn[:, bass.ds(MT * b.n + t, 1), :].rearrange("p o c -> p (o c)"), xt,
                                             m.mv[:, t, 0:1], m.rstd[:, t:t + 1], ALU.subtract, ALU.mult)
                    if t % BT == BT - 1:
                        last.then_inc(m.ln_done, 1)

            def norm_residue(b, half):
                n = 2 * b.n + half
                dve.wait_ge(m.x_round, n + 1)
                dve.tensor_tensor(m.x_lo[half][:], m.norm_bank[half], m.x_hi[half][:].bitcast(F32),
                                  ALU.subtract).then_inc(m.x_split, 1)

            dve.wait_ge(a0.y_done, BATCH)
            first = Block(0, 0, 0)
            ln_stats(first)
            dve.wait_ge(m.small_round, 1)
            dve.tensor_tensor(m.gate_lo[:], m.gate_raw[:], m.gate_hi[:].bitcast(F32), ALU.subtract).then_inc(m.gate_split, 1)
            dve.wait_ge(m.bn_done, 2)
            ln_aggregate(first)
            ln_apply(first)

            def norm(b, behind, ahead):
                if ahead:
                    ln_stats(b.next())
                    dve.wait_ge(m.bn_done, 2 * (b.n + 2))
                norm_residue(b, 0)
                if ahead:
                    ln_aggregate(b.next())
                norm_residue(b, 1)
                if ahead:
                    ln_apply(b.next())

            paired_blocks(dve, MB, norm)

            wide = [P, TILES, EXPERTS]
            top = m.top[:].broadcast_to(wide)
            count = [0]

            def step(instruction):
                count[0] += 1
                instruction.then_inc(m.route, 1)
                dve.wait_ge(m.route, count[0])

            def largest(pick, values):
                rank = m.rank[:].unsqueeze(1).broadcast_to(wide)
                step(dve.tensor_reduce(m.top[:, :, 0], values, AX.X, ALU.max))
                step(dve.tensor_tensor(pick, values, top, ALU.is_ge))
                step(dve.tensor_tensor(pick, pick, rank, ALU.mult))
                step(dve.tensor_reduce(m.top[:, :, 0], pick, AX.X, ALU.max))
                step(dve.tensor_tensor(pick, pick, top, ALU.is_equal))

            dve.wait_ge(m.const_done, 4)
            step(dve.tensor_copy(m.earlier_r[:], m.earlier))
            dve.wait_ge(m.logits_ps, BATCH)
            step(dve.tensor_reduce(m.top[:, :, 0], m.logits, AX.X, ALU.max))
            dve.tensor_tensor(m.p, m.logits, top, ALU.subtract).then_inc(m.logits_read, 1)
            dve.wait_ge(m.gate_exp, 1)
            step(dve.tensor_reduce(m.top[:, :, 0], m.p, AX.X, ALU.add))
            step(dve.reciprocal(m.top[:], m.top[:]))
            step(dve.tensor_tensor(m.p, m.p, top, ALU.mult))
            largest(m.pick[0], m.p)
            step(dve.scalar_tensor_tensor(m.rest, m.pick[0], -2.0, m.p, ALU.mult, ALU.add))
            largest(m.pick[1], m.rest)
            dve.tensor_tensor(m.both, m.pick[0], m.pick[1], ALU.add).then_inc(m.picks_done, 1)
            dve.wait_ge(m.picks_done, 1)
            step(dve.tensor_tensor(m.c[:, :, 0:EXPERTS], m.p, m.both.bitcast(F32), ALU.mult))
            for s in range(2):
                step(dve.tensor_tensor(m.rest, m.p, m.pick[s], ALU.mult))
                step(dve.tensor_reduce(m.top[:, :, 0], m.rest, AX.X, ALU.add))
                step(dve.tensor_scalar(weight[:, :, s:s + 1], m.top[:], gates[:, 2:3], None, ALU.mult))
            dve.wait_ge(m.ranks_ps, 1)
            totals = m.total_ps.rearrange("p (t e) -> p t e", e=EXPERTS)
            step(dve.tensor_copy(m.count[0], totals))
            z, reach = 0, 1
            while reach < TILES:
                step(dve.tensor_copy(m.count[1 - z][:, 0:reach], m.count[z][:, 0:reach]))
                step(dve.tensor_tensor(m.count[1 - z][:, reach:], m.count[z][:, reach:], m.count[z][:, :TILES - reach], ALU.add))
                z, reach = 1 - z, 2 * reach
            counted, other = m.count[z], m.count[1 - z]
            step(dve.tensor_scalar(m.tiles_of[:], counted[:, TILES - 1], 1.0 / P, (P - 0.5) / P - 0.5, ALU.mult, ALU.add))
            step(dve.tensor_scalar(m.tiles_of[:], m.tiles_of[:], ROUND, None, ALU.add))
            step(dve.tensor_scalar(m.tiles_of[:], m.tiles_of[:], ROUND, None, ALU.subtract))
            step(dve.tensor_copy(m.ends[0][:], m.tiles_of[:]))
            y, reach = 0, 1
            while reach < EXPERTS:
                step(dve.tensor_copy(m.ends[1 - y][:, 0:reach], m.ends[y][:, 0:reach]))
                step(dve.tensor_tensor(m.ends[1 - y][:, reach:], m.ends[y][:, reach:], m.ends[y][:, :EXPERTS - reach], ALU.add))
                y, reach = 1 - y, 2 * reach
            ends, starts = m.ends[y], m.ends[1 - y]
            step(dve.tensor_tensor(starts[:], ends[:], m.tiles_of[:], ALU.subtract))
            step(dve.tensor_scalar(starts[:], starts[:], float(P), None, ALU.mult))
            step(dve.tensor_tensor(other, counted[:], totals, ALU.subtract))
            step(dve.tensor_tensor(other, other, m.rank_ps.rearrange("p (t e) -> p t e", e=EXPERTS), ALU.add))
            step(dve.tensor_tensor(other, other, starts[:].unsqueeze(1).broadcast_to(wide), ALU.add))
            for s in range(2):
                step(dve.tensor_tensor(m.rest, other, m.pick[s], ALU.mult))
                step(dve.tensor_reduce(m.top[:, :, 0], m.rest, AX.X, ALU.add))
                last = dve.tensor_copy(slots[:, :, s:s + 1], m.top[:])
                if s == 0:
                    step(last)
            last.then_inc(m.slots_done, 1)
            rows = 2 * EXPERTS
            step(dve.tensor_scalar(m.expert_f[:], m.number[:], ends[0:rows, 0:1], None, ALU.is_ge))
            for e in range(1, EXPERTS):
                step(dve.scalar_tensor_tensor(m.expert_f[:], m.number[:], ends[0:rows, e:e + 1], m.expert_f[:], ALU.is_ge, ALU.add))
            step(dve.tensor_scalar(m.expert_f[:], m.expert_f[:], EXPERTS - 1.0, None, ALU.min))
            step(dve.tensor_scalar(m.chosen[:], m.expert_f[:], m.row_of[:, 0:1], None, ALU.is_equal))
            dve.tensor_scalar(m.expert[:], m.expert_f[0:1, :], float(EXPERT_COLS), None, ALU.mult).then_inc(m.slots_done, 1)
            dve.wait_ge(m.small_round, 2)
            step(dve.tensor_tensor(m.b13[:], m.b13[:], m.b13_parts[:].bitcast(F32), ALU.subtract))
            step(dve.tensor_scalar(m.b13[:], m.b13[:], m.row_of[:, 2:3], None, ALU.mult))
            dve.scalar_tensor_tensor(m.b13_parts[:], m.b13_parts[:].bitcast(F32), m.row_of[:, 1:2], m.b13[:], ALU.mult,
                                     ALU.add).then_inc(m.bias_split, 1)

            def shared_residue(b):
                dve.wait_ge(m.t_round, b.n + 1)
                dve.tensor_tensor(m.x_lo[b.z][:], m.xt_bank, m.x_hi[b.z][:].bitcast(F32),
                                  ALU.subtract).then_inc(m.t_split, 1)

            def add(b):
                dve.wait_ge(m.y_ps, b.n + 1)
                xb = tiles(b)
                dve.scalar_tensor_tensor(xb, m.y_ps_bank, gates[:, 2:3], xb, ALU.mult, ALU.add).then_inc(m.y_done, 1)

            shared_residue(first)

            def shared(b, behind, ahead):
                dve.wait_ge(m.silu_done, b.n + 1)
                for o in range(KC):
                    last = dve.scalar_tensor_tensor(m.h[b.z][:, o], m.up_ps[:, 1, o], cols[:, COL_B3 + o:COL_B3 + o + 1],
                                                    m.h[b.z][:, o], ALU.add, ALU.mult)
                last.then_inc(m.gated, 1)
                if ahead:
                    shared_residue(b.next())
                dve.wait_ge(m.h_round, b.n + 1)
                dve.tensor_tensor(m.h_lo[b.z][:], m.h[b.z][:], m.h_hi[b.z][:].bitcast(F32), ALU.subtract).then_inc(m.h_split, 1)
                if behind:
                    add(b.last())

            paired_blocks(dve, BATCH, shared)
            add(Block(BATCH - 1, 1, (BATCH - 2) // 2))

            def x_residue(g, j):
                dve.wait_ge(m.t_round, SHARED + GROUP * g.n + j + 1)
                dve.tensor_tensor(m.x_lo[j % 2][:, :, 0:P], m.xt_bank[:, :, 0:P], m.x_hi[j % 2][:, :, 0:P].bitcast(F32),
                                  ALU.subtract).then_inc(m.t_split, 1)

            def h_residue(g, j):
                dve.wait_ge(m.h_round, SHARED + GROUP * g.n + j + 1)
                dve.tensor_tensor(m.h_lo[j % 2][:, :, 0:P], m.ht_bank, m.h_hi[j % 2][:, :, 0:P].bitcast(F32),
                                  ALU.subtract).then_inc(m.h_split, 1)

            def gate(g, j):
                dve.wait_ge(m.silu_done, SHARED + GROUP * g.n + j + 1)
                h = m.h[j % 2][:, 0]
                dve.tensor_tensor(h, m.tile_up_ps[:, j % 2, DIM:], h, ALU.mult).then_inc(m.gated, 1)

            for j in range(AHEAD):
                x_residue(first, j)

            def tiles_of(g, behind, ahead):
                for j in range(GROUP):
                    gate(g, j)
                    at(g, j - 1, behind, ahead, h_residue)
                    at(g, j + AHEAD, behind, ahead, x_residue)

            paired_blocks(dve, GROUPS, tiles_of)
            h_residue(final_group, GROUP - 1)

        def mixture_on_tensor(pe, m):
            def every_block(body):
                for n in range(BATCH):
                    body(Block(n, n % 2, n // 2), n > 0, n < BATCH - 1)

            def transpose_normed(b, bank):
                tokens = m.xn[:, BT * b.n:BT * (b.n + 1), :]
                for k in range(KC):
                    for t in range(BT):
                        last = pe.transpose(bank[:, k, t * P:(t + 1) * P], tokens[:, t, k * P:(k + 1) * P], ident[:])
                return last

            def norm_transposed(b):
                pe.wait_ge(m.ln_done, b.n + 1)
                transpose_normed(b, m.norm_bank[b.z]).then_inc(m.xt_ps, 1)

            def logits(b):
                pe.wait_ge(m.x_split, b.n + 1)
                for t in range(BT):
                    part = slice(t * P, (t + 1) * P)
                    last = product(pe, m.logits[:, bass.ds(BT * b.n + t, 1), :],
                                   [(m.x_hi[b.z][:, k, part], m.x_lo[b.z][:, k, part], m.gate_hi[:, k:k + 1], m.gate_lo[:, k:k + 1])
                                    for k in range(KC)])
                last.then_inc(m.logits_ps, 1)

            pe.wait_ge(m.gate_split, 1)
            norm_transposed(Block(0, 0, 0))

            def norm(b, behind, ahead):
                if ahead:
                    norm_transposed(b.next())
                logits(b)

            every_block(norm)

            def shared_transposed(b):
                after(pe, m.c_copied, b.n)
                transpose_normed(b, m.xt_bank)
                for t in range(BT):
                    last = pe.transpose(m.ct_bank[:, t * P:(t + 1) * P],
                                        m.c[:, BT * b.n + t, :], ident[:])
                last.then_inc(m.t_ps, 1)

            pe.wait_ge(m.picks_done, 1)
            both = m.both.rearrange("p t e -> p (t e)")
            pe.matmul(m.rank_ps, m.earlier_r[:], both, start=True, stop=True)
            pe.matmul(m.total_ps, ones_r[:], both, start=True, stop=True).then_inc(m.ranks_ps, 1)
            pe.wait_ge(m.slots_done, 1)
            shared_transposed(Block(0, 0, 0))
            pe.wait_ge(m.late_split, SHARED_PARTS)
            first_chunk = EXPERTS * 3
            up_w = [m.chunk(first_chunk + k) for k in range(KC)]
            down_w = [w.rearrange("p (k c) -> p k c", k=KC) for w in m.chunk(first_chunk + KC)]

            def shared_down(b):
                pe.wait_ge(m.h_split, b.n + 1)
                pe.wait_ge(m.c_copied, b.n + 1)
                after(pe, m.y_done, b.n)
                for t in range(BT):
                    part = slice(t * P, (t + 1) * P)
                    product(pe, m.y_ps_bank[:, t], [(m.h_hi[b.z][:, k, part], m.h_lo[b.z][:, k, part], down_w[0][:, k], down_w[1][:, k])
                                                    for k in range(KC)], stop=False)
                    last = pe.matmul(m.y_ps_bank[:, t], m.c_t[b.z][:, part], m.b2[:], start=False, stop=True)
                last.then_inc(m.y_ps, 1)

            def shared(b, behind, ahead):
                pe.wait_ge(m.t_split, b.n + 1)
                after(pe, m.gated, b.n)
                for g in range(2):
                    for o in range(KC):
                        part = slice(g * DIM + o * P, g * DIM + (o + 1) * P)
                        last = product(pe, m.up_ps[:, g, o], [(up_w[k][0][:, part], up_w[k][1][:, part],
                                                               m.x_hi[b.z][:, k], m.x_lo[b.z][:, k]) for k in range(KC)])
                last.then_inc(m.up_done, 1)
                if ahead:
                    shared_transposed(b.next())
                if behind:
                    shared_down(b.last())

            every_block(shared)
            shared_down(Block(BATCH - 1, 1, (BATCH - 2) // 2))

            def transpose_x(g, j):
                if j == 0:
                    pe.wait_ge(m.tile_in[g.z], 16 * (g.half + 1))
                pe.wait_ge(m.t_split, SHARED + GROUP * g.n + j)
                for k in range(KC):
                    last = pe.transpose(m.xt_bank[:, k, 0:P], m.tile_x[g.z][:, j, k * P:(k + 1) * P], ident[:])
                last.then_inc(m.t_ps, 1)

            def weights(g, j):
                return pe.value_load(m.expert[0:1, bass.ds(GROUP * g.n + j, 1)], min_val=0, max_val=(EXPERTS - 1) * EXPERT_COLS)

            def part(at, n):
                return m.w[:, bass.ds(at + n * MOE_CHUNK, MOE_CHUNK)]

            def up(g, j, w):
                n = GROUP * g.n + j
                pe.wait_ge(m.chosen_done, n + 1)
                pe.wait_ge(m.t_split, SHARED + n + 1)
                ps = m.tile_up_ps[:, j % 2, :]
                pe.matmul(ps, m.choice[j % 2][:], m.b13_parts[:], start=True, stop=False, skip_group_check=True)
                product(pe, ps, [(m.x_hi[j % 2][:, k, 0:P], m.x_lo[j % 2][:, k, 0:P], part(w, 2 * k), part(w, 2 * k + 1))
                                 for k in range(KC)], start=False).then_inc(m.up_done, 1)

            def transpose_h(g, j):
                n = GROUP * g.n + j
                pe.wait_ge(m.gated, SHARED + n + 1)
                pe.wait_ge(m.h_split, SHARED + n)
                for k in range(KC):
                    last = pe.transpose(m.ht_bank[:, k], m.h[j % 2][:, 0, k * P:(k + 1) * P], ident[:])
                last.then_inc(m.ht_ps, 1)

            def down(g, j, w):
                n = GROUP * g.n + j
                hi, lo = (part(w, 2 * KC + n).rearrange("p (k c) -> p k c", k=KC) for n in range(2))
                pe.wait_ge(m.h_split, SHARED + n + 1)
                pe.wait_ge(m.y_done, SHARED + n)
                product(pe, m.y_ps_bank[:, 0], [(m.h_hi[j % 2][:, k, 0:P], m.h_lo[j % 2][:, k, 0:P], hi[:, k], lo[:, k])
                                                for k in range(KC)]).then_inc(m.y_ps, 1)

            pe.wait_ge(m.slots_done, 2)
            pe.wait_ge(m.bias_split, 1)
            pe.wait_ge(m.late_split, len(LATE))
            for j in range(AHEAD):
                transpose_x(Block(0, 0, 0), j)

            def tiles_of(g, behind, ahead):
                offset = {j: weights(g.last(), j + GROUP) for j in (-2, -1) if behind}
                for j in range(GROUP):
                    offset[j] = weights(g, j)
                    up(g, j, offset[j])
                    at(g, j - 1, behind, ahead, transpose_h)
                    at(g, j + AHEAD, behind, ahead, transpose_x)
                    at(g, j - 2, behind, ahead, lambda group, tile: down(group, tile, offset[j - 2]))

            paired_blocks(pe, GROUPS, tiles_of)
            transpose_h(final_group, GROUP - 1)
            for j in (GROUP - 2, GROUP - 1):
                down(final_group, j, weights(final_group, j))

        class ParameterSignals(TokenSignals):
            small_in = sem("p_small_in")
            bias_round = sem("p_bias_round")
            bias_split = sem("p_bias_split")

        class FeedForward(ParameterSignals):

            def __init__(self, scope):
                two, four = range(2), range(4)
                self.norms = sb(scope, "f_norms", [P, 4, DIM])
                self.out_g = sb(scope, "f_out_g", [P, DIM])
                self.out_b = sb(scope, "f_out_b", [P, DIM])
                self.bias_raw = sb(scope, "f_bias_raw", [1, DIM])
                self.bias_hi = sb(scope, "f_bias_hi", [1, DIM], F32R)
                self.bias_lo = sb(scope, "f_bias_lo", [1, DIM], F32R)
                self.stats1 = sb(scope, "f_stats1", [P, MT, 6])
                self.stats2 = sb(scope, "f_stats2", [P, MT, 6])
                self.mv1 = sb(scope, "f_mv1", [P, MT, 2])
                self.mv2 = sb(scope, "f_mv2", [P, MT, 2])
                self.var1 = sb(scope, "f_var1", [P, MT])
                self.var2 = sb(scope, "f_var2", [P, MT])
                self.rstd1 = sb(scope, "f_rstd1", [P, MT])
                self.rstd2 = sb(scope, "f_rstd2", [P, MT])
                self.x1 = [sb(scope, f"f_x1{z}", [P, MT, DIM]) for z in two]
                self.y = sb(scope, "f_y", [P, MT, DIM])
                self.x_hi = [sb(scope, f"f_x_hi{z}", [P, KC, MN], F32R) for z in two]
                self.x_lo = [sb(scope, f"f_x_lo{z}", [P, KC, MN], F32R) for z in two]
                self.h = [sb(scope, f"f_h{z}", [P, MN]) for z in four]
                self.h_hi = [sb(scope, f"f_h_hi{z}", [P, MN], F32R) for z in four]
                self.h_lo = [sb(scope, f"f_h_lo{z}", [P, MN], F32R) for z in four]
                self.up_ps = PSUM[:, 0:4, :]
                self.y_ps_bank = PSUM[:, 4:6, :]
                self.xt_bank = PSUM[:, 6:8, :]
                self.base = BATCH
                self.const_done = sem("f_const_done")
                self.y_sum = sem("f_y_sum")
                self.bn2_done = sem("f_bn2_done")
                self.agg2_done = sem("f_agg2_done")
                self.ln2_stats = sem("f_ln2_stats")
                self.agg1_done = sem("f_agg1_done")
                self.ln2_rstd = sem("f_ln2_rstd")
                self.ln2_done = sem("f_ln2_done")
                self.out_scaled = sem("f_out_scaled")
                self.out_ready = sem("f_out_ready")
                self.x_done = sem("f_x_done")
                self.x1_scaled = sem("f_x1_scaled")
                self.x1_done = sem("f_x1_done")
                self.up_done = sem("f_up_done")
                self.gelu_done = sem("f_gelu_done")
                self.h_round = sem("f_h_round")
                self.h_split = sem("f_h_split")
                self.y_ps = sem("f_y_ps")

        def ffn_on_scalar(act, f):
            act.wait_ge(a1.y_done, 2 * BATCH)
            act.wait_ge(side_split, 2 * BATCH)
            act.dma_start(f.norms[:].rearrange("p r c -> p (r c)"),
                          d["norms"].rearrange("r c -> (r c)").partition_broadcast(P)).then_inc(f.small_in, 16)
            act.dma_start(f.bias_raw[:], d["bias"][2:3]).then_inc(f.small_in, 16)
            act.wait_ge(f.small_in, 32)
            act.activation(f.bias_hi[:], f.bias_raw[:], ACT.Copy).then_inc(f.bias_round, 1)
            act.activation(f.out_g[:], f.norms[:, 2], ACT.Copy, scale=gates[:, 1:2])
            act.activation(f.out_b[:], f.norms[:, 3], ACT.Copy, scale=gates[:, 1:2]).then_inc(f.const_done, 1)

            def x_rounded(b):
                act.wait_ge(f.xt_ps, b.count + 1)
                act.activation(f.x_hi[b.z][:], f.xt_bank, ACT.Copy).then_inc(f.x_round, 1)

            x_rounded(Block(0, 0, 0, f.base))

            def body(b, behind, ahead):
                for m in range(HC):
                    at = HC * b.n + m
                    act.wait_ge(f.up_done, at + 1)
                    after(act, f.h_split, at - 3)
                    act.activation(f.h[m % 4][:], f.up_ps[:, m % 4], ACT.Gelu,
                                   bias=cols[:, COL_FB1 + m:COL_FB1 + m + 1]).then_inc(f.gelu_done, 1)
                    act.wait_ge(f.gelu_done, at + 1)
                    act.activation(f.h_hi[m % 4][:], f.h[m % 4][:], ACT.Copy).then_inc(f.h_round, 1)
                    if m == HC - 1 and ahead:
                        x_rounded(b.next())
                if not ahead:
                    ternary_rows_on_scalar(act, w)

            paired_blocks(act, MB, body, f.base)

        def ffn_on_gpsimd(pool, f):
            pool.wait_ge(f.const_done, 1)

            def norm_1(b):
                pool.wait_ge(f.ln_stats, b.count + 1)
                pool.tensor_tensor(f.rstd1[:], f.var1[:], neghalf[:, 0:MT], ALU.pow).then_inc(f.ln_rstd, 1)

            def affine_1(b):
                pool.wait_ge(f.ln_done, b.count + 1)
                pool.tensor_tensor(f.x1[b.z][:], f.x1[b.z][:], f.norms[:, 0:1].broadcast_to([P, MT, DIM]),
                                   ALU.mult).then_inc(f.x1_scaled, 1)
                pool.wait_ge(f.x1_scaled, b.n + 1)
                pool.tensor_tensor(f.x1[b.z][:], f.x1[b.z][:], f.norms[:, 1:2].broadcast_to([P, MT, DIM]),
                                   ALU.add).then_inc(f.x1_done, 1)

            def norm_2(b):
                pool.wait_ge(f.ln2_stats, b.n + 1)
                pool.tensor_tensor(f.rstd2[:], f.var2[:], neghalf[:, 0:MT], ALU.pow).then_inc(f.ln2_rstd, 1)

            def affine_2(b):
                pool.wait_ge(f.ln2_done, b.n + 1)
                pool.tensor_tensor(f.y[:], f.y[:], f.out_g[:].unsqueeze(1).broadcast_to([P, MT, DIM]),
                                   ALU.mult).then_inc(f.out_scaled, 1)
                pool.wait_ge(f.out_scaled, b.n + 1)
                pool.tensor_tensor(f.y[:], f.y[:], f.out_b[:].unsqueeze(1).broadcast_to([P, MT, DIM]),
                                   ALU.add).then_inc(f.out_ready, 1)

            norm_1(Block(0, 0, 0, f.base))
            affine_1(Block(0, 0, 0, f.base))

            def body(b, behind, ahead):
                for m in range(HC):
                    at = HC * b.n + m
                    if m == 1 and behind:
                        norm_2(b.last())
                    if m == 1 and ahead:
                        norm_1(b.next())
                    if m == 2 and ahead:
                        affine_1(b.next())
                    if m == 4 and behind:
                        affine_2(b.last())
                    pool.wait_ge(f.h_round, at + 1)
                    pool.tensor_tensor(f.h_lo[m % 4][:], f.h[m % 4][:], f.h_hi[m % 4][:].bitcast(F32),
                                       ALU.subtract).then_inc(f.h_split, 1)

            paired_blocks(pool, MB, body, f.base)
            final = Block(MB - 1, 1, (MB - 2) // 2, f.base)
            norm_2(final)
            affine_2(final)

        def ffn_on_vector(dve, f):
            def stats_1(b):
                for t in range(MT):
                    last = dve.bn_stats(f.stats1[:, t, :], z_sum[:, bass.ds(MT * b.n + t, 1), :])
                last.then_inc(f.bn_done, 1)

            def aggregate_1(b):
                if isinstance(b.n, int):
                    dve.wait_ge(f.bn_done, b.count + 1)
                for t in range(MT):
                    last = dve.bn_aggr(f.mv1[:, t, :], f.stats1[:, t, :])
                last.then_inc(f.agg1_done, 1)
                dve.wait_ge(f.agg1_done, b.n + 1)
                dve.tensor_scalar(f.var1[:], f.mv1[:, :, 1], EPS, None, ALU.add).then_inc(f.ln_stats, 1)

            def apply_1(b):
                dve.wait_ge(f.ln_rstd, b.count + 1)
                after(dve, f.y_sum, b.n - 1)
                for t in range(MT):
                    last = dve.tensor_scalar(f.x1[b.z][:, t, :], z_sum[:, bass.ds(MT * b.n + t, 1), :].rearrange("p o c -> p (o c)"),
                                             f.mv1[:, t, 0:1], f.rstd1[:, t:t + 1], ALU.subtract, ALU.mult)
                last.then_inc(f.ln_done, 1)

            def x_residue(b):
                dve.wait_ge(f.x_round, b.count + 1)
                dve.tensor_tensor(f.x_lo[b.z][:], f.xt_bank, f.x_hi[b.z][:].bitcast(F32),
                                  ALU.subtract).then_inc(f.x_split, 1)

            def sums(b):
                dve.wait_ge(f.y_ps, b.n + 1)
                if isinstance(b.n, int):
                    after(dve, f.x_done, b.n)
                else:
                    dve.wait_ge(f.x_split, b.count + 2)
                dve.tensor_tensor(f.y[:].rearrange("p t c -> p (t c)"), f.y_ps_bank.rearrange("p b n -> p (b n)"),
                                  f.x1[b.z][:].rearrange("p t c -> p (t c)"), ALU.add).then_inc(f.y_sum, 1)
                dve.wait_ge(f.y_sum, b.n + 1)
                for t in range(MT):
                    last = dve.bn_stats(f.stats2[:, t, :], f.y[:, t])
                last.then_inc(f.bn2_done, 1)

            def aggregate_2(b, covered):
                if not covered:
                    dve.wait_ge(f.bn2_done, b.n + 1)
                for t in range(MT):
                    last = dve.bn_aggr(f.mv2[:, t, :], f.stats2[:, t, :])
                last.then_inc(f.agg2_done, 1)
                dve.wait_ge(f.agg2_done, b.n + 1)
                dve.tensor_scalar(f.var2[:], f.mv2[:, :, 1], EPS, None, ALU.add).then_inc(f.ln2_stats, 1)

            def apply_2(b):
                dve.wait_ge(f.ln2_rstd, b.n + 1)
                for t in range(MT):
                    last = dve.tensor_scalar(f.y[:, t], f.y[:, t], f.mv2[:, t, 0:1], f.rstd2[:, t:t + 1],
                                             ALU.subtract, ALU.mult)
                last.then_inc(f.ln2_done, 1)

            def residual(b):
                dve.wait_ge(f.out_ready, b.n + 1)
                xb = x[:, bass.ds(MT * b.n, MT), :]
                dve.tensor_tensor(xb, xb, f.y[:], ALU.add).then_inc(f.x_done, 1)

            dve.wait_ge(f.bias_round, 1)
            dve.tensor_tensor(f.bias_lo[:], f.bias_raw[:], f.bias_hi[:].bitcast(F32), ALU.subtract).then_inc(f.bias_split, 1)
            dve.wait_ge(a1.y_done, 2 * BATCH)
            first = Block(0, 0, 0, f.base)
            stats_1(first)
            aggregate_1(first)
            apply_1(first)
            x_residue(first)

            def body(b, behind, ahead):
                if behind:
                    sums(b.last())
                if ahead:
                    if behind:
                        dve.wait_ge(f.bn2_done, b.n)
                    stats_1(b.next())
                if behind:
                    aggregate_2(b.last(), ahead)
                if ahead:
                    aggregate_1(b.next())
                    apply_1(b.next())
                if behind:
                    apply_2(b.last())
                    residual(b.last())
                if not behind:
                    ternary_weights_on_vector(dve, w)
                if ahead:
                    x_residue(b.next())
                else:
                    ternary_rows_on_vector(dve, w)

            paired_blocks(dve, MB, body, f.base)
            final = Block(MB - 1, 1, (MB - 2) // 2, f.base)
            sums(final)
            aggregate_2(final, False)
            apply_2(final)
            residual(final)

        def ffn_on_tensor(pe, f):
            w1 = [both[:, 0:KC * HID].rearrange("p (k n) -> p k n", k=KC) for both in (ffn_hi, ffn_lo)]
            w2 = [both[:, KC * HID:].rearrange("p (k n) -> p k n", k=HC) for both in (ffn_hi, ffn_lo)]

            def transpose_x(b):
                pe.wait_ge(f.x1_done, b.n + 1)
                after(pe, f.x_split, b.count)
                for k in range(KC):
                    for t in range(MT):
                        last = pe.transpose(f.xt_bank[:, k, t * P:(t + 1) * P], f.x1[b.z][:, t, k * P:(k + 1) * P], ident[:])
                last.then_inc(f.xt_ps, 1)

            def up(b, m):
                part = slice(m * P, (m + 1) * P)
                pe.wait_ge(f.x_split, b.count + 1)
                after(pe, f.gelu_done, HC * b.n + m - 3)
                product(pe, f.up_ps[:, m % 4], [(w1[0][:, k, part], w1[1][:, k, part], f.x_hi[b.z][:, k], f.x_lo[b.z][:, k])
                                                for k in range(KC)]).then_inc(f.up_done, 1)

            def down(b, m):
                if m == 0:
                    after(pe, f.y_sum, b.n)
                    for half in range(2):
                        for n, part in enumerate((f.bias_hi, f.bias_lo)):
                            pe.matmul(f.y_ps_bank[:, half].rearrange("p (t c) -> p t c", c=DIM), ones_r[0:1, :],
                                      part[:].unsqueeze(1).broadcast_to([1, 2, DIM]), start=n == 0, stop=False,
                                      skip_group_check=True)
                pe.wait_ge(f.h_split, HC * b.n + m + 1)
                for t in range(MT):
                    part = slice(t * P, (t + 1) * P)
                    last = product(pe, f.y_ps_bank[:, t // 2, t % 2 * DIM:(t % 2 + 1) * DIM],
                                   [(f.h_hi[m % 4][:, part], f.h_lo[m % 4][:, part], w2[0][:, m], w2[1][:, m])],
                                   start=False, stop=m == HC - 1)
                if m == HC - 1:
                    last.then_inc(f.y_ps, 1)

            pe.wait_ge(side_split, 2 * BATCH)
            pe.wait_ge(f.bias_split, 1)
            transpose_x(Block(0, 0, 0, f.base))

            def body(b, behind, ahead):
                up(b, 0)
                up(b, 1)
                for m in range(2, HC):
                    up(b, m)
                    down(b, m - 2)
                if not behind:
                    ternary_weights_on_tensor(pe, w)
                    pe.wait_ge(w.size_done, 1)
                if ahead:
                    transpose_x(b.next())
                down(b, HC - 2)
                down(b, HC - 1)

            paired_blocks(pe, MB, body, f.base)

        class Ternary(ParameterSignals):

            def __init__(self, scope):
                self.raw = sb(scope, "t_raw", [P, 2, TER_COLS])
                self.code = sb(scope, "t_code", [P, 2, TER_COLS], F32R)
                self.rows_hi = sb(scope, "t_rows_hi", [P, 2, HC, P], F32R)
                self.rows_lo = sb(scope, "t_rows_lo", [P, 2, HC, P], F32R)
                self.sums = sb(scope, "t_sums", [P, 2])
                self.size = sb(scope, "t_size", [P, 2])
                self.scale = sb(scope, "t_scale", [P, 2])
                self.gate = sb(scope, "t_gate", [P, 1])
                self.neg_gate = sb(scope, "t_neg_gate", [P, 1])
                self.base = BATCH + MB
                self.raw_in = sem("r_raw_in")
                self.sums_done = sem("r_sums_done")
                self.total_ps = sem("r_total_ps")
                self.size_done = sem("r_size_done")
                self.code_done = sem("r_code_done")
                self.scale_done = sem("r_scale_done")
                self.bias_scaled = sem("r_bias_scaled")
                self.rows_round = sem("r_rows_round")
                self.rows_split = sem("r_rows_split")
                self.rows_ps = sem("r_rows_ps")
                self.rows_done = sem("r_rows_done")
                self.agg1_done = sem("r_agg1_done")
                self.xk_ps = sem("r_xk_ps")
                self.x_affine = sem("r_x_affine")
                self.up_done = sem("r_up_done")
                self.gelu_done = sem("r_gelu_done")
                self.gh_done = sem("r_gh_done")
                self.bn2_done = sem("r_bn2_done")
                self.agg2_done = sem("r_agg2_done")
                self.norm_step = sem("r_norm_step")
                self.rg_done = sem("r_rg_done")
                self.ht_ps = sem("r_ht_ps")
                self.h_round = sem("r_h_round")
                self.h_split = sem("r_h_split")
                self.y_ps = sem("r_y_ps")
                self.centred = sem("r_centred")
                self.x_shift = sem("r_x_shift")
                self.x_done = sem("r_x_done")

            def work_buffers(self, work):
                two, four = range(2), range(4)
                self.b1 = sb(work, "t_b1", [1, HID])
                self.b1_hi = sb(work, "t_b1_hi", [1, HID], F32R)
                self.b1_lo = sb(work, "t_b1_lo", [1, HID], F32R)
                self.b2 = sb(work, "t_b2", [P, DIM])
                self.g2 = sb(work, "t_g2", [P, HID])
                self.mean_row = sb(work, "t_mean_row", [P, DIM])
                self.shift_row = sb(work, "t_shift_row", [P, DIM])
                self.stats1 = sb(work, "t_stats1", [P, MT, 6])
                self.mv1 = sb(work, "t_mv1", [P, MT, 2])
                self.var1 = sb(work, "t_var1", [P, MT])
                self.rstd1 = sb(work, "t_rstd1", [P, MT])
                self.xn = sb(work, "t_xn", [P, MT, DIM])
                self.xa = sb(work, "t_xa", [P, KC, MN])
                self.x_hi = [sb(work, f"t_x_hi{z}", [P, KC, MN], F32R) for z in two]
                self.x_lo = [sb(work, f"t_x_lo{z}", [P, KC, MN], F32R) for z in two]
                self.h = [sb(work, f"t_h{z}", [P, HID]) for z in two]
                self.gh = [sb(work, f"t_gh{z}", [P, HID]) for z in two]
                self.stats2 = [sb(work, f"t_stats2{z}", [P, 2, 6]) for z in four]
                self.mv2 = [sb(work, f"t_mv2{z}", [P, 2]) for z in four]
                self.var2 = [sb(work, f"t_var2{z}", [P, 1]) for z in four]
                self.rstd2 = [sb(work, f"t_rstd2{z}", [P, 1]) for z in four]
                self.rg = [sb(work, f"t_rg{z}", [P, 1]) for z in four]
                self.h_hi = [sb(work, f"t_h_hi{z}", [P, HC, P], F32R) for z in two]
                self.h_lo = [sb(work, f"t_h_lo{z}", [P, HC, P], F32R) for z in two]
                self.y = sb(work, "t_y", [P, DIM])
                self.up_ps = PSUM[:, 0:4, :].rearrange("p (z b) n -> p z b n", z=2)
                self.ht_bank = PSUM[:, 4:6, :]
                self.y_bank = PSUM[:, 6, 0:DIM]
                self.xt_bank = PSUM[:, 7, :]
                self.rows_ps_bank = PSUM[:, 6:8, 0:DIM]
                self.total = PSUM[:, 7, 0:2]

        def ternary_weights_on_tensor(pe, w):
            pe.wait_ge(w.sums_done, 1)
            pe.matmul(w.total, ones[:], w.sums[:], start=True, stop=True).then_inc(w.total_ps, 1)

        def ternary_weights_on_vector(dve, w):
            count = [0]

            def step(instruction):
                count[0] += 1
                instruction.then_inc(w.code_done, 1)
                dve.wait_ge(w.code_done, count[0])

            dve.wait_ge(w.raw_in, 32)
            for n in range(2):
                last = dve.tensor_reduce(w.sums[:, n:n + 1], w.raw[:, n], AX.X, ALU.add, apply_absolute_value=True)
            last.then_inc(w.sums_done, 1)
            dve.wait_ge(w.total_ps, 1)
            dve.tensor_scalar(w.size[:], w.total, 1.0 / (HID * DIM), 1e-5, ALU.mult, ALU.max).then_inc(w.size_done, 1)
            dve.wait_ge(w.size_done, 1)
            step(dve.reciprocal(w.scale[:], w.size[:]))
            for n in range(2):
                step(dve.tensor_scalar(w.raw[:, n], w.raw[:, n], w.scale[:, n:n + 1], -1.0, ALU.mult, ALU.max))
                step(dve.tensor_scalar(w.raw[:, n], w.raw[:, n], 1.0, ROUND, ALU.min, ALU.add))
                step(dve.tensor_scalar(w.code[:, n], w.raw[:, n], ROUND, None, ALU.subtract))
            step(dve.reciprocal(w.size[:], w.scale[:]))
            step(dve.tensor_scalar(w.gate[:], w.size[:, 1:2], gates[:, 3:4], None, ALU.mult))
            dve.tensor_scalar(w.neg_gate[:], w.gate[:], -1.0, None, ALU.mult).then_inc(w.scale_done, 1)

        def ternary_rows_on_scalar(act, w):
            for n, col in enumerate((COL_G2, COL_T2)):
                last = act.activation(w.rows_hi[:, n], cols[:, col:col + HC].unsqueeze(2).broadcast_to([P, HC, P]), ACT.Copy)
            last.then_inc(w.rows_round, 1)

        def ternary_rows_on_vector(dve, w):
            dve.wait_ge(w.rows_round, 1)
            for n, col in enumerate((COL_G2, COL_T2)):
                last = dve.tensor_tensor(w.rows_lo[:, n], cols[:, col:col + HC].unsqueeze(2).broadcast_to([P, HC, P]),
                                         w.rows_hi[:, n].bitcast(F32), ALU.subtract)
            last.then_inc(w.rows_split, 1)

        def ternary_on_scalar(act, w):
            act.wait_ge(f.x_done, MB)
            for dst, src in ((w.b1[:], d["ter_b1"]), (w.b2[:], d["ter_b2"].partition_broadcast(P)),
                             (w.g2[:], d["ter_g2"].partition_broadcast(P))):
                act.dma_start(dst, src).then_inc(w.small_in, 16)
            act.wait_ge(w.bias_scaled, 1)
            act.activation(w.b1_hi[:], w.b1[:], ACT.Copy).then_inc(w.bias_round, 1)

            def x_affine(b, k):
                act.wait_ge(w.xk_ps, KC * b.n + k + 1)
                if k == 0:
                    after(act, w.x_split, b.count)
                act.activation(w.xa[:, k], w.xt_bank, ACT.Identity, scale=cols[:, COL_G1 + k:COL_G1 + k + 1],
                               bias=cols[:, COL_T1 + k:COL_T1 + k + 1]).then_inc(w.x_affine, 1)

            def x_rounded(b):
                act.wait_ge(w.x_affine, KC * (b.n + 1))
                act.activation(w.x_hi[b.z][:], w.xa[:], ACT.Copy).then_inc(w.x_round, 1)

            def gelu(b, t):
                at = MT * b.n + t
                act.wait_ge(w.up_done, at + 1)
                after(act, w.gh_done, at - 1)
                after(act, w.bn2_done, at - 1)
                act.activation(w.h[t % 2][:], w.up_ps[:, t % 2].rearrange("p b n -> p (b n)"), ACT.Gelu,
                               scale=w.size[:, 0:1]).then_inc(w.gelu_done, 1)

            def rounded(b, t):
                at = MT * b.n + t
                act.wait_ge(w.ht_ps, at + 1)
                after(act, w.y_ps, at - 1)
                act.activation(w.h_hi[t % 2][:], w.ht_bank.rearrange("p b (k n) -> p (b k) n", n=P),
                               ACT.Copy).then_inc(w.h_round, 1)

            first = Block(0, 0, 0, w.base)
            for k in range(KC):
                x_affine(first, k)
            x_rounded(first)

            def body(b, behind, ahead):
                for t in range(MT):
                    if t == 3 and ahead:
                        x_affine(b.next(), 1)
                        x_rounded(b.next())
                    gelu(b, t)
                    if t >= 1:
                        rounded(b, t - 1)
                    elif behind:
                        rounded(b.last(), MT - 1)
                    if t == 2 and ahead:
                        x_affine(b.next(), 0)

            paired_blocks(act, MB, body, w.base)
            rounded(Block(MB - 1, 1, (MB - 2) // 2, w.base), MT - 1)

        def ternary_on_gpsimd(pool, w):
            pool.wait_ge(f.x_done, MB)

            def inverse_std(b):
                pool.wait_ge(w.ln_stats, b.count + 1)
                pool.tensor_tensor(w.rstd1[:], w.var1[:], neghalf[:, 0:MT], ALU.pow).then_inc(w.ln_rstd, 1)

            def scale_h(b, t):
                at = MT * b.n + t
                pool.wait_ge(w.gelu_done, at + 1)
                after(pool, w.ht_ps, at - 1)
                pool.tensor_tensor(w.gh[t % 2][:], w.h[t % 2][:], w.g2[:], ALU.mult).then_inc(w.gh_done, 1)

            def norm_2(b, t):
                at = MT * b.n + t
                pool.wait_ge(w.agg2_done, at + 1)
                pool.tensor_tensor(w.var2[t][:], w.mv2[t][:, 1:2], eps_tile[:, 0:1], ALU.add).then_inc(w.norm_step, 1)
                pool.wait_ge(w.norm_step, 2 * at + 1)
                pool.tensor_tensor(w.rstd2[t][:], w.var2[t][:], neghalf[:, 0:1], ALU.pow).then_inc(w.norm_step, 1)
                pool.wait_ge(w.norm_step, 2 * at + 2)
                pool.tensor_tensor(w.rg[t][:], w.rstd2[t][:], w.neg_gate[:], ALU.mult).then_inc(w.rg_done, 1)

            def shift(b):
                pool.wait_ge(w.ln_done, b.count + 1)
                xb = x[:, bass.ds(MT * b.n, MT), :]
                pool.tensor_tensor(xb, xb, w.shift_row[:].unsqueeze(1).broadcast_to([P, MT, DIM]),
                                   ALU.add).then_inc(w.x_shift, 1)

            inverse_std(Block(0, 0, 0, w.base))
            pool.wait_ge(w.small_in, 80)
            pool.wait_ge(w.rows_done, 2)

            def body(b, behind, ahead):
                for t in range(MT):
                    scale_h(b, t)
                    if t == 1 and ahead:
                        inverse_std(b.next())
                    norm_2(b, t)
                    if t == 0:
                        shift(b)

            paired_blocks(pool, MB, body, w.base)

        def ternary_on_vector(dve, w):
            def stats_1(b):
                for t in range(MT):
                    last = dve.bn_stats(w.stats1[:, t, :], x[:, bass.ds(MT * b.n + t, 1), :])
                last.then_inc(w.bn_done, 1)

            def aggregate_1(b):
                if isinstance(b.n, int):
                    dve.wait_ge(w.bn_done, b.count + 1)
                for t in range(MT):
                    last = dve.bn_aggr(w.mv1[:, t, :], w.stats1[:, t, :])
                last.then_inc(w.agg1_done, 1)
                dve.wait_ge(w.agg1_done, b.n + 1)
                dve.tensor_scalar(w.var1[:], w.mv1[:, :, 1], 1.0 + EPS, EPS * EPS, ALU.mult, ALU.add).then_inc(w.ln_stats, 1)

            def apply_1(b):
                dve.wait_ge(w.ln_rstd, b.count + 1)
                after(dve, w.xk_ps, KC * b.n)
                for t in range(MT):
                    last = dve.tensor_scalar(w.xn[:, t, :], x[:, bass.ds(MT * b.n + t, 1), :].rearrange("p o c -> p (o c)"),
                                             w.mv1[:, t, 0:1], w.rstd1[:, t:t + 1], ALU.subtract, ALU.mult)
                last.then_inc(w.ln_done, 1)

            def x_residue(b):
                dve.wait_ge(w.x_round, b.count + 1)
                dve.tensor_tensor(w.x_lo[b.z][:], w.xa[:], w.x_hi[b.z][:].bitcast(F32), ALU.subtract).then_inc(w.x_split, 1)

            def stats_2(b, t):
                at = MT * b.n + t
                dve.wait_ge(w.gelu_done, at + 1)
                for c in range(2):
                    last = dve.bn_stats(w.stats2[t][:, c], w.h[t % 2][:, c * 512:(c + 1) * 512])
                last.then_inc(w.bn2_done, 1)

            def aggregate_2(b, t):
                if isinstance(b.n, int):
                    dve.wait_ge(w.bn2_done, MT * b.n + t + 1)
                dve.bn_aggr(w.mv2[t][:], w.stats2[t][:].rearrange("p c s -> p (c s)")).then_inc(w.agg2_done, 1)

            def residue(b, t):
                dve.wait_ge(w.h_round, MT * b.n + t + 1)
                dve.tensor_tensor(w.h_lo[t % 2][:], w.ht_bank.rearrange("p b (k n) -> p (b k) n", n=P),
                                  w.h_hi[t % 2][:].bitcast(F32), ALU.subtract).then_inc(w.h_split, 1)

            def residual(b, t):
                at = MT * b.n + t
                dve.wait_ge(w.y_ps, at + 1)
                dve.wait_ge(w.rg_done, at + 1)
                after(dve, w.x_done, at)
                dve.scalar_tensor_tensor(w.y[:], w.mean_row[:], w.mv2[t][:, 0:1], w.y_bank, ALU.mult,
                                         ALU.subtract).then_inc(w.centred, 1)
                dve.wait_ge(w.centred, at + 1)
                if t == 0:
                    dve.wait_ge(w.x_shift, b.n + 1)
                xt = x[:, bass.ds(at, 1), :].rearrange("p o c -> p (o c)")
                dve.scalar_tensor_tensor(xt, w.y[:], w.rg[t][:], xt, ALU.mult, ALU.add).then_inc(w.x_done, 1)

            dve.wait_ge(f.x_done, MB)
            first = Block(0, 0, 0, w.base)
            stats_1(first)
            aggregate_1(first)
            dve.wait_ge(w.small_in, 80)
            dve.wait_ge(w.scale_done, 1)
            dve.tensor_scalar(w.b1[:], w.b1[:], w.scale[0:1, 0:1], None, ALU.mult).then_inc(w.bias_scaled, 1)
            dve.wait_ge(w.rows_ps, 1)
            dve.tensor_copy(w.mean_row[:], w.rows_ps_bank[:, 0])
            dve.tensor_scalar(w.shift_row[:], w.b2[:], gates[:, 3:4], None, ALU.mult).then_inc(w.rows_done, 1)
            apply_1(first)
            dve.wait_ge(w.rows_done, 1)
            dve.scalar_tensor_tensor(w.shift_row[:], w.rows_ps_bank[:, 1], w.gate[:], w.shift_row[:], ALU.mult,
                                     ALU.add).then_inc(w.rows_done, 1)
            dve.wait_ge(w.bias_round, 2)
            dve.tensor_tensor(w.b1_lo[:], w.b1[:], w.b1_hi[:].bitcast(F32), ALU.subtract).then_inc(w.bias_split, 1)
            x_residue(first)

            def body(b, behind, ahead):
                for t in range(MT):
                    if t == 2 and ahead:
                        apply_1(b.next())
                    if t == 3 and ahead:
                        x_residue(b.next())
                    stats_2(b, t)
                    if t == 0 and ahead:
                        stats_1(b.next())
                    if t >= 1:
                        residue(b, t - 1)
                    elif behind:
                        residue(b.last(), MT - 1)
                    if t >= 2:
                        residual(b, t - 2)
                    elif behind:
                        residual(b.last(), t - 2 + MT)
                    aggregate_2(b, t)
                    if t == 0 and ahead:
                        aggregate_1(b.next())

            paired_blocks(dve, MB, body, w.base)
            final = Block(MB - 1, 1, (MB - 2) // 2, w.base)
            residue(final, MT - 1)
            residual(final, MT - 2)
            residual(final, MT - 1)

        def ternary_on_tensor(pe, w):
            w1 = w.code[:, 0].rearrange("p (k n) -> p k n", k=KC)
            w2 = w.code[:, 1].rearrange("p (k n) -> p k n", k=HC)

            def transpose_x(b, k):
                if k == 0:
                    pe.wait_ge(w.ln_done, b.count + 1)
                after(pe, w.x_affine, KC * b.n + k)
                for t in range(MT):
                    last = pe.transpose(w.xt_bank[:, t * P:(t + 1) * P], w.xn[:, t, k * P:(k + 1) * P], ident[:])
                last.then_inc(w.xk_ps, 1)

            def up(b, t):
                part = slice(t * P, (t + 1) * P)
                pe.wait_ge(w.x_split, b.count + 1)
                after(pe, w.gelu_done, MT * b.n + t - 1)
                for c in range(2):
                    n = slice(c * 512, (c + 1) * 512)
                    ps = w.up_ps[:, t % 2, c]
                    pe.matmul(ps, ones_r[0:1, :], w.b1_hi[:, n], start=True, stop=False)
                    pe.matmul(ps, ones_r[0:1, :], w.b1_lo[:, n], start=False, stop=False)
                    for k in range(KC):
                        pe.matmul(ps, w.x_hi[b.z][:, k, part], w1[:, k, n], start=False, stop=False)
                        last = pe.matmul(ps, w.x_lo[b.z][:, k, part], w1[:, k, n], start=False, stop=k == KC - 1)
                last.then_inc(w.up_done, 1)

            def transpose_h(b, t):
                at = MT * b.n + t
                pe.wait_ge(w.gh_done, at + 1)
                after(pe, w.h_split, at)
                for k in range(HC):
                    last = pe.transpose(w.ht_bank[:, k // 4, k % 4 * P:(k % 4 + 1) * P], w.gh[t % 2][:, k * P:(k + 1) * P], ident[:])
                last.then_inc(w.ht_ps, 1)

            def down(b, t):
                at = MT * b.n + t
                pe.wait_ge(w.h_split, at + 1)
                after(pe, w.x_done, at)
                for k in range(HC):
                    pe.matmul(w.y_bank, w.h_hi[t % 2][:, k], w2[:, k], start=k == 0, stop=False)
                    last = pe.matmul(w.y_bank, w.h_lo[t % 2][:, k], w2[:, k], start=False, stop=k == HC - 1)
                last.then_inc(w.y_ps, 1)

            pe.wait_ge(w.rows_split, 1)
            pe.wait_ge(w.scale_done, 1)
            for n in range(2):
                for k in range(HC):
                    pe.matmul(w.rows_ps_bank[:, n], w.rows_hi[:, n, k], w2[:, k], start=k == 0, stop=False)
                    last = pe.matmul(w.rows_ps_bank[:, n], w.rows_lo[:, n, k], w2[:, k], start=False, stop=k == HC - 1)
            last.then_inc(w.rows_ps, 1)
            pe.wait_ge(w.rows_done, 2)
            for k in range(KC):
                transpose_x(Block(0, 0, 0, w.base), k)
            pe.wait_ge(w.bias_split, 2)

            def body(b, behind, ahead):
                for t in range(MT):
                    if t == 3 and ahead:
                        transpose_x(b.next(), 1)
                    up(b, t)
                    if t >= 1:
                        transpose_h(b, t - 1)
                    elif behind:
                        transpose_h(b.last(), MT - 1)
                    if t == 2 and ahead:
                        transpose_x(b.next(), 0)
                    if t >= 2:
                        down(b, t - 2)
                    elif behind:
                        down(b.last(), t - 2 + MT)

            paired_blocks(pe, MB, body, w.base)
            final = Block(MB - 1, 1, (MB - 2) // 2, w.base)
            transpose_h(final, MT - 1)
            down(final, MT - 2)
            down(final, MT - 1)

        weight_scope = root.enter_context(ExitStack())
        moe_w = sb(weight_scope, "moe_w", [P, (EXPERTS + 1) * EXPERT_COLS], F32R)
        weight_scope.close()
        early_scope = root.enter_context(ExitStack())
        sb(early_scope, "moe_early_place", [P, EARLY_CHUNKS * 2 * MOE_CHUNK], F32R)
        zeros = sb(early_scope, "zeros", [P, DIM])
        moe_raw = [sb(early_scope, f"moe_raw{z}", [P, MOE_CHUNK]) for z in range(2)]
        a0 = Attention(0, early_scope)
        early_scope.close()
        mix_scope = root.enter_context(ExitStack())
        mix = Mixture(mix_scope)
        mix_scope.close()

        layer1_scope = root.enter_context(ExitStack())
        z_sum = sb(layer1_scope, "z_sum", [P, TILES, DIM])
        ffn_hi = sb(layer1_scope, "ffn_hi", [P, FFN_COLS], F32R)
        ffn_lo = sb(layer1_scope, "ffn_lo", [P, FFN_COLS], F32R)
        att1_scope = layer1_scope.enter_context(ExitStack())
        ffn_raw = [sb(att1_scope, f"ffn_raw{z}", [P, FFN_CHUNK]) for z in range(2)]
        a1 = Attention(1, att1_scope, z_sum)
        att1_scope.close()
        f = FeedForward(layer1_scope)
        w = Ternary(layer1_scope)
        layer1_scope.close()
        w.work_buffers(root)

        side_in = [sem(f"side_in{z}") for z in range(2)]
        side_round = sem("side_round")
        side_split = sem("side_split")
        zeros_out = sem("zeros_out")
        out_done = sem("out_done")
        WA_ORDER = (1, 2, 0, 3)

        block = root.enter_context(nc.Block())

        @block.sync
        def _(sp):
            def load(a, b):
                if a.stage == 0:
                    after(sp, a.x_in[b.z], 16 * b.half)
                    sp.dma_start(tiles(b), x_dram[:, bass.ds(BT * b.n, BT), :]).then_inc(a.x_in[b.z], 16)
                after(sp, a.ctx_split, b.count - 1)
                sp.dma_start(a.ctx[b.z][:], ctx_dram[bass.ds(b.n, 1)].rearrange("o p k n -> p (o k) n")).then_inc(a.ctx_in[b.z], 16)

            def spread(a, b):
                sp.wait_ge(a.x_split, b.count + 1)
                values = a.v[b.z][:].rearrange("k (m h) n -> k m h n", m=KC)
                for h, key, keys, c, row in value_pieces():
                    at = column_of(c) + (h - heads_of(c)[0]) * VW
                    sp.dma_start(a.v_diagonal[b.z][row:row + keys, :, at:at + VW],
                                 values[key:key + keys, :, h]).then_inc(a.v_spread[b.z], 16)

            def load_moe(b):
                after(sp, side_split, b.count - 1)
                sp.dma_start(moe_raw[b.z][:], d["moe_w"][:, bass.ds(b.n * MOE_CHUNK, MOE_CHUNK)]).then_inc(side_in[b.z], 16)

            for n in range(2):
                load(a0, Block(n, n, 0))
            sp.wait_ge(pool_const, 6)

            def clear(b, count=ZERO_TILES):
                sp.dma_start(d["sorted_x"].rearrange("(t p) c -> p t c", p=P)[:, bass.ds(ZERO_TILES * b.n, count), :],
                             zeros[:].unsqueeze(1).broadcast_to([P, count, DIM])).then_inc(zeros_out, 16)

            load_moe(Block(0, 0, 0))
            sp.wait_ge(a0.v_ones, 2)
            spread(a0, Block(0, 0, 0))

            def body(b, behind, ahead):
                if ahead > 1:
                    load(a0, b.next().next())
                if ahead:
                    load_moe(b.next())
                    spread(a0, b.next())
                clear(b)

            paired_blocks(sp, BATCH, body, 0, 3)
            clear(Block(BATCH, 0, BATCH // 2), SORTED - ZERO_TILES * BATCH)
            if stages > 1:
                mixture_on_sync(sp, mix)
            if stages > 2:
                sp.wait_ge(mix.y_done, SHARED + SORTED)
                def load_ffn(b):
                    after(sp, side_split, b.count - 1)
                    sp.dma_start(ffn_raw[b.z][:], d["ffn_w"][:, bass.ds(b.n * FFN_CHUNK, FFN_CHUNK)]).then_inc(side_in[b.z], 16)

                for n in range(2):
                    load(a1, Block(n, n, 0, a1.base))
                load_ffn(Block(0, 0, 0, a1.base))
                sp.wait_ge(a1.v_ones, 4)
                spread(a1, Block(0, 0, 0, a1.base))

                def body(b, behind, ahead):
                    if ahead > 1:
                        load(a1, b.next().next())
                    if ahead:
                        load_ffn(b.next())
                        spread(a1, b.next())

                paired_blocks(sp, BATCH, body, a1.base, 3)
            if stages > 3:
                sp.wait_ge(a1.y_done, 2 * BATCH)
                sp.wait_ge(side_split, 2 * BATCH)
                for n, name in enumerate(("ter_w1", "ter_w2")):
                    sp.dma_start(w.raw[:, n], d[name]).then_inc(w.raw_in, 16)
            for b in range(BATCH):
                if stages == 1:
                    sp.wait_ge(a0.y_done, b + 1)
                elif stages == 2:
                    sp.wait_ge(mix.y_done, SHARED + SORTED)
                elif stages == 3:
                    sp.wait_ge(a1.y_done, BATCH + b + 1)
                    sp.dma_start(out_dram[:, BT * b:BT * (b + 1), :], z_sum[:, BT * b:BT * (b + 1), :]).then_inc(out_done, 16)
                    continue
                elif stages == 5:
                    sp.wait_ge(f.x_done, b // 2 + 1)
                else:
                    sp.wait_ge(w.x_done, BT * (b + 1))
                sp.dma_start(out_dram[:, BT * b:BT * (b + 1), :], x[:, BT * b:BT * (b + 1), :]).then_inc(out_done, 16)
            sp.wait_ge(out_done, 16 * BATCH)

        @block.gpsimd
        def _(pool):
            pool.memset(ident[:], 0.0).then_inc(pool_const, 1)
            pool.memset(headmask[:], 1.0).then_inc(pool_const, 1)
            pool.memset(ones[:], 1.0).then_inc(pool_const, 1)
            pool.memset(neghalf[:], -0.5)
            pool.memset(eps_tile[:], EPS).then_inc(pool_const, 1)
            pool.memset(a0.mask_raw[:], 0.0).then_inc(pool_const, 1)
            pool.memset(zeros[:], 0.0).then_inc(pool_const, 1)
            pool.wait_ge(pool_const, 6)
            pool.affine_select(out=ident[:], in_=ident[:], compare_op=ALU.not_equal, fill=1.0, base=0,
                               pattern=[[-1, P]], channel_multiplier=1).then_inc(pool_const, 1)
            pool.affine_select(out=headmask[:], in_=headmask[:], compare_op=ALU.is_ge, fill=0.0, base=0,
                               pattern=[[-HD, HPC]], channel_multiplier=1).then_inc(pool_const, 1)
            pool.wait_ge(pool_const, 8)
            pool.affine_select(out=headmask[:], in_=headmask[:], compare_op=ALU.is_ge, fill=0.0, base=HD - 1,
                               pattern=[[HD, HPC]], channel_multiplier=-1).then_inc(pool_const, 1)
            pool.wait_ge(pool_const, 9)

            def split_moe(b):
                hi, lo = (moe_w[:, bass.ds((2 * b.n + part) * MOE_CHUNK, MOE_CHUNK)] for part in range(2))
                pool.wait_ge(side_in[b.z], 16 * (b.half + 1))
                pool.tensor_tensor(hi, moe_raw[b.z][:], one([P, MOE_CHUNK]), ALU.mult).then_inc(side_round, 1)
                pool.wait_ge(side_round, b.n + 1)
                pool.tensor_tensor(lo, moe_raw[b.z][:], hi.bitcast(F32), ALU.subtract).then_inc(side_split, 1)

            attention_on_gpsimd(pool, a0, None, split_moe)
            if stages > 1:
                mixture_on_gpsimd(pool, mix)

            def split_ffn(b):
                part = bass.ds(b.n * FFN_CHUNK, FFN_CHUNK)
                pool.wait_ge(side_in[b.z], 16 * (b.half + b.base // 2 + 1))
                pool.tensor_tensor(ffn_hi[:, part], ffn_raw[b.z][:], one([P, FFN_CHUNK]), ALU.mult).then_inc(side_round, 1)
                pool.wait_ge(side_round, b.count + 1)
                pool.tensor_tensor(ffn_lo[:, part], ffn_raw[b.z][:], ffn_hi[:, part].bitcast(F32),
                                   ALU.subtract).then_inc(side_split, 1)

            if stages > 2:
                pool.wait_ge(mix.y_done, SHARED + SORTED)
                for z in range(2):
                    pool.wait_ge(mix.tile_out[z], 16 * GROUPS // 2)
                pool.memset(a1.mask_raw, 1.0)
                attention_on_gpsimd(pool, a1, z_sum, split_ffn)
            if stages > 3:
                ffn_on_gpsimd(pool, f)
            if stages == 4:
                ternary_on_gpsimd(pool, w)

        @block.scalar
        def _(act):
            act.dma_start(a0.w_raw[:, 1], d["wa0"][:, 1]).then_inc(a0.w_in[1], 16)
            act.dma_start(a0.w_raw[:, 2], d["wa0"][:, 2]).then_inc(a0.w_in[2], 16)
            act.dma_start(cols[:], d["cols"]).then_inc(consts_in, 16)
            act.dma_start(a0.bv[:], d["bv"][0].partition_broadcast(CTXP)).then_inc(a0.small_in, 16)
            act.dma_start(a0.w_raw[:, 0], d["wa0"][:, 0]).then_inc(a0.w_in[0], 16)
            act.dma_start(a0.bias_raw[:], d["bias"][0:1]).then_inc(a0.small_in, 16)
            act.dma_start(gates_raw[:], d["gates"].partition_broadcast(P)).then_inc(consts_in, 16)
            act.wait_ge(pool_const, 5)
            act.dma_start(a0.mask_raw[:, :, 0:CTX], d["mask_q"].rearrange("(t p) n -> p t n", p=P)).then_inc(a0.mask_in, 16)
            act.dma_start(a0.w_raw[:, 3], d["wa0"][:, 3]).then_inc(a0.w_in[3], 16)
            for n, i in enumerate(WA_ORDER):
                act.wait_ge(a0.w_in[i], 16)
                act.activation(a0.w_hi[:, i].rearrange("p k n -> p (k n)"), a0.w_raw[:, i], ACT.Copy).then_inc(a0.w_round, 1)
                if n == 0:
                    act.wait_ge(consts_in, 32)
                    act.wait_ge(a0.small_in, 32)
                    act.activation(a0.bias_hi[:], a0.bias_raw[:], ACT.Copy).then_inc(a0.bias_round, 1)
                    act.activation(gates[:], gates_raw[:], ACT.Tanh).then_inc(gates_done, 1)
            attention_on_scalar(act, a0)
            if stages > 1:
                mixture_on_scalar(act, mix)
            if stages > 2:
                act.wait_ge(mix.y_done, SHARED + SORTED)
                for i in WA_ORDER:
                    act.dma_start(a1.w_raw[:, i], d["wa1"][:, i]).then_inc(a1.w_in[i], 16)
                act.dma_start(a1.bv[:], d["bv"][1].partition_broadcast(CTXP)).then_inc(a1.small_in, 16)
                act.dma_start(a1.bias_raw[:], d["bias"][1:2]).then_inc(a1.small_in, 16)
                act.dma_start(a1.mask_u8[:], d["mask_k"]).then_inc(a1.mask_in, 16)
                for n, i in enumerate(WA_ORDER):
                    act.wait_ge(a1.w_in[i], 32)
                    act.activation(a1.w_hi[:, i].rearrange("p k n -> p (k n)"), a1.w_raw[:, i], ACT.Copy).then_inc(a1.w_round, 1)
                    if n == 0:
                        act.wait_ge(a1.small_in, 64)
                        act.activation(a1.bias_hi[:], a1.bias_raw[:], ACT.Copy).then_inc(a1.bias_round, 1)
                attention_on_scalar(act, a1)
            if stages > 3:
                ffn_on_scalar(act, f)
            if stages == 4:
                ternary_on_scalar(act, w)

        @block.vector
        def _(dve):
            dve.wait_ge(pool_const, 9)
            dve.tensor_copy(a0.ident[:], ident[:])
            dve.tensor_copy(ones_r[:], ones[:]).then_inc(consts_done, 1)
            dve.wait_ge(a0.bias_round, 1)
            dve.tensor_tensor(a0.bias_lo[:], a0.bias_raw[:], a0.bias_hi[:].bitcast(F32), ALU.subtract).then_inc(a0.bias_split, 1)
            for n, i in enumerate(WA_ORDER):
                dve.wait_ge(a0.w_round, n + 1)
                dve.tensor_tensor(a0.w_lo[:, i].rearrange("p k n -> p (k n)"), a0.w_raw[:, i],
                                  a0.w_hi[:, i].bitcast(F32).rearrange("p k n -> p (k n)"), ALU.subtract).then_inc(a0.w_split, 1)
            dve.wait_ge(a0.mask_in, 16)
            dve.tensor_scalar(a0.mask[:], a0.mask_raw[:], 0.0, MASKED, ALU.is_equal, ALU.mult).then_inc(a0.mask_done, 1)
            attention_on_vector(dve, a0, None)
            if stages > 1:
                mixture_on_vector(dve, mix)
            if stages > 2:
                dve.wait_ge(mix.y_done, SHARED + SORTED)
                dve.wait_ge(a1.bias_round, 2)
                dve.tensor_tensor(a1.bias_lo[:], a1.bias_raw[:], a1.bias_hi[:].bitcast(F32), ALU.subtract).then_inc(a1.bias_split, 1)
                for n, i in enumerate(WA_ORDER):
                    dve.wait_ge(a1.w_round, 4 + n + 1)
                    dve.tensor_tensor(a1.w_lo[:, i].rearrange("p k n -> p (k n)"), a1.w_raw[:, i],
                                      a1.w_hi[:, i].bitcast(F32).rearrange("p k n -> p (k n)"), ALU.subtract).then_inc(a1.w_split, 1)
                dve.wait_ge(a1.mask_in, 32)
                dve.wait_ge(a1.v_ones, 4)
                dve.tensor_copy(a1.mask_raw[:, :, 0:CTX], a1.mask_u8[:]).then_inc(a1.mask_cast, 1)
                dve.wait_ge(a1.mask_cast, 1)
                dve.tensor_scalar(a1.mask[:], a1.mask_raw, MASKED, None, ALU.mult).then_inc(a1.mask_done, 1)
                attention_on_vector(dve, a1, z_sum)
            if stages > 3:
                ffn_on_vector(dve, f)
            if stages == 4:
                ternary_on_vector(dve, w)

        @block.tensor
        def _(pe):
            attention_on_tensor(pe, a0)
            if stages > 1:
                mixture_on_tensor(pe, mix)
            if stages > 2:
                attention_on_tensor(pe, a1)
            if stages > 3:
                ffn_on_tensor(pe, f)
            if stages == 4:
                ternary_on_tensor(pe, w)


_SHAPE = (BATCH, SEQ, DIM)


def kernel(**inputs):
    import concourse.bacc as bacc
    from concourse.bass_utils import run_bass_kernel_spmd

    nc = bacc.Bacc("TRN2", target_bir_lowering=False, num_devices=1)
    arrays = lay_out({k: np.asarray(v) for k, v in inputs.items()})
    d = {n: nc.dram_tensor(n, a.shape, mybir.dt.from_np(a.dtype), kind="ExternalInput").ap() for n, a in arrays.items()}
    out = nc.dram_tensor("y", _SHAPE, F32, kind="ExternalOutput").ap()
    flamingo_kernel(nc, d, out)
    r = run_bass_kernel_spmd(nc, [arrays], core_ids=[0])
    return r.results[0]["y"]
```

```python
import numpy as np
from contextlib import ExitStack

import concourse.bass as bass
from concourse import mybir
from concourse.alu_op_type import AluOpType as ALU

F32 = mybir.dt.float32
F32R = mybir.dt.float32r
U8 = mybir.dt.uint8
U32 = mybir.dt.uint32
I32 = mybir.dt.int32
ACT = mybir.ActivationFunctionType
AX = mybir.AxisListType

P = 128
BATCH, SEQ, DIM = 16, 256, 256
CTX = 77
CTXP = CTX + 1
HEADS, HD = 16, 16
EXPERTS = 8
KC = DIM // P
TILES = BATCH * SEQ // P
BT = SEQ // P
HPC = P // HD
VW = HD + 2
UNITS = KC * BT
PAIRS = HPC * CTXP
PC = -(-PAIRS // P)
MT = 4
MB = TILES // MT
MN = MT * P
HID = 1024
HC = HID // P
EPS = 1e-5
MASKED = -1e30
MATRIX = KC * DIM
MOE_CHUNK = 2 * DIM
EXPERT_COLS = 3 * 2 * MOE_CHUNK
EARLY_CHUNKS = BATCH
LATE_CHUNKS = 3 * (EXPERTS + 1) - EARLY_CHUNKS
BIAS_ROWS = 2 * (EXPERTS + 1)
CHOICES = 4
SORTED = 2 * TILES + EXPERTS
GROUP = 6
GROUPS = SORTED // GROUP
ZERO_TILES = SORTED // BATCH
FFN_COLS = 2 * KC * HID
FFN_CHUNK = FFN_COLS // BATCH
TER_COLS = KC * HID
ROUND = 1.5 * 2 ** 23

COL_BQ, COL_BK = (0, 4), (2, 6)
COL_B1 = 8
COL_B3 = COL_B1 + KC
COL_FB1 = COL_B3 + KC
COL_G1 = COL_FB1 + HC
COL_T1 = COL_G1 + KC
COL_G2 = COL_T1 + KC
COL_T2 = COL_G2 + HC
COLS = COL_T2 + HC


def heads_of(chunk):
    if chunk == 0:
        return 0, HPC
    first = chunk * P // CTXP
    return first, (min((chunk + 1) * P, PAIRS) - 1) // CTXP - first + 1


def column_of(chunk):
    return sum(heads_of(c)[1] for c in range(chunk)) * VW


def value_pieces():
    for h in range(HPC):
        pair, end = h * CTXP, (h + 1) * CTXP
        while pair < end:
            stop = min(end, (pair // P + 1) * P)
            yield h, pair - h * CTXP, stop - pair, pair // P, pair % P
            pair = stop


PIECES = len(list(value_pieces()))


def after(engine, semaphore, value):
    if not (isinstance(value, int) and value <= 0):
        engine.wait_ge(semaphore, value)


class Block:

    def __init__(self, n, parity, half, base=0):
        self.n, self.z, self.half, self.base = n, parity, half, base
        self.count = n + base

    def next(self):
        return Block(self.n + 1, 1 - self.z, self.half + self.z, self.base)

    def last(self):
        return Block(self.n - 1, 1 - self.z, self.half - (1 - self.z), self.base)


def paired_blocks(engine, count, body, base=0, reach=1):
    body(Block(0, 0, 0, base), False, reach)
    with engine.Fori(0, (count - 1 - reach) // 2) as i:
        body(Block(2 * i + 1, 1, i, base), True, reach)
        body(Block(2 * i + 2, 0, i + 1, base), True, reach)
    for n in range(count - reach, count):
        body(Block(n, n % 2, n // 2, base), True, count - 1 - n)

def lay_out(i):
    def chunks(w):
        return w.reshape(-1, P, w.shape[1]).transpose(1, 0, 2)

    def flat(w):
        return chunks(w).reshape(P, -1)

    def col(b):
        return b.reshape(-1, P).T

    ctx = np.zeros((BATCH, P, KC, CTXP), np.float32)
    ctx[..., :CTX] = i["ctx_1024"].transpose(0, 2, 1).reshape(BATCH, KC, P, CTX).transpose(0, 2, 1, 3)
    moe = []
    for w1, w3, w2 in [[i[f"L0_ffn_sw{n}"] for n in (1, 3, 2)]] + [[i[f"L0_ffn_w{n}"][e] for n in (1, 3, 2)] for e in range(EXPERTS)]:
        moe += [chunks(np.concatenate([w1, w3], 1)).reshape(P, -1), flat(w2)]
    biases = [np.concatenate([i[f"L0_ffn_b{n}"], i[f"L0_ffn_sb{n}"][None]]) for n in (1, 3, 2)]
    cols = [col(i[n]) for n in ("L0_xattn_bq", "L0_xattn_bk", "L1_xattn_bq", "L1_xattn_bk")]
    cols += [col(i["L0_ffn_sb1"]), col(i["L0_ffn_sb3"])]
    cols += [col(i[n]) for n in ("L1_xattn_b1", "L1_ffn_ln1_g", "L1_ffn_ln1_b", "L1_ffn_ln2_g", "L1_ffn_ln2_b")]
    arrays = {
        "x": i["x"],
        "ctx": ctx,
        "mask_q": i["mask_1x1xSxS2_fk0"].reshape(SEQ, CTX),
        "mask_k": i["mask_BxS2_bf0"].reshape(1, BATCH, CTX),
        "wa0": np.stack([flat(i[f"L0_xattn_W{n}"].T) for n in "qkvp"], 1),
        "wa1": np.stack([flat(i[f"L1_xattn_W{n}"]) for n in "qkvo"], 1),
        "moe_w": np.concatenate(moe, 1),
        "moe_b": np.repeat(np.concatenate(biases, 1), 2, 0),
        "tile_numbers": np.tile(np.arange(SORTED, dtype=np.float32), (BIAS_ROWS, 1)),
        "row_of": np.array([[r // 2, 1 - r % 2, r % 2, r // 2 == EXPERTS] for r in range(BIAS_ROWS)], np.float32),
        "gate_w": flat(i["L0_ffn_gate_w"].T),
        "ffn_w": np.concatenate([flat(i["L1_xattn_W1"]), flat(i["L1_xattn_W2"])], 1),
        "ter_w1": flat(i["L1_ffn_w1"].T),
        "ter_w2": flat(i["L1_ffn_w2"].T),
        "ter_g2": i["L1_ffn_ln2_g"],
        "ter_b1": i["L1_ffn_b1"][None],
        "ter_b2": i["L1_ffn_b2"],
        "cols": np.concatenate(cols, 1),
        "bv": np.stack([i["L0_xattn_bv"], i["L1_xattn_bv"]]),
        "bias": np.stack([i[n] for n in ("L0_xattn_bp", "L1_xattn_bo", "L1_xattn_b2")]),
        "norms": np.stack([i[n] for n in ("L1_xattn_ln1_g", "L1_xattn_ln1_b", "L1_xattn_ln2_g", "L1_xattn_ln2_b")]),
        "gates": np.concatenate([i["g_xattn"], i["g_ffn"]]),
    }
    return {n: np.ascontiguousarray(a) for n, a in arrays.items()}


def flamingo_kernel(nc, d, out):
    x_dram = d["x"].rearrange("b (t p) c -> p (b t) c", p=P)
    out_dram = out.rearrange("b (t p) c -> p (b t) c", p=P)
    ctx_dram = d["ctx"]
    d = {**d, **{n: nc.dram_tensor(n, (SORTED * P, DIM), F32, kind="Internal").ap() for n in ("sorted_x", "sorted_y")}}
    root = ExitStack()
    with root:
        def sb(scope, name, shape, dt=F32):
            return scope.enter_context(nc.sbuf_tensor("s_" + name, shape, dt))

        def sem(name):
            return root.enter_context(nc.semaphore(name))

        x = sb(root, "x", [P, TILES, DIM])
        ident = sb(root, "ident", [P, P])
        ones_r = sb(root, "ones_r", [P, P], F32R)
        ones = sb(root, "ones", [P, P])
        headmask = sb(root, "headmask", [P, HPC])
        neghalf = sb(root, "neghalf", [P, 8])
        eps_tile = sb(root, "eps_tile", [P, 8])
        cols = sb(root, "cols", [P, COLS])
        gates_raw = sb(root, "gates_raw", [P, 4])
        gates = sb(root, "gates", [P, 4])
        slots = sb(root, "slots", [P, TILES, 2], U32)
        weight = sb(root, "weight", [P, TILES, 2])

        PSUM = root.enter_context(nc.psum_tensor("PSUM", [P, 8, 512], F32))

        consts_in = sem("consts_in")
        consts_done = sem("consts_done")
        pool_const = sem("pool_const")
        gates_done = sem("gates_done")

        def one(shape):
            ap = ones[:, 0:1]
            for _ in shape[2:]:
                ap = ap.unsqueeze(1)
            return ap.broadcast_to(shape)

        class AttentionSignals:
            x_in = [sem(f"a_x_in{z}") for z in range(2)]
            rows_in = [sem(f"a_rows_in{z}") for z in range(2)]
            ctx_in = [sem(f"a_ctx_in{z}") for z in range(2)]
            w_in = [sem(f"a_w_in{i}") for i in range(4)]
            small_in = sem("a_small_in")
            bias_round = sem("a_bias_round")
            bias_split = sem("a_bias_split")
            w_round = sem("a_w_round")
            w_split = sem("a_w_split")
            mask_in = sem("a_mask_in")
            mask_done = sem("a_mask_done")
            v_ones = sem("a_v_ones")
            v_spread = [sem(f"a_v_spread{z}") for z in range(2)]
            ctx_round = sem("a_ctx_round")
            ctx_split = sem("a_ctx_split")
            bn_done = sem("a_bn_done")
            ln_stats = sem("a_ln_stats")
            ln_eps = sem("a_ln_eps")
            ln_rstd = sem("a_ln_rstd")
            ln_done = sem("a_ln_done")
            ln_kept = sem("a_ln_kept")
            xt_ps = sem("a_xt_ps")
            x_round = sem("a_x_round")
            x_split = sem("a_x_split")
            q_ps = sem("a_q_ps")
            q_round = sem("a_q_round")
            q_split = sem("a_q_split")
            kv_ps = sem("a_kv_ps")
            kv_done = sem("a_kv_done")
            k_rounded = sem("a_k_rounded")
            k_residue = sem("a_k_residue")
            kd_done = sem("a_kd_done")
            scores_ps = sem("a_scores_ps")
            max_done = sem("a_max_done")
            scores_read = sem("a_scores_read")
            exp_done = sem("a_exp_done")
            pt_ps = sem("a_pt_ps")
            pt_done = sem("a_pt_done")
            pv_ps = sem("a_pv_ps")
            sum_done = sem("a_sum_done")
            o_done = sem("a_o_done")
            ot_ps = sem("a_ot_ps")
            o_round = sem("a_o_round")
            o_split = sem("a_o_split")
            y_ps = sem("a_y_ps")
            y_done = sem("a_y_done")
            mixed = sem("a_mixed")
            slot_copied = sem("a_slot_copied")
            mask_cast = sem("a_mask_cast")

        class Attention(AttentionSignals):

            def __init__(self, stage, scope, sums=None, w_raw=None):
                self.stage = stage
                self.base = BATCH * stage
                n = f"a{stage}_"
                two = range(2)
                self.w_raw = w_raw if stage else sb(scope, n + "w_raw", [P, 4, MATRIX])
                self.w_hi = sb(scope, n + "w_hi", [P, 4, KC, DIM], F32R)
                self.w_lo = sb(scope, n + "w_lo", [P, 4, KC, DIM], F32R)
                self.bv = sb(scope, n + "bv", [CTXP, DIM])
                self.bias_raw = sb(scope, n + "bias_raw", [1, DIM])
                self.bias_hi = sb(scope, n + "bias_hi", [1, DIM], F32R)
                self.bias_lo = sb(scope, n + "bias_lo", [1, DIM], F32R)
                self.bq, self.bk = COL_BQ[stage], COL_BK[stage]
                self.mv = sb(scope, n + "mv", [P, BT, 2])
                self.stats = sb(scope, n + "stats", [P, BT, 6])
                self.var_eps = sb(scope, n + "var_eps", [P, BT])
                self.rstd = sb(scope, n + "rstd", [P, BT])
                self.xn = sb(scope, n + "xn", [P, BT, DIM])
                self.x_hi = sb(scope, n + "x_hi", [P, KC, SEQ], F32R)
                self.x_lo = sb(scope, n + "x_lo", [P, KC, SEQ], F32R)
                self.q_hi = [sb(scope, n + f"q_hi{z}", [P, KC, SEQ], F32R) for z in two]
                self.q_lo = [sb(scope, n + f"q_lo{z}", [P, KC, SEQ], F32R) for z in two]
                self.ctx = [sb(scope, n + f"ctx{z}", [P, KC, CTXP]) for z in two]
                self.ctx_hi = [sb(scope, n + f"ctx_hi{z}", [P, KC, CTXP], F32R) for z in two]
                self.ctx_lo = [sb(scope, n + f"ctx_lo{z}", [P, KC, CTXP], F32R) for z in two]
                self.k = sb(scope, n + "k", [P, KC, CTXP])
                self.k_round = sb(scope, n + "k_round", [P, KC, CTXP], F32R)
                self.k_rest = sb(scope, n + "k_rest", [P, KC, CTXP])
                self.kd_hi = [sb(scope, n + f"kd_hi{z}", [P, KC, HPC, CTXP], F32R) for z in two]
                self.kd_lo = [sb(scope, n + f"kd_lo{z}", [P, KC, HPC, CTXP], F32R) for z in two]
                self.v = [sb(scope, n + f"v{z}", [CTXP, HEADS, VW]) for z in two]
                self.v_diagonal = [sb(scope, n + f"v_diagonal{z}", [P, KC, column_of(PC)]) for z in two]
                self.pairs = [sb(scope, n + f"prob{z}", [P, PC, P]) for z in two]
                self.prob = [t[:].rearrange("p c n -> p (c n)")[:, 0:PAIRS].rearrange("p (h n) -> p h n", n=CTXP) for t in self.pairs]
                self.row_max = [sb(scope, n + f"row_max{z}", [P, HPC]) for z in two]
                self.prob_t = [sb(scope, n + f"prob_t{z}", [P, PC, P]) for z in two]
                self.row_sum = [sb(scope, n + f"row_sum{z}", [P, HPC, 1]) for z in two]
                self.o = [sb(scope, n + f"o{z}", [P, BT, DIM]) for z in two]
                self.o_hi = sb(scope, n + "o_hi", [P, KC, SEQ], F32R)
                self.o_lo = sb(scope, n + "o_lo", [P, KC, SEQ], F32R)
                if stage == 0:
                    self.mask_raw = sb(scope, n + "mask_raw", [P, BT, CTXP])
                    self.mask = sb(scope, n + "mask", [P, BT, CTXP], F32R)
                    self.ident = sb(scope, n + "ident", [P, P], F32R)
                else:
                    self.slot = [sb(scope, n + f"slot{z}", [P, BT, 2], U32) for z in two]
                    self.rows = sb(scope, n + "rows", [P, BT, 2, DIM])
                    self.mask_u8 = sb(scope, n + "mask_u8", [1, BATCH, CTX], U8)
                    late_sums = sums[0:1, TILES // 2:, :].rearrange("p t c -> p (t c)")
                    self.mask_raw = late_sums[:, 0:BATCH * CTXP].rearrange("p (b n) -> p b n", n=CTXP)
                    self.mask = sb(scope, n + "mask", [1, BATCH, CTXP], F32R)
                self.scores = PSUM[:, 0:4, :].rearrange("p (b c) n -> p b c n", b=2)
                self.prob_t_ps = PSUM[:, 4:6, :].rearrange("p c (h n) -> p (c h) n", n=P)[:, 0:PC]
                self.o_ps = PSUM[:, 6, 0:HPC * VW].rearrange("p (h n) -> p h n", n=VW)
                self.o_t_bank = PSUM[:, 6, :]
                self.misc = PSUM[:, 7, :]

        def tiles(b):
            return x[:, bass.ds(BT * b.n, BT), :]

        def attention_on_vector(dve, a, z_kept, next_stats=None, next_norm=None):
            def mix(b, s):
                if s == 0:
                    dve.wait_ge(a.rows_in[b.z], 16 * 2 * BT * (b.half + 1))
                else:
                    dve.wait_ge(a.mixed, 2 * b.n + 1)
                for t in range(BT):
                    xt = x[:, bass.ds(BT * b.n + t, 1), :].rearrange("p o c -> p (o c)")
                    last = dve.scalar_tensor_tensor(xt, a.rows[:, t, s, :],
                                                    weight[:, bass.ds(BT * b.n + t, 1), s:s + 1].rearrange("p o c -> p (o c)"),
                                                    xt, ALU.mult, ALU.add)
                last.then_inc(a.mixed, 1)
                if s == 1:
                    dve.wait_ge(a.mixed, 2 * b.n + 2)

            def ln_stats(b):
                if a.stage == 0:
                    dve.wait_ge(a.x_in[b.z], 16 * (b.half + 1))
                for t in range(BT):
                    last = dve.bn_stats(a.stats[:, t, :], x[:, bass.ds(BT * b.n + t, 1), :])
                last.then_inc(a.bn_done, 1)

            def ln_aggregate(b):
                if isinstance(b.n, int):
                    dve.wait_ge(a.bn_done, b.count + 1)
                for t in range(BT):
                    last = dve.bn_aggr(a.mv[:, t, :], a.stats[:, t, :])
                last.then_inc(a.ln_stats, 1)

            def ln_apply(b):
                dve.wait_ge(a.ln_rstd, b.count + 1)
                after(dve, a.xt_ps, b.count)
                if a.stage == 1:
                    after(dve, a.ln_kept, b.n)
                for t in range(BT):
                    last = dve.tensor_scalar(a.xn[:, t, :], x[:, bass.ds(BT * b.n + t, 1), :].rearrange("p o c -> p (o c)"),
                                             a.mv[:, t, 0:1], a.rstd[:, t:t + 1], ALU.subtract, ALU.mult)
                last.then_inc(a.ln_done, 1)

            def x_residue(b):
                dve.wait_ge(a.x_round, b.count + 1)
                dve.tensor_tensor(a.x_lo[:].rearrange("p k n -> p (k n)"), a.misc,
                                  a.x_hi[:].bitcast(F32).rearrange("p k n -> p (k n)"),
                                  ALU.subtract).then_inc(a.x_split, 1)

            def q_residue(b):
                dve.wait_ge(a.q_round, b.count + 1)
                for m in range(KC):
                    last = dve.scalar_tensor_tensor(a.q_lo[b.z][:, m, :], a.misc[:, m * SEQ:(m + 1) * SEQ],
                                                    cols[:, a.bq + m:a.bq + m + 1],
                                                    a.q_hi[b.z][:, m, :].bitcast(F32), ALU.add, ALU.subtract)
                last.then_inc(a.q_split, 1)

            def keys_values(b):
                dve.wait_ge(a.kv_ps, b.count + 1)
                after(dve, a.kd_done, b.count)
                after(dve, a.v_spread[b.z], 16 * PIECES * (b.half + a.base // 2))
                dve.tensor_tensor(a.k[:], a.misc[:, 0:KC * CTXP].rearrange("p (k n) -> p k n", k=KC),
                                  cols[:, a.bk:a.bk + KC].unsqueeze(2).broadcast_to([P, KC, CTXP]), ALU.add)
                dve.tensor_tensor(a.v[b.z][:, :, 0:HD],
                                  a.misc[0:CTXP, DIM:2 * DIM].rearrange("p (h n) -> p h n", n=HD),
                                  a.bv[:].rearrange("p (h n) -> p h n", n=HD),
                                  ALU.add).then_inc(a.kv_done, 1)

            def scores_and_max(j):
                return (a.scores[:, j % 2, :, 0:HPC // 2 * CTXP].rearrange("p c (h n) -> p c h n", n=CTXP),
                        a.row_max[j % 2][:].rearrange("p (c h) -> p c h", c=2))

            def score_max(b, j):
                s, mx = scores_and_max(j)
                dve.wait_ge(a.scores_ps, UNITS * b.count + j + 1)
                dve.tensor_reduce(mx, s, AX.X, ALU.max).then_inc(a.max_done, 1)

            def less_max(b, j):
                u = UNITS * b.count + j
                s, mx = scores_and_max(j)
                dve.wait_ge(a.max_done, u + 1)
                after(dve, a.pt_ps, u - 1)
                dve.tensor_tensor(a.prob[j % 2].rearrange("p (c h) n -> p c h n", c=2), s,
                                  mx.unsqueeze(3).broadcast_to([P, 2, HPC // 2, CTXP]),
                                  ALU.subtract).then_inc(a.scores_read, 1)

            def normalise(b, j):
                u = UNITS * b.count + j
                m, qt = j // BT, j % BT
                dve.wait_ge(a.pv_ps, u + 1)
                dve.reciprocal(a.row_sum[j % 2][:], a.o_ps[:, :, HD:HD + 1]).then_inc(a.sum_done, 1)
                dve.wait_ge(a.sum_done, u + 1)
                dve.tensor_tensor(a.o[b.z][:, qt, m * P:(m + 1) * P].rearrange("p (h n) -> p h n", n=HD),
                                  a.o_ps[:, :, 0:HD], a.row_sum[j % 2][:].broadcast_to([P, HPC, HD]),
                                  ALU.mult).then_inc(a.o_done, 1)

            def o_residue(b):
                dve.wait_ge(a.o_round, b.count + 1)
                dve.tensor_tensor(a.o_lo[:].rearrange("p k n -> p (k n)"), a.o_t_bank,
                                  a.o_hi[:].bitcast(F32).rearrange("p k n -> p (k n)"),
                                  ALU.subtract).then_inc(a.o_split, 1)

            def residual(b):
                dve.wait_ge(a.y_ps, b.count + 1)
                y = a.misc.rearrange("p (t c) -> p t c", t=BT)
                if a.stage == 0:
                    dve.scalar_tensor_tensor(tiles(b), y, gates[:, 0:1], tiles(b), ALU.mult,
                                             ALU.add).then_inc(a.y_done, 1)
                else:
                    kept = z_kept[:, bass.ds(BT * b.n, BT), :]
                    dve.wait_ge(a.ln_kept, b.n + 1)
                    dve.tensor_tensor(kept, y, kept, ALU.add).then_inc(a.y_done, 1)

            dve.wait_ge(consts_done, 1)
            dve.wait_ge(gates_done, 1)
            dve.wait_ge(a.small_in, 32 * (a.stage + 1))
            first = Block(0, 0, 0, a.base)
            second = first.next()
            if a.stage == 1:
                for s in range(2):
                    mix(first, s)
            ln_stats(first)
            ln_aggregate(first)
            ln_apply(first)
            keys_values(first)
            x_residue(first)
            q_residue(first)
            if a.stage == 1:
                for s in range(2):
                    mix(second, s)
            ln_stats(second)
            ln_aggregate(second)

            def body(b, behind, ahead):
                mixing = ahead > 1 and a.stage == 1
                score_max(b, 0)
                less_max(b, 0)
                if behind:
                    normalise(b.last(), 2)
                if ahead:
                    ln_apply(b.next())
                    keys_values(b.next())
                score_max(b, 1)
                less_max(b, 1)
                if behind:
                    normalise(b.last(), 3)
                if ahead:
                    x_residue(b.next())
                score_max(b, 2)
                normalise(b, 0)
                less_max(b, 2)
                if mixing:
                    mix(b.next().next(), 0)
                if behind:
                    o_residue(b.last())
                if mixing:
                    mix(b.next().next(), 1)
                if ahead:
                    q_residue(b.next())
                score_max(b, 3)
                less_max(b, 3)
                if ahead > 1:
                    ln_stats(b.next().next())
                normalise(b, 1)
                if behind:
                    residual(b.last())
                if ahead > 1:
                    ln_aggregate(b.next().next())

            paired_blocks(dve, BATCH, body, a.base, 3)
            final = Block(BATCH - 1, 1, (BATCH - 2) // 2, a.base)
            normalise(final, 2)
            if next_stats:
                next_stats()
            normalise(final, 3)
            o_residue(final)
            if next_norm:
                next_norm()
            residual(final)

        def attention_on_scalar(act, a):
            def x_rounded(b):
                act.wait_ge(a.xt_ps, b.count + 1)
                after(act, a.q_ps, b.count)
                act.activation(a.x_hi[:].rearrange("p k n -> p (k n)"), a.misc, ACT.Copy).then_inc(a.x_round, 1)

            def q_rounded(b):
                act.wait_ge(a.q_ps, b.count + 1)
                for m in range(KC):
                    last = act.activation(a.q_hi[b.z][:, m, :], a.misc[:, m * SEQ:(m + 1) * SEQ], ACT.Identity,
                                          bias=cols[:, a.bq + m:a.bq + m + 1])
                last.then_inc(a.q_round, 1)

            def exponential(b, j):
                act.wait_ge(a.scores_read, UNITS * b.count + j + 1)
                act.activation(a.prob[j % 2], a.prob[j % 2], ACT.Exp,
                               scale=HD ** -0.5).then_inc(a.exp_done, 1)

            def transposed(b, j):
                u = UNITS * b.count + j
                act.wait_ge(a.pt_ps, u + 1)
                after(act, a.pv_ps, u - 1)
                act.activation(a.prob_t[j % 2][:], a.prob_t_ps, ACT.Copy).then_inc(a.pt_done, 1)

            def o_rounded(b):
                act.wait_ge(a.ot_ps, b.count + 1)
                act.activation(a.o_hi[:].rearrange("p k n -> p (k n)"), a.o_t_bank, ACT.Copy).then_inc(a.o_round, 1)

            act.wait_ge(consts_done, 1)
            x_rounded(Block(0, 0, 0, a.base))
            q_rounded(Block(0, 0, 0, a.base))

            def body(b, behind, ahead):
                if behind:
                    transposed(b.last(), 3)
                exponential(b, 0)
                transposed(b, 0)
                exponential(b, 1)
                if ahead:
                    x_rounded(b.next())
                transposed(b, 1)
                if behind:
                    o_rounded(b.last())
                exponential(b, 2)
                if ahead:
                    q_rounded(b.next())
                exponential(b, 3)
                transposed(b, 2)

            paired_blocks(act, BATCH, body, a.base)
            final = Block(BATCH - 1, 1, (BATCH - 2) // 2, a.base)
            transposed(final, 3)
            o_rounded(final)

        def product(pe, ps, pairs, start=True, stop=True):
            n = len(pairs)
            for i, (lh, ll, rh, rl) in enumerate(pairs):
                pe.matmul(ps, lh, rh, start=start and i == 0, stop=False, skip_group_check=not start)
                pe.matmul(ps, ll, rh, start=False, stop=False, skip_group_check=not start)
                last = pe.matmul(ps, lh, rl, start=False, stop=stop and i == n - 1, skip_group_check=not start)
            return last

        def attention_on_tensor(pe, a):
            WQ, WK, WV, WP = range(4)

            def keys_values(b):
                pe.wait_ge(a.ctx_split, b.count + 1)
                after(pe, a.y_done, b.count - 1)
                for m in range(KC):
                    product(pe, a.misc[:, m * CTXP:(m + 1) * CTXP],
                            [(a.w_hi[:, WK, k, m * P:(m + 1) * P], a.w_lo[:, WK, k, m * P:(m + 1) * P],
                              a.ctx_hi[b.z][:, k, :], a.ctx_lo[b.z][:, k, :]) for k in range(KC)])
                product(pe, a.misc[0:CTXP, DIM:2 * DIM],
                        [(a.ctx_hi[b.z][:, k, :], a.ctx_lo[b.z][:, k, :], a.w_hi[:, WV, k, :], a.w_lo[:, WV, k, :])
                         for k in range(KC)]).then_inc(a.kv_ps, 1)

            def transpose_x(b):
                pe.wait_ge(a.ln_done, b.count + 1)
                pe.wait_ge(a.kv_done, b.count + 1)
                for k in range(KC):
                    for t in range(BT):
                        last = pe.transpose(a.misc[:, k * SEQ + t * P:k * SEQ + (t + 1) * P],
                                            a.xn[:, t, k * P:(k + 1) * P], ident[:])
                last.then_inc(a.xt_ps, 1)

            def queries(b):
                pe.wait_ge(a.x_split, b.count + 1)
                for m in range(KC):
                    last = product(pe, a.misc[:, m * SEQ:(m + 1) * SEQ],
                                   [(a.w_hi[:, WQ, k, m * P:(m + 1) * P], a.w_lo[:, WQ, k, m * P:(m + 1) * P],
                                     a.x_hi[:, k, :], a.x_lo[:, k, :]) for k in range(KC)])
                last.then_inc(a.q_ps, 1)

            def score(b, j):
                u = UNITS * b.count + j
                m, qt = j // BT, j % BT
                pe.wait_ge(a.kd_done, b.count + 1)
                pe.wait_ge(a.q_split, b.count + 1)
                after(pe, a.scores_read, u - 1)
                q_hi = a.q_hi[b.z][:, m, qt * P:(qt + 1) * P]
                q_lo = a.q_lo[b.z][:, m, qt * P:(qt + 1) * P]
                for c in range(2):
                    heads = slice(c * HPC // 2, (c + 1) * HPC // 2)
                    ps = a.scores[:, j % 2, c, 0:HPC // 2 * CTXP].rearrange("p (h n) -> p h n", n=CTXP)
                    product(pe, ps, [(q_hi, q_lo, a.kd_hi[b.z][:, m, heads, :], a.kd_lo[b.z][:, m, heads, :])],
                            stop=False)
                    if a.stage == 0:
                        lhs, mask = a.ident[:], a.mask[:, qt, :].unsqueeze(1)
                    else:
                        lhs, mask = ones_r[0:1, :], a.mask[:, bass.ds(b.n, 1), :]
                    last = pe.matmul(ps, lhs, mask.broadcast_to([mask.shape[0], HPC // 2, CTXP]),
                                     start=False, stop=True)
                last.then_inc(a.scores_ps, 1)

            def transpose_prob(b, j):
                u = UNITS * b.count + j
                pe.wait_ge(a.exp_done, u + 1)
                after(pe, a.pt_done, u)
                for c in range(PC):
                    last = pe.transpose(a.prob_t_ps[:, c, :], a.pairs[j % 2][:, c, :], ident[:])
                last.then_inc(a.pt_ps, 1)

            def weigh_values(b, j):
                u = UNITS * b.count + j
                pe.wait_ge(a.pt_done, u + 1)
                after(pe, a.o_done, u)
                if j == 1:
                    after(pe, a.o_split, b.count)
                if j == 0:
                    pe.wait_ge(a.v_spread[b.z], 16 * PIECES * (b.half + a.base // 2 + 1))
                for c in range(PC):
                    first, heads = heads_of(c)
                    at = column_of(c)
                    last = pe.matmul(a.o_ps[:, first:first + heads, :], a.prob_t[j % 2][:, c, :],
                                     a.v_diagonal[b.z][:, j // BT, at:at + heads * VW].rearrange("p (h n) -> p h n", n=VW),
                                     start=c == 0, stop=c == PC - 1, skip_group_check=True)
                last.then_inc(a.pv_ps, 1)

            def transpose_o(b, later):
                pe.wait_ge(a.o_done, UNITS * (b.count + 1) + later)
                for k in range(KC):
                    for t in range(BT):
                        last = pe.transpose(a.o_t_bank[:, k * SEQ + t * P:k * SEQ + (t + 1) * P],
                                            a.o[b.z][:, t, k * P:(k + 1) * P], ident[:])
                last.then_inc(a.ot_ps, 1)

            def project(b, ahead):
                pe.wait_ge(a.o_split, b.count + 1)
                if ahead:
                    pe.wait_ge(a.q_split, b.count + 3)
                else:
                    pe.wait_ge(a.y_done, b.count + 1)
                for t in range(BT):
                    ps = a.misc[:, t * DIM:(t + 1) * DIM]
                    product(pe, ps, [(a.o_hi[:, k, t * P:(t + 1) * P], a.o_lo[:, k, t * P:(t + 1) * P],
                                      a.w_hi[:, WP, k, :], a.w_lo[:, WP, k, :]) for k in range(KC)], stop=False)
                    pe.matmul(ps, ones_r[0:1, :], a.bias_hi[:], start=False, stop=False)
                    last = pe.matmul(ps, ones_r[0:1, :], a.bias_lo[:], start=False, stop=True)
                last.then_inc(a.y_ps, 1)

            pe.wait_ge(consts_done, 1)
            pe.wait_ge(a.bias_split, a.stage + 1)
            pe.wait_ge(a.mask_done, a.stage + 1)
            pe.wait_ge(a.v_ones, 2 * (a.stage + 1))
            pe.wait_ge(a.w_split, 4 * (a.stage + 1))
            first = Block(0, 0, 0, a.base)
            keys_values(first)
            transpose_x(first)
            queries(first)

            def body(b, behind, ahead):
                score(b, 0)
                if behind:
                    weigh_values(b.last(), 2)
                    transpose_prob(b.last(), 3)
                score(b, 1)
                if ahead:
                    keys_values(b.next())
                if behind:
                    weigh_values(b.last(), 3)
                transpose_prob(b, 0)
                if ahead:
                    transpose_x(b.next())
                score(b, 2)
                weigh_values(b, 0)
                transpose_prob(b, 1)
                score(b, 3)
                if behind:
                    transpose_o(b.last(), 1)
                if ahead:
                    queries(b.next())
                weigh_values(b, 1)
                transpose_prob(b, 2)
                if behind:
                    project(b.last(), ahead)

            paired_blocks(pe, BATCH, body, a.base)
            final = Block(BATCH - 1, 1, (BATCH - 2) // 2, a.base)
            weigh_values(final, 2)
            transpose_prob(final, 3)
            weigh_values(final, 3)
            transpose_o(final, 0)
            project(final, False)

        def attention_on_gpsimd(pool, a, z_kept, side_job):
            def split_context(b):
                pool.wait_ge(a.ctx_in[b.z], 16 * (b.half + a.base // 2 + 1))
                after(pool, a.kv_ps, b.count - 1)
                pool.tensor_tensor(a.ctx_hi[b.z][:], a.ctx[b.z][:], one([P, KC, CTXP]), ALU.mult).then_inc(a.ctx_round, 1)
                pool.wait_ge(a.ctx_round, b.count + 1)
                pool.tensor_tensor(a.ctx_lo[b.z][:], a.ctx[b.z][:], a.ctx_hi[b.z][:].bitcast(F32),
                                   ALU.subtract).then_inc(a.ctx_split, 1)

            def inverse_std(b):
                pool.wait_ge(a.ln_stats, b.count + 1)
                after(pool, a.ln_done, b.count)
                pool.tensor_tensor(a.var_eps[:], a.mv[:, :, 1], eps_tile[:, 0:BT], ALU.add).then_inc(a.ln_eps, 1)
                pool.wait_ge(a.ln_eps, b.count + 1)
                pool.tensor_tensor(a.rstd[:], a.var_eps[:], neghalf[:, 0:BT], ALU.pow).then_inc(a.ln_rstd, 1)

            def keep_query(b):
                pool.wait_ge(a.ln_done, b.count + 1)
                pool.tensor_tensor(z_kept[:, bass.ds(BT * b.n, BT), :], a.xn[:], one([P, BT, DIM]),
                                   ALU.mult).then_inc(a.ln_kept, 1)

            def diagonal_keys(b):
                pool.wait_ge(a.kv_done, b.count + 1)
                pool.tensor_tensor(a.k_round[:], a.k[:], one([P, KC, CTXP]), ALU.mult).then_inc(a.k_rounded, 1)
                pool.wait_ge(a.k_rounded, b.count + 1)
                pool.tensor_tensor(a.k_rest[:], a.k[:], a.k_round[:].bitcast(F32),
                                   ALU.subtract).then_inc(a.k_residue, 1)
                pool.wait_ge(a.k_residue, b.count + 1)
                hm = headmask[:].unsqueeze(2).broadcast_to([P, HPC, CTXP])
                for part, kd in ((a.k, a.kd_hi), (a.k_rest, a.kd_lo)):
                    for m in range(KC):
                        last = pool.tensor_tensor(kd[b.z][:, m], part[:, m, :].unsqueeze(1).broadcast_to([P, HPC, CTXP]),
                                                  hm, ALU.mult)
                last.then_inc(a.kd_done, 1)

            def slots_of(b):
                after(pool, a.mixed, 2 * b.n)
                pool.tensor_copy(a.slot[b.z][:], slots[:, bass.ds(BT * b.n, BT), :]).then_inc(a.slot_copied, 1)
                pool.wait_ge(a.slot_copied, b.n + 1)

            def fetch(b):
                for t in range(BT):
                    for s in range(2):
                        pool.indirect_dma_start(a.rows[:, t, s, :], None, d["sorted_y"],
                                                bass.IndirectOffsetOnAxis(ap=a.slot[b.z][:, t, s:s + 1], axis=0)).then_inc(a.rows_in[b.z], 16)

            first = Block(0, 0, 0, a.base)
            if a.stage == 1:
                slots_of(first)
                fetch(first)
            for z in range(2):
                pool.memset(a.v[z][:], 1.0)
                pool.memset(a.pairs[z][:], 0.0)
                pool.memset(a.v_diagonal[z][:], 0.0).then_inc(a.v_ones, 1)
            split_context(first)
            if a.stage == 1:
                slots_of(first.next())
            inverse_std(first)
            if a.stage == 1:
                fetch(first.next())
                keep_query(first)
            diagonal_keys(first)
            split_context(first.next())

            def body(b, behind, ahead):
                if ahead > 1 and a.stage == 1:
                    slots_of(b.next().next())
                if ahead:
                    inverse_std(b.next())
                if ahead > 1 and a.stage == 1:
                    fetch(b.next().next())
                if ahead:
                    diagonal_keys(b.next())
                    if a.stage == 1:
                        keep_query(b.next())
                if ahead > 1:
                    split_context(b.next().next())
                side_job(b)

            paired_blocks(pool, BATCH, body, a.base, 3)

        class TokenSignals:
            bn_done = sem("t_bn_done")
            ln_stats = sem("t_ln_stats")
            ln_rstd = sem("t_ln_rstd")
            ln_done = sem("t_ln_done")
            xt_ps = sem("t_xt_ps")
            x_round = sem("t_x_round")
            x_split = sem("t_x_split")

        class Mixture(TokenSignals):

            def __init__(self, scope):
                two = range(2)
                sb(scope, "moe_w_place", [P, (EXPERTS + 1) * EXPERT_COLS], F32R)
                self.w = moe_w
                self.raw = [sb(scope, f"late_raw{z}", [P, MOE_CHUNK]) for z in two]
                self.gate = sb(scope, "m_gate", [P, KC, EXPERTS])
                self.bias = sb(scope, "m_bias", [BIAS_ROWS, 3 * DIM])
                self.bias_parts = sb(scope, "m_bias_parts", [BIAS_ROWS, 3 * DIM], F32R)
                self.row_of = sb(scope, "m_row_of", [BIAS_ROWS, 4])
                self.expert_f, self.chosen = (self.bias[:, n * SORTED:(n + 1) * SORTED] for n in two)
                self.shared_choice = sb(scope, "m_shared_choice", [BIAS_ROWS, P], F32R)
                self.stats = [sb(scope, f"m_stats{z}", [P, MT, 6]) for z in two]
                self.mv = [sb(scope, f"m_mv{z}", [P, MT, 2]) for z in two]
                self.var_eps = [sb(scope, f"m_var_eps{z}", [P, MT]) for z in two]
                self.rstd = [sb(scope, f"m_rstd{z}", [P, MT]) for z in two]
                self.xn = sb(scope, "m_xn", [P, TILES, DIM])
                self.x_hi = [sb(scope, f"m_x_hi{z}", [P, KC, SEQ], F32R) for z in two]
                self.x_lo = [sb(scope, f"m_x_lo{z}", [P, KC, SEQ], F32R) for z in two]
                self.h = [sb(scope, f"m_h{z}", [P, KC, SEQ]) for z in two]
                self.h_hi = [sb(scope, f"m_h_hi{z}", [P, KC, SEQ], F32R) for z in two]
                self.h_lo = [sb(scope, f"m_h_lo{z}", [P, KC, SEQ], F32R) for z in two]
                self.tile_x = [self.xn[:, z * GROUP:(z + 1) * GROUP, :] for z in two]
                self.tile_y = [self.xn[:, (2 + z) * GROUP:(3 + z) * GROUP, :] for z in two]
                self.choice = [self.x_hi[z // KC][0:BIAS_ROWS, z % KC, P:] for z in range(CHOICES)]

                def by_token(buffer):
                    return buffer.rearrange("p (t e) -> p t e", e=EXPERTS)

                def by_expert(buffer):
                    return buffer.rearrange("p (e t) -> p e t", e=EXPERTS)
                self.p, self.rest = (by_token(self.h[1][:, n, :]) for n in two)
                self.place, self.count = (by_expert(self.h[1][:, n, :]) for n in two)
                self.pick = [by_token(self.h_lo[0][:, n, :]) for n in two]
                self.both = by_token(self.h_hi[1][:, 0, :])
                self.earlier_r = self.h_hi[1][:, 1, 0:P]
                self.earlier = sb(scope, "m_earlier", [P, P])
                self.restart = sb(scope, "m_restart", [P, EXPERTS, TILES])
                self.rank = sb(scope, "m_rank", [P, EXPERTS])
                self.top = sb(scope, "m_top", [P, TILES, 1])
                self.ends = sb(scope, "m_ends", [P, EXPERTS])
                self.starts = sb(scope, "m_starts", [P, EXPERTS])
                self.tiles_of = sb(scope, "m_tiles_of", [P, EXPERTS])
                self.number = sb(scope, "m_number", [BIAS_ROWS, SORTED])
                self.expert = sb(scope, "m_expert", [1, SORTED], I32)
                self.up_ps = PSUM[:, 0:2, :].rearrange("p g (o n) -> p g o n", o=KC)
                self.tile_up_ps = PSUM[:, 0:2, :]
                self.xt_bank = PSUM[:, 2, :].rearrange("p (k n) -> p k n", k=KC)
                self.ht_bank = PSUM[:, 3, 0:DIM].rearrange("p (k n) -> p k n", k=KC)
                self.y_ps_bank = PSUM[:, 4, :].rearrange("p (t c) -> p t c", c=DIM)
                self.logits = PSUM[:, 5, 0:TILES * EXPERTS].rearrange("p (t e) -> p t e", e=EXPERTS)
                self.norm_bank = [PSUM[:, 6 + z, :].rearrange("p (k n) -> p k n", k=KC) for z in two]
                self.rank_ps = PSUM[:, 6, 0:TILES * EXPERTS].rearrange("p (e t) -> p e t", t=TILES)
                self.total_ps = PSUM[:, 7, 0:TILES * EXPERTS].rearrange("p (e t) -> p e t", t=TILES)
                self.late_in = [sem(f"m_late_in{z}") for z in two]
                self.tile_in = [sem(f"m_tile_in{z}") for z in two]
                self.tile_out = [sem(f"m_tile_out{z}") for z in two]
                self.small_in = sem("m_small_in")
                self.const_done = sem("m_const_done")
                self.small_round = sem("m_small_round")
                self.late_round = sem("m_late_round")
                self.late_split = sem("m_late_split")
                self.bias_split = sem("m_bias_split")
                self.ln_eps = sem("m_ln_eps")
                self.logits_ps = sem("m_logits_ps")
                self.logits_read = sem("m_logits_read")
                self.gate_exp = sem("m_gate_exp")
                self.route = sem("m_route")
                self.picks_done = sem("m_picks_done")
                self.ranks_ps = sem("m_ranks_ps")
                self.slots_done = sem("m_slots_done")
                self.chosen_done = sem("m_chosen_done")
                self.scattered = sem("m_scattered")
                self.t_ps = sem("m_t_ps")
                self.t_round = sem("m_t_round")
                self.t_split = sem("m_t_split")
                self.up_done = sem("m_up_done")
                self.silu_done = sem("m_silu_done")
                self.gated = sem("m_gated")
                self.ht_ps = sem("m_ht_ps")
                self.h_round = sem("m_h_round")
                self.h_split = sem("m_h_split")
                self.y_ps = sem("m_y_ps")
                self.y_done = sem("m_y_done")

            def choice_of(self, g, j):
                return self.choice[(GROUP * g.z + j) % CHOICES]

            def chunk(self, n):
                return tuple(self.w[:, bass.ds((2 * n + part) * MOE_CHUNK, MOE_CHUNK)] for part in range(2))

        SHARED = BATCH
        AHEAD = 2
        final_group = Block(GROUPS - 1, 1, (GROUPS - 2) // 2)

        def at(g, j, behind, ahead, step):
            if j < 0:
                if behind:
                    step(g.last(), j + GROUP)
            elif j < GROUP:
                step(g, j)
            elif ahead:
                step(g.next(), j - GROUP)

        def mixture_on_sync(sp, m):
            sp.wait_ge(a0.y_done, BATCH + 1)
            sp.wait_ge(side_split, EARLY_CHUNKS)
            for dst, name in ((m.gate[:].rearrange("p k e -> p (k e)"), "gate_w"), (m.bias[:], "moe_b"),
                              (m.number[:], "tile_numbers"), (m.row_of[:], "row_of")):
                sp.dma_start(dst, d[name]).then_inc(m.small_in, 16)

            def load_late(b, behind, ahead):
                after(sp, m.late_split, b.n - 1)
                sp.dma_start(m.raw[b.z][:], d["moe_w"][:, bass.ds((EARLY_CHUNKS + b.n) * MOE_CHUNK, MOE_CHUNK)]
                             ).then_inc(m.late_in[b.z], 16)

            load_late(Block(0, 0, 0), False, True)
            load_late(Block(1, 1, 0), True, True)
            with sp.Fori(1, LATE_CHUNKS // 2) as i:
                load_late(Block(2 * i, 0, i), True, True)
                load_late(Block(2 * i + 1, 1, i), True, True)
            load_late(Block(LATE_CHUNKS - 1, 0, LATE_CHUNKS // 2), True, False)
            sp.wait_ge(m.scattered, 16 * 2 * TILES)

            sorted_x, sorted_y = (d[n].rearrange("(t p) c -> p t c", p=P) for n in ("sorted_x", "sorted_y"))

            def load(g):
                after(sp, m.t_ps, SHARED + GROUP * (g.n - 1))
                sp.dma_start(m.tile_x[g.z], sorted_x[:, bass.ds(GROUP * g.n, GROUP), :]).then_inc(m.tile_in[g.z], 16)

            def store(g):
                sp.wait_ge(m.y_done, SHARED + GROUP * (g.n + 1))
                sp.dma_start(sorted_y[:, bass.ds(GROUP * g.n, GROUP), :], m.tile_y[g.z]).then_inc(m.tile_out[g.z], 16)

            sp.wait_ge(m.t_ps, SHARED)
            load(Block(0, 0, 0))

            def body(g, behind, ahead):
                if ahead:
                    load(g.next())
                if behind:
                    store(g.last())

            paired_blocks(sp, GROUPS, body)
            store(Block(GROUPS - 1, 1, (GROUPS - 2) // 2))

        def mixture_on_gpsimd(pool, m):
            pool.wait_ge(a0.y_done, BATCH + 1)
            for e in range(EXPERTS):
                last = pool.memset(m.rank[:, e:e + 1], float(EXPERTS - e))
            last.then_inc(m.const_done, 1)
            pool.memset(m.restart[:], 1.0).then_inc(m.const_done, 1)
            pool.memset(m.earlier[:], 1.0).then_inc(m.const_done, 1)
            pool.wait_ge(m.const_done, 3)
            pool.memset(m.restart[:, :, 0:1], 0.0).then_inc(m.const_done, 1)
            pool.affine_select(out=m.earlier[:], in_=m.earlier[:], compare_op=ALU.is_ge, fill=0.0, base=-1,
                               pattern=[[1, P]], channel_multiplier=-1).then_inc(m.const_done, 1)

            def inverse_std(b):
                pool.wait_ge(m.ln_stats, 2 * (b.n + 1))
                after(pool, m.ln_done, 2 * (b.n - 1))
                pool.tensor_tensor(m.var_eps[b.z][:], m.mv[b.z][:, :, 1], eps_tile[:, 0:MT], ALU.add).then_inc(m.ln_eps, 1)
                pool.wait_ge(m.ln_eps, b.n + 1)
                pool.tensor_tensor(m.rstd[b.z][:], m.var_eps[b.z][:], neghalf[:, 0:MT], ALU.pow).then_inc(m.ln_rstd, 2)

            def split_late(b):
                hi, lo = m.chunk(EARLY_CHUNKS + b.n)
                pool.wait_ge(m.late_in[b.z], 16 * (b.half + 1))
                pool.tensor_tensor(hi, m.raw[b.z][:], one([P, MOE_CHUNK]), ALU.mult).then_inc(m.late_round, 1)
                pool.wait_ge(m.late_round, b.n + 1)
                pool.tensor_tensor(lo, m.raw[b.z][:], hi.bitcast(F32), ALU.subtract).then_inc(m.late_split, 1)

            inverse_std(Block(0, 0, 0))

            def body(b, behind, ahead):
                if ahead:
                    inverse_std(b.next())
                split_late(b)

            paired_blocks(pool, MB, body)
            for n in range(MB, LATE_CHUNKS):
                split_late(Block(n, n % 2, n // 2))
            pool.wait_ge(m.slots_done, 1)
            pool.wait_ge(zeros_out, 16 * (BATCH + 1))
            for t in range(TILES):
                for s in range(2):
                    pool.indirect_dma_start(d["sorted_x"], bass.IndirectOffsetOnAxis(ap=slots[:, t, s:s + 1], axis=0),
                                            m.xn[:, t, :], None).then_inc(m.scattered, 16)
            pool.wait_ge(m.up_done, SHARED)
            pool.wait_ge(m.slots_done, 2)

            def choose(g, behind, ahead):
                for j in range(GROUP):
                    n = GROUP * g.n + j
                    after(pool, m.y_ps, SHARED + n - CHOICES + 1)
                    column = m.chosen[:, bass.ds(n, 1)].broadcast_to([BIAS_ROWS, P])
                    pool.tensor_tensor(m.choice_of(g, j), column, ones[0:BIAS_ROWS, :], ALU.mult).then_inc(m.chosen_done, 1)

            paired_blocks(pool, GROUPS, choose)

        def mixture_on_scalar(act, m):
            act.wait_ge(a0.y_done, BATCH + 1)
            act.wait_ge(m.small_in, 64)
            act.activation(m.bias_parts[:], m.bias[:], ACT.Copy).then_inc(m.small_round, 1)

            def norm_copied(b, behind, ahead):
                act.wait_ge(m.xt_ps, b.n + 1)
                after(act, m.logits_ps, b.n - 1)
                act.activation(m.h[b.z][:], m.norm_bank[b.z], ACT.Copy).then_inc(m.x_round, 1)

            paired_blocks(act, BATCH, norm_copied)
            act.wait_ge(m.logits_read, 1)
            act.activation(m.p, m.p, ACT.Exp).then_inc(m.gate_exp, 1)

            def shared_rounded(b):
                act.wait_ge(m.t_ps, b.n + 1)
                act.activation(m.x_hi[b.z][:], m.xt_bank, ACT.Copy).then_inc(m.t_round, 1)

            shared_rounded(Block(0, 0, 0))

            def shared(b, behind, ahead):
                act.wait_ge(m.up_done, b.n + 1)
                after(act, m.h_split, b.n - 1)
                for o in range(KC):
                    last = act.activation(m.h[b.z][:, o], m.up_ps[:, 0, o], ACT.Silu, bias=cols[:, COL_B1 + o:COL_B1 + o + 1])
                last.then_inc(m.silu_done, 1)
                if ahead:
                    shared_rounded(b.next())
                act.wait_ge(m.gated, b.n + 1)
                after(act, m.y_ps, b.n - 1)
                act.activation(m.h_hi[b.z][:], m.h[b.z][:], ACT.Copy).then_inc(m.h_round, 1)

            paired_blocks(act, BATCH, shared)

            def x_rounded(g, j):
                act.wait_ge(m.t_ps, SHARED + GROUP * g.n + j + 1)
                act.activation(m.x_hi[j % 2][:, :, 0:P], m.xt_bank[:, :, 0:P], ACT.Copy).then_inc(m.t_round, 1)

            def activate(g, j):
                act.wait_ge(m.up_done, SHARED + GROUP * g.n + j + 1)
                act.activation(m.h[j % 2][:, 0], m.tile_up_ps[:, j % 2, 0:DIM], ACT.Silu).then_inc(m.silu_done, 1)

            def h_rounded(g, j):
                act.wait_ge(m.ht_ps, GROUP * g.n + j + 1)
                act.activation(m.h_hi[j % 2][:, :, 0:P], m.ht_bank, ACT.Copy).then_inc(m.h_round, 1)

            def output(g, j):
                act.wait_ge(m.y_ps, SHARED + GROUP * g.n + j + 1)
                if j == 0:
                    after(act, m.tile_out[g.z], 16 * g.half)
                act.activation(m.tile_y[g.z][:, j, :], m.y_ps_bank[:, 0], ACT.Copy).then_inc(m.y_done, 1)

            act.wait_ge(m.y_ps, SHARED)
            act.wait_ge(m.scattered, 16 * 2 * TILES)
            for j in range(AHEAD):
                x_rounded(Block(0, 0, 0), j)

            def tiles_of(g, behind, ahead):
                for j in range(GROUP):
                    activate(g, j)
                    at(g, j - 1, behind, ahead, h_rounded)
                    at(g, j + AHEAD, behind, ahead, x_rounded)
                    at(g, j - 2, behind, ahead, output)

            paired_blocks(act, GROUPS, tiles_of)
            h_rounded(final_group, GROUP - 1)
            output(final_group, GROUP - 2)
            output(final_group, GROUP - 1)

        def mixture_on_vector(dve, m):
            def ln_stats(b):
                for t in range(MT):
                    last = dve.bn_stats(m.stats[b.z][:, t, :], x[:, bass.ds(MT * b.n + t, 1), :])
                last.then_inc(m.bn_done, 2)
                dve.wait_ge(m.bn_done, 2 * (b.n + 1))

            def ln_aggregate(b):
                for t in range(MT):
                    last = dve.bn_aggr(m.mv[b.z][:, t, :], m.stats[b.z][:, t, :])
                last.then_inc(m.ln_stats, 2)

            def ln_apply(b):
                dve.wait_ge(m.ln_rstd, 2 * (b.n + 1))
                for t in range(MT):
                    xt = x[:, bass.ds(MT * b.n + t, 1), :].rearrange("p o c -> p (o c)")
                    last = dve.tensor_scalar(m.xn[:, bass.ds(MT * b.n + t, 1), :].rearrange("p o c -> p (o c)"), xt,
                                             m.mv[b.z][:, t, 0:1], m.rstd[b.z][:, t:t + 1], ALU.subtract, ALU.mult)
                    if t % BT == BT - 1:
                        last.then_inc(m.ln_done, 1)

            dve.wait_ge(a0.y_done, BATCH + 1)
            first = Block(0, 0, 0)
            ln_stats(first)
            ln_aggregate(first)

            def norm(b, behind, ahead):
                if ahead:
                    ln_stats(b.next())
                ln_apply(b)
                if ahead:
                    ln_aggregate(b.next())

            paired_blocks(dve, MB, norm)

            def shared_residue(b):
                dve.wait_ge(m.t_round, b.n + 1)
                dve.tensor_tensor(m.x_lo[b.z][:], m.xt_bank, m.x_hi[b.z][:].bitcast(F32),
                                  ALU.subtract).then_inc(m.x_split, 1)

            wide = [P, TILES, EXPERTS]

            def flat(values):
                return values.rearrange("p e t -> p (e t)")

            top = m.top[:].broadcast_to(wide)
            count = [0]

            def step(instruction):
                count[0] += 1
                instruction.then_inc(m.route, 1)
                dve.wait_ge(m.route, count[0])

            def largest(pick, values):
                rank = m.rank[:].unsqueeze(1).broadcast_to(wide)
                step(dve.tensor_reduce(m.top[:, :, 0], values, AX.X, ALU.max))
                step(dve.tensor_tensor(pick, values, top, ALU.is_ge))
                step(dve.tensor_tensor(pick, pick.bitcast(F32), rank, ALU.mult))
                step(dve.tensor_reduce(m.top[:, :, 0], pick.bitcast(F32), AX.X, ALU.max))
                step(dve.tensor_tensor(pick, pick.bitcast(F32), top, ALU.is_equal))

            dve.wait_ge(m.small_round, 1)
            step(dve.tensor_tensor(m.bias[:], m.bias[:], m.bias_parts[:].bitcast(F32), ALU.subtract))
            step(dve.tensor_scalar(m.bias[:], m.bias[:], m.row_of[:, 2:3], None, ALU.mult))
            dve.tensor_scalar(m.shared_choice[:], ones[0:BIAS_ROWS, :], m.row_of[:, 3:4], None, ALU.mult)
            dve.scalar_tensor_tensor(m.bias_parts[:], m.bias_parts[:].bitcast(F32), m.row_of[:, 1:2], m.bias[:], ALU.mult,
                                     ALU.add).then_inc(m.bias_split, 1)
            dve.wait_ge(m.const_done, 5)
            step(dve.tensor_copy(m.earlier_r, m.earlier[:]))
            dve.wait_ge(m.logits_ps, BATCH)
            step(dve.tensor_reduce(m.top[:, :, 0], m.logits, AX.X, ALU.max))
            dve.tensor_tensor(m.p, m.logits, top, ALU.subtract).then_inc(m.logits_read, 1)
            shared_residue(first)
            dve.wait_ge(m.gate_exp, 1)
            step(dve.tensor_reduce(m.top[:, :, 0], m.p, AX.X, ALU.add))
            step(dve.reciprocal(m.top[:], m.top[:]))
            step(dve.tensor_tensor(m.p, m.p, top, ALU.mult))
            largest(m.pick[0], m.p)
            step(dve.scalar_tensor_tensor(m.rest, m.pick[0].bitcast(F32), -2.0, m.p, ALU.mult, ALU.add))
            largest(m.pick[1], m.rest)
            dve.tensor_tensor(m.both, m.pick[0].bitcast(F32), m.pick[1].bitcast(F32), ALU.add).then_inc(m.picks_done, 1)
            for s in range(2):
                step(dve.tensor_tensor(m.rest, m.p, m.pick[s].bitcast(F32), ALU.mult))
                step(dve.tensor_reduce(m.top[:, :, 0], m.rest, AX.X, ALU.add))
                step(dve.tensor_scalar(weight[:, :, s:s + 1], m.top[:], gates[:, 2:3], None, ALU.mult))
            dve.wait_ge(m.ranks_ps, 1)
            step(dve.tensor_tensor_scan(flat(m.count), flat(m.restart[:]), flat(m.total_ps), 0.0, ALU.mult, ALU.add))
            step(dve.tensor_scalar(m.tiles_of[:], m.count[:, :, TILES - 1], 1.0 / P, (P - 0.5) / P - 0.5, ALU.mult, ALU.add))
            step(dve.tensor_scalar(m.tiles_of[:], m.tiles_of[:], ROUND, None, ALU.add))
            step(dve.tensor_scalar(m.tiles_of[:], m.tiles_of[:], ROUND, None, ALU.subtract))
            step(dve.tensor_tensor_scan(m.ends[:], ones[:, 0:EXPERTS], m.tiles_of[:], 0.0, ALU.mult, ALU.add))
            step(dve.tensor_tensor(m.starts[:], m.ends[:], m.tiles_of[:], ALU.subtract))
            step(dve.tensor_scalar(m.starts[:], m.starts[:], float(P), None, ALU.mult))
            step(dve.tensor_tensor(m.place, m.count, m.total_ps, ALU.subtract))
            step(dve.tensor_tensor(m.place, m.place, m.rank_ps, ALU.add))
            step(dve.tensor_tensor(m.place, m.place, m.starts[:].unsqueeze(2).broadcast_to([P, EXPERTS, TILES]), ALU.add))
            place = m.place.rearrange("p e t -> p t e")
            for s in range(2):
                step(dve.tensor_tensor(m.rest, place, m.pick[s].bitcast(F32), ALU.mult))
                step(dve.tensor_reduce(m.top[:, :, 0], m.rest, AX.X, ALU.add))
                last = dve.tensor_copy(slots[:, :, s:s + 1], m.top[:])
                if s == 0:
                    step(last)
            last.then_inc(m.slots_done, 1)

            def tile_experts():
                step(dve.tensor_scalar(m.expert_f, m.number[:], m.ends[0:BIAS_ROWS, 0:1], None, ALU.is_ge))
                for e in range(1, EXPERTS):
                    step(dve.scalar_tensor_tensor(m.expert_f, m.number[:], m.ends[0:BIAS_ROWS, e:e + 1], m.expert_f,
                                                  ALU.is_ge, ALU.add))
                step(dve.tensor_scalar(m.expert_f, m.expert_f, EXPERTS - 1.0, None, ALU.min))
                step(dve.tensor_scalar(m.chosen, m.expert_f, m.row_of[:, 0:1], None, ALU.is_equal))
                dve.tensor_scalar(m.expert[:], m.expert_f[0:1, :], float(EXPERT_COLS), float(EXPERT_COLS), ALU.mult,
                                  ALU.add).then_inc(m.slots_done, 1)

            def add(b):
                dve.wait_ge(m.y_ps, b.n + 1)
                xb = tiles(b)
                dve.scalar_tensor_tensor(xb, m.y_ps_bank, gates[:, 2:3], xb, ALU.mult, ALU.add).then_inc(m.y_done, 1)

            def shared(b, behind, ahead):
                dve.wait_ge(m.silu_done, b.n + 1)
                for o in range(KC):
                    last = dve.scalar_tensor_tensor(m.h[b.z][:, o], m.up_ps[:, 1, o], cols[:, COL_B3 + o:COL_B3 + o + 1],
                                                    m.h[b.z][:, o], ALU.add, ALU.mult)
                last.then_inc(m.gated, 1)
                if ahead:
                    shared_residue(b.next())
                dve.wait_ge(m.h_round, b.n + 1)
                dve.tensor_tensor(m.h_lo[b.z][:], m.h[b.z][:], m.h_hi[b.z][:].bitcast(F32), ALU.subtract).then_inc(m.h_split, 1)
                if behind:
                    add(b.last())
                if not ahead:
                    tile_experts()

            paired_blocks(dve, BATCH, shared)
            add(Block(BATCH - 1, 1, (BATCH - 2) // 2))

            def x_residue(g, j):
                dve.wait_ge(m.t_round, SHARED + GROUP * g.n + j + 1)
                dve.tensor_tensor(m.x_lo[j % 2][:, :, 0:P], m.xt_bank[:, :, 0:P], m.x_hi[j % 2][:, :, 0:P].bitcast(F32),
                                  ALU.subtract).then_inc(m.t_split, 1)

            def h_residue(g, j):
                dve.wait_ge(m.h_round, SHARED + GROUP * g.n + j + 1)
                dve.tensor_tensor(m.h_lo[j % 2][:, :, 0:P], m.ht_bank, m.h_hi[j % 2][:, :, 0:P].bitcast(F32),
                                  ALU.subtract).then_inc(m.h_split, 1)

            def gate(g, j):
                dve.wait_ge(m.silu_done, SHARED + GROUP * g.n + j + 1)
                h = m.h[j % 2][:, 0]
                dve.tensor_tensor(h, m.tile_up_ps[:, j % 2, DIM:], h, ALU.mult).then_inc(m.gated, 1)

            for j in range(AHEAD):
                x_residue(first, j)

            def tiles_of(g, behind, ahead):
                for j in range(GROUP):
                    gate(g, j)
                    at(g, j - 1, behind, ahead, h_residue)
                    at(g, j + AHEAD, behind, ahead, x_residue)

            paired_blocks(dve, GROUPS, tiles_of)
            h_residue(final_group, GROUP - 1)

        def mixture_on_tensor(pe, m):
            def every_block(body):
                for n in range(BATCH):
                    body(Block(n, n % 2, n // 2), n > 0, n < BATCH - 1)

            def transpose_normed(b, bank):
                tokens = m.xn[:, BT * b.n:BT * (b.n + 1), :]
                for k in range(KC):
                    for t in range(BT):
                        last = pe.transpose(bank[:, k, t * P:(t + 1) * P], tokens[:, t, k * P:(k + 1) * P], ident[:])
                return last

            def norm_transposed(b):
                pe.wait_ge(m.ln_done, b.n + 1)
                transpose_normed(b, m.norm_bank[b.z]).then_inc(m.xt_ps, 1)

            def logits(b):
                pe.wait_ge(m.x_round, b.n + 1)
                for t in range(BT):
                    for k in range(KC):
                        last = pe.matmul(m.logits[:, BT * b.n + t, :], m.h[b.z][:, k, t * P:(t + 1) * P], m.gate[:, k],
                                         start=k == 0, stop=k == KC - 1)
                last.then_inc(m.logits_ps, 1)

            pe.wait_ge(m.small_in, 64)
            norm_transposed(Block(0, 0, 0))

            def norm(b, behind, ahead):
                if ahead:
                    norm_transposed(b.next())
                logits(b)

            every_block(norm)

            def shared_transposed(b):
                transpose_normed(b, m.xt_bank).then_inc(m.t_ps, 1)

            def ranks():
                both = m.both.rearrange("p t e -> p e t")
                pe.wait_ge(m.picks_done, 1)
                pe.matmul(m.rank_ps, m.earlier_r, both, start=True, stop=True)
                pe.matmul(m.total_ps, ones_r[:], both, start=True, stop=True).then_inc(m.ranks_ps, 1)

            shared_transposed(Block(0, 0, 0))
            up_w = [m.chunk(k) for k in range(KC)]
            down_w = [w.rearrange("p (k c) -> p k c", k=KC) for w in m.chunk(KC)]

            def shared_down(b):
                pe.wait_ge(m.h_split, b.n + 1)
                after(pe, m.y_done, b.n)
                for t in range(BT):
                    part = slice(t * P, (t + 1) * P)
                    product(pe, m.y_ps_bank[:, t], [(m.h_hi[b.z][:, k, part], m.h_lo[b.z][:, k, part], down_w[0][:, k], down_w[1][:, k])
                                                    for k in range(KC)], stop=False)
                    last = pe.matmul(m.y_ps_bank[:, t], m.shared_choice[:], m.bias_parts[:, 2 * DIM:], start=False, stop=True)
                last.then_inc(m.y_ps, 1)

            def shared(b, behind, ahead):
                pe.wait_ge(m.x_split, b.n + 1)
                after(pe, m.gated, b.n)
                for g in range(2):
                    for o in range(KC):
                        part = slice(g * DIM + o * P, g * DIM + (o + 1) * P)
                        last = product(pe, m.up_ps[:, g, o], [(up_w[k][0][:, part], up_w[k][1][:, part],
                                                               m.x_hi[b.z][:, k], m.x_lo[b.z][:, k]) for k in range(KC)])
                last.then_inc(m.up_done, 1)
                if ahead:
                    shared_transposed(b.next())
                if behind:
                    shared_down(b.last())
                else:
                    ranks()
                    pe.wait_ge(m.bias_split, 1)

            every_block(shared)
            shared_down(Block(BATCH - 1, 1, (BATCH - 2) // 2))

            def transpose_x(g, j):
                if j == 0:
                    pe.wait_ge(m.tile_in[g.z], 16 * (g.half + 1))
                after(pe, m.t_split, GROUP * g.n + j)
                for k in range(KC):
                    last = pe.transpose(m.xt_bank[:, k, 0:P], m.tile_x[g.z][:, j, k * P:(k + 1) * P], ident[:])
                last.then_inc(m.t_ps, 1)

            def weights(g, j):
                return pe.value_load(m.expert[0:1, bass.ds(GROUP * g.n + j, 1)], min_val=EXPERT_COLS,
                                     max_val=EXPERTS * EXPERT_COLS)

            def part(at, n):
                return m.w[:, bass.ds(at + n * MOE_CHUNK, MOE_CHUNK)]

            def up(g, j, w):
                n = GROUP * g.n + j
                pe.wait_ge(m.chosen_done, n + 1)
                pe.wait_ge(m.t_split, n + 1)
                ps = m.tile_up_ps[:, j % 2, :]
                pe.matmul(ps, m.choice_of(g, j), m.bias_parts[:, 0:2 * DIM], start=True, stop=False, skip_group_check=True)
                product(pe, ps, [(m.x_hi[j % 2][:, k, 0:P], m.x_lo[j % 2][:, k, 0:P], part(w, 2 * k), part(w, 2 * k + 1))
                                 for k in range(KC)], start=False).then_inc(m.up_done, 1)

            def transpose_h(g, j):
                n = GROUP * g.n + j
                pe.wait_ge(m.gated, SHARED + n + 1)
                pe.wait_ge(m.h_split, SHARED + n)
                for k in range(KC):
                    last = pe.transpose(m.ht_bank[:, k], m.h[j % 2][:, 0, k * P:(k + 1) * P], ident[:])
                last.then_inc(m.ht_ps, 1)

            def down(g, j, w):
                n = GROUP * g.n + j
                hi, lo = (part(w, 2 * KC + n).rearrange("p (k c) -> p k c", k=KC) for n in range(2))
                pe.wait_ge(m.h_split, SHARED + n + 1)
                pe.wait_ge(m.y_done, SHARED + n)
                product(pe, m.y_ps_bank[:, 0], [(m.h_hi[j % 2][:, k, 0:P], m.h_lo[j % 2][:, k, 0:P], hi[:, k], lo[:, k])
                                                for k in range(KC)], stop=False)
                pe.matmul(m.y_ps_bank[:, 0], m.choice_of(g, j), m.bias_parts[:, 2 * DIM:], start=False, stop=True).then_inc(m.y_ps, 1)

            pe.wait_ge(m.slots_done, 2)
            pe.wait_ge(m.late_split, LATE_CHUNKS)
            for j in range(AHEAD):
                transpose_x(Block(0, 0, 0), j)

            def tiles_of(g, behind, ahead):
                offset = {j: weights(g.last(), j + GROUP) for j in (-2, -1) if behind}
                for j in range(GROUP):
                    offset[j] = weights(g, j)
                    up(g, j, offset[j])
                    at(g, j - 1, behind, ahead, transpose_h)
                    at(g, j + AHEAD, behind, ahead, transpose_x)
                    at(g, j - 2, behind, ahead, lambda group, tile: down(group, tile, offset[j - 2]))

            paired_blocks(pe, GROUPS, tiles_of)
            transpose_h(final_group, GROUP - 1)
            for j in (GROUP - 2, GROUP - 1):
                down(final_group, j, weights(final_group, j))

        class ParameterSignals(TokenSignals):
            small_in = sem("p_small_in")
            bias_round = sem("p_bias_round")
            bias_split = sem("p_bias_split")

        class FeedForward(ParameterSignals):

            def __init__(self, scope, w_raw):
                self.norm1 = sb(scope, "f_norm1", [P, 2, DIM])
                self.stats1 = sb(scope, "f_stats1", [P, MT, 6])
                self.mv1 = sb(scope, "f_mv1", [P, MT, 2])
                self.var1 = sb(scope, "f_var1", [P, MT])
                self.rstd1 = sb(scope, "f_rstd1", [P, MT])
                self.x1 = [w_raw[:, KC * z:KC * (z + 1)].rearrange("p i (k c) -> p (i k) c", k=KC) for z in range(2)]
                self.up_ps = PSUM[:, 0:4, :]
                self.y_ps_bank = PSUM[:, 4:6, :]
                self.xt_bank = PSUM[:, 6:8, :]
                self.base = BATCH
                self.const_done = sem("f_const_done")
                self.y_sum = sem("f_y_sum")
                self.bn2_done = sem("f_bn2_done")
                self.agg2_done = sem("f_agg2_done")
                self.ln2_stats = sem("f_ln2_stats")
                self.agg1_done = sem("f_agg1_done")
                self.ln2_rstd = sem("f_ln2_rstd")
                self.out_scaled = sem("f_out_scaled")
                self.out_ready = sem("f_out_ready")
                self.x_done = sem("f_x_done")
                self.x1_scaled = sem("f_x1_scaled")
                self.up_done = sem("f_up_done")
                self.gelu_done = sem("f_gelu_done")
                self.h_round = sem("f_h_round")
                self.h_split = sem("f_h_split")
                self.y_ps = sem("f_y_ps")

            def later_buffers(self, scope):
                two, four = range(2), range(4)
                self.norm2 = sb(scope, "f_norm2", [P, 2, DIM])
                self.out_g = sb(scope, "f_out_g", [P, DIM])
                self.out_b = sb(scope, "f_out_b", [P, DIM])
                self.bias_raw = sb(scope, "f_bias_raw", [1, DIM])
                self.bias_hi = sb(scope, "f_bias_hi", [1, DIM], F32R)
                self.bias_lo = sb(scope, "f_bias_lo", [1, DIM], F32R)
                self.stats2 = sb(scope, "f_stats2", [P, MT, 6])
                self.mv2 = sb(scope, "f_mv2", [P, MT, 2])
                self.var2 = sb(scope, "f_var2", [P, MT])
                self.rstd2 = sb(scope, "f_rstd2", [P, MT])
                self.y = sb(scope, "f_y", [P, MT, DIM])
                self.x_hi = [sb(scope, f"f_x_hi{z}", [P, KC, MN], F32R) for z in two]
                self.x_lo = [sb(scope, f"f_x_lo{z}", [P, KC, MN], F32R) for z in two]
                self.h = [sb(scope, f"f_h{z}", [P, MN]) for z in four]
                self.h_hi = [sb(scope, f"f_h_hi{z}", [P, MN], F32R) for z in four]
                self.h_lo = [sb(scope, f"f_h_lo{z}", [P, MN], F32R) for z in four]

        def ffn_on_scalar(act, f):
            ternary_first = Block(0, 0, 0, w.base)

            def tokens_rounded(b):
                act.wait_ge(f.xt_ps, b.count + 1)
                act.activation(f.x_hi[b.z][:], f.xt_bank, ACT.Copy).then_inc(f.x_round, 1)

            act.wait_ge(a1.y_done, 2 * BATCH + 1)
            act.wait_ge(side_split, 2 * BATCH)
            act.dma_start(f.bias_raw[:], d["bias"][2:3]).then_inc(f.small_in, 16)
            act.dma_start(f.norm2[:].rearrange("p r c -> p (r c)"),
                          d["norms"][2:4].rearrange("r c -> (r c)").partition_broadcast(P)).then_inc(f.small_in, 16)
            for dst, src in ((w.b1[:], d["ter_b1"].partition_broadcast(2)), (w.b2[:], d["ter_b2"].partition_broadcast(P)),
                             (w.g2[:], d["ter_g2"].partition_broadcast(P))):
                act.dma_start(dst, src).then_inc(w.ter_in, 16)
            tokens_rounded(Block(0, 0, 0, f.base))
            act.wait_ge(f.small_in, 48)
            act.activation(f.bias_hi[:], f.bias_raw[:], ACT.Copy).then_inc(f.bias_round, 1)
            act.activation(f.out_g[:], f.norm2[:, 0], ACT.Copy, scale=gates[:, 1:2])
            act.activation(f.out_b[:], f.norm2[:, 1], ACT.Copy, scale=gates[:, 1:2]).then_inc(f.const_done, 1)

            def body(b, behind, ahead):
                for m in range(HC):
                    at = HC * b.n + m
                    act.wait_ge(f.up_done, at + 1)
                    after(act, f.h_split, at - 3)
                    act.activation(f.h[m % 4][:], f.up_ps[:, m % 4], ACT.Gelu,
                                   bias=cols[:, COL_FB1 + m:COL_FB1 + m + 1]).then_inc(f.gelu_done, 1)
                    act.wait_ge(f.gelu_done, at + 1)
                    act.activation(f.h_hi[m % 4][:], f.h[m % 4][:], ACT.Copy).then_inc(f.h_round, 1)
                    if m == HC - 1 and ahead:
                        tokens_rounded(b.next())
                    if m == 0 and not ahead:
                        ternary_rows_on_scalar(act, w)
                    if m >= HC - KC and not ahead:
                        x_affine(act, w, ternary_first, m - (HC - KC))
                if not ahead:
                    x_rounded(act, w, ternary_first)

            paired_blocks(act, MB, body, f.base)

        def ffn_on_gpsimd(pool, f):
            def norm_1(b):
                pool.wait_ge(f.ln_stats, b.count + 1)
                pool.tensor_tensor(f.rstd1[:], f.var1[:], neghalf[:, 0:MT], ALU.pow).then_inc(f.ln_rstd, 1)

            def norm_2(b):
                pool.wait_ge(f.ln2_stats, b.n + 1)
                pool.tensor_tensor(f.rstd2[:], f.var2[:], neghalf[:, 0:MT], ALU.pow).then_inc(f.ln2_rstd, 1)

            norm_1(Block(0, 0, 0, f.base))

            def body(b, behind, ahead):
                for m in range(HC):
                    at = HC * b.n + m
                    if m == 1 and behind:
                        norm_2(b.last())
                    if m == HC // 2 and not ahead:
                        ternary_inverse_std(pool, w, Block(0, 0, 0, w.base))
                    if m == 1 and ahead:
                        norm_1(b.next())
                    pool.wait_ge(f.h_round, at + 1)
                    pool.tensor_tensor(f.h_lo[m % 4][:], f.h[m % 4][:], f.h_hi[m % 4][:].bitcast(F32),
                                       ALU.subtract).then_inc(f.h_split, 1)

            paired_blocks(pool, MB, body, f.base)
            final = Block(MB - 1, 1, (MB - 2) // 2, f.base)
            norm_2(final)

        def stats_1(dve, f, b):
            for t in range(MT):
                last = dve.bn_stats(f.stats1[:, t, :], z_sum[:, bass.ds(MT * b.n + t, 1), :])
            last.then_inc(f.bn_done, 1)

        def aggregate_1(dve, f, b):
            if isinstance(b.n, int):
                dve.wait_ge(f.bn_done, b.count + 1)
            for t in range(MT):
                last = dve.bn_aggr(f.mv1[:, t, :], f.stats1[:, t, :])
            last.then_inc(f.agg1_done, 1)
            dve.wait_ge(f.agg1_done, b.n + 1)
            dve.tensor_scalar(f.var1[:], f.mv1[:, :, 1], EPS, None, ALU.add).then_inc(f.ln_stats, 1)

        def apply_1(dve, f, b):
            after(dve, f.y_sum, b.n - 1)
            for t in range(MT):
                last = dve.scalar_tensor_tensor(f.x1[b.z][:, t, :], z_sum[:, bass.ds(MT * b.n + t, 1), :].rearrange("p o c -> p (o c)"),
                                                f.mv1[:, t, 0:1], f.norm1[:, 0], ALU.subtract, ALU.mult)
            last.then_inc(f.x1_scaled, 1)
            dve.wait_ge(f.x1_scaled, b.n + 1)
            dve.wait_ge(f.ln_rstd, b.count + 1)
            for t in range(MT):
                last = dve.scalar_tensor_tensor(f.x1[b.z][:, t, :], f.x1[b.z][:, t, :], f.rstd1[:, t:t + 1], f.norm1[:, 1],
                                                ALU.mult, ALU.add)
            last.then_inc(f.ln_done, 1)

        def ffn_first_stats_on_vector(dve, f):
            stats_1(dve, f, Block(0, 0, 0, f.base))
            aggregate_1(dve, f, Block(0, 0, 0, f.base))

        def ffn_first_norm_on_vector(dve, f):
            dve.wait_ge(f.small_in, 16)
            apply_1(dve, f, Block(0, 0, 0, f.base))

        def ffn_on_vector(dve, f):
            def x_residue(b):
                dve.wait_ge(f.x_round, b.count + 1)
                dve.tensor_tensor(f.x_lo[b.z][:], f.xt_bank, f.x_hi[b.z][:].bitcast(F32),
                                  ALU.subtract).then_inc(f.x_split, 1)

            def sums(b):
                dve.wait_ge(f.y_ps, b.n + 1)
                if isinstance(b.n, int):
                    after(dve, f.x_done, b.n)
                else:
                    dve.wait_ge(f.x_split, b.count + 2)
                dve.tensor_tensor(f.y[:].rearrange("p t c -> p (t c)"), f.y_ps_bank.rearrange("p b n -> p (b n)"),
                                  f.x1[b.z][:].rearrange("p t c -> p (t c)"), ALU.add).then_inc(f.y_sum, 1)
                dve.wait_ge(f.y_sum, b.n + 1)
                for t in range(MT):
                    last = dve.bn_stats(f.stats2[:, t, :], f.y[:, t])
                last.then_inc(f.bn2_done, 1)

            def aggregate_2(b, covered):
                if not covered:
                    dve.wait_ge(f.bn2_done, b.n + 1)
                for t in range(MT):
                    last = dve.bn_aggr(f.mv2[:, t, :], f.stats2[:, t, :])
                last.then_inc(f.agg2_done, 1)
                dve.wait_ge(f.agg2_done, b.n + 1)
                dve.tensor_scalar(f.var2[:], f.mv2[:, :, 1], EPS, None, ALU.add).then_inc(f.ln2_stats, 1)

            def apply_2(b):
                for t in range(MT):
                    last = dve.scalar_tensor_tensor(f.y[:, t], f.y[:, t], f.mv2[:, t, 0:1], f.out_g[:], ALU.subtract, ALU.mult)
                last.then_inc(f.out_scaled, 1)
                dve.wait_ge(f.out_scaled, b.n + 1)
                dve.wait_ge(f.ln2_rstd, b.n + 1)
                for t in range(MT):
                    last = dve.scalar_tensor_tensor(f.y[:, t], f.y[:, t], f.rstd2[:, t:t + 1], f.out_b[:], ALU.mult, ALU.add)
                last.then_inc(f.out_ready, 1)

            def residual(b):
                dve.wait_ge(f.out_ready, b.n + 1)
                xb = x[:, bass.ds(MT * b.n, MT), :]
                dve.tensor_tensor(xb, xb, f.y[:], ALU.add).then_inc(f.x_done, 1)

            first = Block(0, 0, 0, f.base)
            x_residue(first)
            dve.wait_ge(f.bias_round, 1)
            dve.tensor_tensor(f.bias_lo[:], f.bias_raw[:], f.bias_hi[:].bitcast(F32), ALU.subtract).then_inc(f.bias_split, 1)
            dve.wait_ge(f.const_done, 1)

            def body(b, behind, ahead):
                if behind:
                    sums(b.last())
                if ahead:
                    if behind:
                        dve.wait_ge(f.bn2_done, b.n)
                    stats_1(dve, f, b.next())
                if behind:
                    aggregate_2(b.last(), ahead)
                if ahead:
                    aggregate_1(dve, f, b.next())
                    apply_1(dve, f, b.next())
                if behind:
                    apply_2(b.last())
                    residual(b.last())
                if not behind:
                    ternary_weights_on_vector(dve, w)
                if ahead:
                    x_residue(b.next())
                else:
                    first = Block(0, 0, 0, w.base)
                    ternary_stats(dve, w, first)
                    ternary_aggregate(dve, w, first)
                    ternary_norm(dve, w, first)
                    ternary_rows_on_vector(dve, w)
                    ternary_residue(dve, w, first)

            paired_blocks(dve, MB, body, f.base)
            final = Block(MB - 1, 1, (MB - 2) // 2, f.base)
            sums(final)
            aggregate_2(final, False)
            apply_2(final)
            residual(final)

        def ffn_on_tensor(pe, f):
            w1 = [both[:, 0:KC * HID].rearrange("p (k n) -> p k n", k=KC) for both in (ffn_hi, ffn_lo)]
            w2 = [both[:, KC * HID:].rearrange("p (k n) -> p k n", k=HC) for both in (ffn_hi, ffn_lo)]

            def transpose_x(b):
                pe.wait_ge(f.ln_done, b.count + 1)
                after(pe, f.x_split, b.count)
                for k in range(KC):
                    for t in range(MT):
                        last = pe.transpose(f.xt_bank[:, k, t * P:(t + 1) * P], f.x1[b.z][:, t, k * P:(k + 1) * P], ident[:])
                last.then_inc(f.xt_ps, 1)

            def up(b, m):
                part = slice(m * P, (m + 1) * P)
                pe.wait_ge(f.x_split, b.count + 1)
                after(pe, f.gelu_done, HC * b.n + m - 3)
                product(pe, f.up_ps[:, m % 4], [(w1[0][:, k, part], w1[1][:, k, part], f.x_hi[b.z][:, k], f.x_lo[b.z][:, k])
                                                for k in range(KC)]).then_inc(f.up_done, 1)

            def down(b, m):
                if m == 0:
                    after(pe, f.y_sum, b.n)
                    for half in range(2):
                        for n, part in enumerate((f.bias_hi, f.bias_lo)):
                            pe.matmul(f.y_ps_bank[:, half].rearrange("p (t c) -> p t c", c=DIM), ones_r[0:1, :],
                                      part[:].unsqueeze(1).broadcast_to([1, 2, DIM]), start=n == 0, stop=False,
                                      skip_group_check=True)
                pe.wait_ge(f.h_split, HC * b.n + m + 1)
                for t in range(MT):
                    part = slice(t * P, (t + 1) * P)
                    last = product(pe, f.y_ps_bank[:, t // 2, t % 2 * DIM:(t % 2 + 1) * DIM],
                                   [(f.h_hi[m % 4][:, part], f.h_lo[m % 4][:, part], w2[0][:, m], w2[1][:, m])],
                                   start=False, stop=m == HC - 1)
                if m == HC - 1:
                    last.then_inc(f.y_ps, 1)

            pe.wait_ge(side_split, 2 * BATCH)
            pe.wait_ge(a1.y_done, 2 * BATCH + 1)
            transpose_x(Block(0, 0, 0, f.base))

            def body(b, behind, ahead):
                up(b, 0)
                up(b, 1)
                for m in range(2, HC):
                    up(b, m)
                    if m == 2 and not behind:
                        pe.wait_ge(f.bias_split, 1)
                    down(b, m - 2)
                    if m == HC - 3 and not behind:
                        ternary_weights_on_tensor(pe, w)
                    if m >= HC - KC and not ahead:
                        ternary_transpose(pe, w, Block(0, 0, 0, w.base), m - (HC - KC))
                if not behind:
                    pe.wait_ge(w.size_done, 1)
                if ahead:
                    transpose_x(b.next())
                down(b, HC - 2)
                down(b, HC - 1)

            paired_blocks(pe, MB, body, f.base)

        class Ternary(ParameterSignals):

            def __init__(self, scope):
                self.raw = sb(scope, "t_raw", [P, 2, TER_COLS])
                self.code = sb(scope, "t_code", [P, 2, TER_COLS], F32R)
                self.b1 = sb(scope, "t_b1", [2, HID])
                self.b1_parts = sb(scope, "t_b1_parts", [2, HID], F32R)
                self.b2 = sb(scope, "t_b2", [P, DIM])
                self.g2 = sb(scope, "t_g2", [P, HID])
                self.stats1 = sb(scope, "t_stats1", [P, MT, 6])
                self.mv1 = sb(scope, "t_mv1", [P, MT, 2])
                self.var1 = sb(scope, "t_var1", [P, MT])
                self.rstd1 = sb(scope, "t_rstd1", [P, MT])
                self.sums = sb(scope, "t_sums", [P, 2])
                self.size = sb(scope, "t_size", [P, 2])
                self.scale = sb(scope, "t_scale", [P, 2])
                self.gate = sb(scope, "t_gate", [P, 1])
                self.neg_gate = sb(scope, "t_neg_gate", [P, 1])
                self.base = BATCH + MB
                self.raw_in = sem("r_raw_in")
                self.ter_in = sem("r_ter_in")
                self.sums_done = sem("r_sums_done")
                self.total_ps = sem("r_total_ps")
                self.size_done = sem("r_size_done")
                self.code_done = sem("r_code_done")
                self.scale_done = sem("r_scale_done")
                self.bias_scaled = sem("r_bias_scaled")
                self.rows_round = sem("r_rows_round")
                self.rows_split = sem("r_rows_split")
                self.rows_ps = sem("r_rows_ps")
                self.rows_done = sem("r_rows_done")
                self.agg1_done = sem("r_agg1_done")
                self.xk_ps = sem("r_xk_ps")
                self.x_affine = sem("r_x_affine")
                self.up_done = sem("r_up_done")
                self.gelu_done = sem("r_gelu_done")
                self.gh_done = sem("r_gh_done")
                self.bn2_done = sem("r_bn2_done")
                self.agg2_done = sem("r_agg2_done")
                self.norm_step = sem("r_norm_step")
                self.rg_done = sem("r_rg_done")
                self.ht_ps = sem("r_ht_ps")
                self.h_round = sem("r_h_round")
                self.h_split = sem("r_h_split")
                self.y_ps = sem("r_y_ps")
                self.centred = sem("r_centred")
                self.x_shift = sem("r_x_shift")
                self.x_done = sem("r_x_done")

            def work_buffers(self, work):
                two, four = range(2), range(4)
                self.rows_hi = sb(work, "t_rows_hi", [P, 2, HC, P], F32R)
                self.rows_lo = sb(work, "t_rows_lo", [P, 2, HC, P], F32R)
                self.xn = sb(work, "t_xn", [P, MT, DIM])
                self.xa = sb(work, "t_xa", [P, KC, MN])
                self.x_hi = [sb(work, "t_x_hi0", [P, KC, MN], F32R)]
                self.x_lo = [sb(work, "t_x_lo0", [P, KC, MN], F32R)]
                self.x_hi.append(sb(work, "t_x_hi1", [P, KC, MN], F32R))
                self.x_lo.append(sb(work, "t_x_lo1", [P, KC, MN], F32R))
                self.mean_row = sb(work, "t_mean_row", [P, DIM])
                self.shift_row = sb(work, "t_shift_row", [P, DIM])
                self.y = sb(work, "t_y", [P, DIM])
                self.h = [sb(work, f"t_h{z}", [P, HID]) for z in two]
                self.gh = [sb(work, f"t_gh{z}", [P, HID]) for z in two]
                self.stats2 = [sb(work, f"t_stats2{z}", [P, 2, 6]) for z in four]
                self.mv2 = [sb(work, f"t_mv2{z}", [P, 2]) for z in four]
                self.var2 = [sb(work, f"t_var2{z}", [P, 1]) for z in four]
                self.rstd2 = [sb(work, f"t_rstd2{z}", [P, 1]) for z in four]
                self.rg = [sb(work, f"t_rg{z}", [P, 1]) for z in four]
                self.h_hi = [sb(work, f"t_h_hi{z}", [P, HC, P], F32R) for z in two]
                self.h_lo = [sb(work, f"t_h_lo{z}", [P, HC, P], F32R) for z in two]
                self.up_ps = PSUM[:, 0:4, :].rearrange("p (z b) n -> p z b n", z=2)
                self.ht_bank = PSUM[:, 4:6, :]
                self.y_bank = PSUM[:, 6, 0:DIM]
                self.xt_bank = PSUM[:, 7, :]
                self.rows_ps_bank = PSUM[:, 6:8, 0:DIM]
                self.total = PSUM[:, 7, 0:2]

        def ternary_weights_on_tensor(pe, w):
            pe.wait_ge(w.sums_done, 1)
            pe.matmul(w.total, ones[:], w.sums[:], start=True, stop=True).then_inc(w.total_ps, 1)

        def ternary_weights_on_vector(dve, w):
            count = [0]

            def step(instruction):
                count[0] += 1
                instruction.then_inc(w.code_done, 1)
                dve.wait_ge(w.code_done, count[0])

            dve.wait_ge(w.raw_in, 32)
            for n in range(2):
                last = dve.tensor_reduce(w.sums[:, n:n + 1], w.raw[:, n], AX.X, ALU.add, apply_absolute_value=True)
            last.then_inc(w.sums_done, 1)
            dve.wait_ge(w.total_ps, 1)
            dve.tensor_scalar(w.size[:], w.total, 1.0 / (HID * DIM), 1e-5, ALU.mult, ALU.max).then_inc(w.size_done, 1)
            dve.wait_ge(w.size_done, 1)
            step(dve.reciprocal(w.scale[:], w.size[:]))
            for n in range(2):
                step(dve.tensor_scalar(w.raw[:, n], w.raw[:, n], w.scale[:, n:n + 1], -1.0, ALU.mult, ALU.max))
                step(dve.tensor_scalar(w.raw[:, n], w.raw[:, n], 1.0, ROUND, ALU.min, ALU.add))
                step(dve.tensor_scalar(w.code[:, n], w.raw[:, n], ROUND, None, ALU.subtract))
            step(dve.reciprocal(w.size[:], w.scale[:]))
            step(dve.tensor_scalar(w.gate[:], w.size[:, 1:2], gates[:, 3:4], None, ALU.mult))
            dve.tensor_scalar(w.neg_gate[:], w.gate[:], -1.0, None, ALU.mult).then_inc(w.scale_done, 1)
            dve.wait_ge(w.ter_in, 48)
            dve.tensor_scalar(w.b1[:], w.b1[:], w.scale[0:2, 0:1], None, ALU.mult).then_inc(w.bias_scaled, 1)

        def ternary_rows_on_scalar(act, w):
            for n, col in enumerate((COL_G2, COL_T2)):
                last = act.activation(w.rows_hi[:, n], cols[:, col:col + HC].unsqueeze(2).broadcast_to([P, HC, P]), ACT.Copy)
            last.then_inc(w.rows_round, 1)
            act.wait_ge(w.bias_scaled, 1)
            act.activation(w.b1_parts[:], w.b1[:], ACT.Copy).then_inc(w.bias_round, 1)

        def ternary_rows_on_vector(dve, w):
            dve.wait_ge(w.rows_round, 1)
            for n, col in enumerate((COL_G2, COL_T2)):
                last = dve.tensor_tensor(w.rows_lo[:, n], cols[:, col:col + HC].unsqueeze(2).broadcast_to([P, HC, P]),
                                         w.rows_hi[:, n].bitcast(F32), ALU.subtract)
            last.then_inc(w.rows_split, 1)
            dve.wait_ge(w.bias_round, 2)
            dve.tensor_tensor(w.b1[:], w.b1[:], w.b1_parts[:].bitcast(F32), ALU.subtract).then_inc(w.bias_scaled, 1)
            dve.wait_ge(w.bias_scaled, 2)
            dve.tensor_scalar(w.b1[:], w.b1[:], ident[0:2, 1:2], None, ALU.mult).then_inc(w.bias_scaled, 1)
            dve.wait_ge(w.bias_scaled, 3)
            dve.scalar_tensor_tensor(w.b1_parts[:], w.b1_parts[:].bitcast(F32), ident[0:2, 0:1], w.b1[:], ALU.mult,
                                     ALU.add).then_inc(w.bias_split, 1)

        def x_affine(act, w, b, k):
            act.wait_ge(w.xk_ps, KC * b.n + k + 1)
            if k == 0:
                after(act, w.x_split, b.count)
            act.activation(w.xa[:, k], w.xt_bank, ACT.Identity, scale=cols[:, COL_G1 + k:COL_G1 + k + 1],
                           bias=cols[:, COL_T1 + k:COL_T1 + k + 1]).then_inc(w.x_affine, 1)

        def x_rounded(act, w, b):
            act.wait_ge(w.x_affine, KC * (b.n + 1))
            act.activation(w.x_hi[b.z][:], w.xa[:], ACT.Copy).then_inc(w.x_round, 1)

        def ternary_on_scalar(act, w):
            act.wait_ge(f.y_ps, MB)

            def gelu(b, t):
                at = MT * b.n + t
                act.wait_ge(w.up_done, at + 1)
                after(act, w.gh_done, at - 1)
                after(act, w.bn2_done, at - 1)
                act.activation(w.h[t % 2][:], w.up_ps[:, t % 2].rearrange("p b n -> p (b n)"), ACT.Gelu,
                               scale=w.size[:, 0:1]).then_inc(w.gelu_done, 1)

            def rounded(b, t):
                at = MT * b.n + t
                act.wait_ge(w.ht_ps, at + 1)
                after(act, w.y_ps, at - 1)
                act.activation(w.h_hi[t % 2][:], w.ht_bank.rearrange("p b (k n) -> p (b k) n", n=P),
                               ACT.Copy).then_inc(w.h_round, 1)

            def body(b, behind, ahead):
                for t in range(MT):
                    if t == 3 and ahead:
                        x_affine(act, w, b.next(), 1)
                        x_rounded(act, w, b.next())
                    gelu(b, t)
                    if t == 2 and ahead:
                        x_affine(act, w, b.next(), 0)
                    if t >= 1:
                        rounded(b, t - 1)
                    elif behind:
                        rounded(b.last(), MT - 1)

            paired_blocks(act, MB, body, w.base)
            rounded(Block(MB - 1, 1, (MB - 2) // 2, w.base), MT - 1)

        def ternary_inverse_std(pool, w, b):
            pool.wait_ge(w.ln_stats, b.count + 1)
            pool.tensor_tensor(w.rstd1[:], w.var1[:], neghalf[:, 0:MT], ALU.pow).then_inc(w.ln_rstd, 1)

        def ternary_on_gpsimd(pool, w):

            def scale_h(b, t):
                at = MT * b.n + t
                pool.wait_ge(w.gelu_done, at + 1)
                after(pool, w.ht_ps, at - 1)
                pool.tensor_tensor(w.gh[t % 2][:], w.h[t % 2][:], w.g2[:], ALU.mult).then_inc(w.gh_done, 1)

            def norm_2(b, t):
                at = MT * b.n + t
                pool.wait_ge(w.agg2_done, at + 1)
                pool.tensor_tensor(w.var2[t][:], w.mv2[t][:, 1:2], eps_tile[:, 0:1], ALU.add).then_inc(w.norm_step, 1)
                pool.wait_ge(w.norm_step, 2 * at + 1)
                pool.tensor_tensor(w.rstd2[t][:], w.var2[t][:], neghalf[:, 0:1], ALU.pow).then_inc(w.norm_step, 1)
                pool.wait_ge(w.norm_step, 2 * at + 2)
                pool.tensor_tensor(w.rg[t][:], w.rstd2[t][:], w.neg_gate[:], ALU.mult).then_inc(w.rg_done, 1)

            def shift(b, half):
                pool.wait_ge(w.ln_done, b.count + 1)
                xb = x[:, bass.ds(MT * b.n + half * MT // 2, MT // 2), :]
                pool.tensor_tensor(xb, xb, w.shift_row[:].unsqueeze(1).broadcast_to([P, MT // 2, DIM]),
                                   ALU.add).then_inc(w.x_shift, 1)

            pool.wait_ge(w.ter_in, 48)
            def body(b, behind, ahead):
                for t in range(MT):
                    scale_h(b, t)
                    if t >= 1:
                        norm_2(b, t - 1)
                    elif behind:
                        norm_2(b.last(), MT - 1)
                    if t == 0 and ahead:
                        ternary_inverse_std(pool, w, b.next())
                    if t == 1 and not behind:
                        pool.wait_ge(w.rows_done, 2)
                    if t in (1, 2):
                        shift(b, t - 1)

            paired_blocks(pool, MB, body, w.base)
            norm_2(Block(MB - 1, 1, (MB - 2) // 2, w.base), MT - 1)

        def ternary_stats(dve, w, b):
            for t in range(MT):
                last = dve.bn_stats(w.stats1[:, t, :], x[:, bass.ds(MT * b.n + t, 1), :])
            last.then_inc(w.bn_done, 1)

        def ternary_aggregate(dve, w, b):
            if isinstance(b.n, int):
                dve.wait_ge(w.bn_done, b.count + 1)
            for t in range(MT):
                last = dve.bn_aggr(w.mv1[:, t, :], w.stats1[:, t, :])
            last.then_inc(w.agg1_done, 1)
            dve.wait_ge(w.agg1_done, b.n + 1)
            dve.tensor_scalar(w.var1[:], w.mv1[:, :, 1], 1.0 + EPS, EPS * EPS, ALU.mult, ALU.add).then_inc(w.ln_stats, 1)

        def ternary_norm(dve, w, b):
            dve.wait_ge(w.ln_rstd, b.count + 1)
            after(dve, w.xk_ps, KC * b.n)
            for t in range(MT):
                last = dve.tensor_scalar(w.xn[:, t, :], x[:, bass.ds(MT * b.n + t, 1), :].rearrange("p o c -> p (o c)"),
                                         w.mv1[:, t, 0:1], w.rstd1[:, t:t + 1], ALU.subtract, ALU.mult)
            last.then_inc(w.ln_done, 1)

        def ternary_residue(dve, w, b):
            dve.wait_ge(w.x_round, b.count + 1)
            dve.tensor_tensor(w.x_lo[b.z][:], w.xa[:], w.x_hi[b.z][:].bitcast(F32), ALU.subtract).then_inc(w.x_split, 1)

        def ternary_on_vector(dve, w):
            def stats_2(b, t):
                at = MT * b.n + t
                dve.wait_ge(w.gelu_done, at + 1)
                for c in range(2):
                    last = dve.bn_stats(w.stats2[t][:, c], w.h[t % 2][:, c * 512:(c + 1) * 512])
                last.then_inc(w.bn2_done, 1)

            def aggregate_2(b, t):
                if isinstance(b.n, int):
                    dve.wait_ge(w.bn2_done, MT * b.n + t + 1)
                dve.bn_aggr(w.mv2[t][:], w.stats2[t][:].rearrange("p c s -> p (c s)")).then_inc(w.agg2_done, 1)

            def residue(b, t):
                dve.wait_ge(w.h_round, MT * b.n + t + 1)
                dve.tensor_tensor(w.h_lo[t % 2][:], w.ht_bank.rearrange("p b (k n) -> p (b k) n", n=P),
                                  w.h_hi[t % 2][:].bitcast(F32), ALU.subtract).then_inc(w.h_split, 1)

            def residual(b, t):
                at = MT * b.n + t
                dve.wait_ge(w.y_ps, at + 1)
                dve.wait_ge(w.rg_done, at + 1)
                after(dve, w.x_done, at)
                dve.scalar_tensor_tensor(w.y[:], w.mean_row[:], w.mv2[t][:, 0:1], w.y_bank, ALU.mult,
                                         ALU.subtract).then_inc(w.centred, 1)
                dve.wait_ge(w.centred, at + 1)
                if t % 2 == 0:
                    dve.wait_ge(w.x_shift, 2 * b.n + t // 2 + 1)
                xt = x[:, bass.ds(at, 1), :].rearrange("p o c -> p (o c)")
                dve.scalar_tensor_tensor(xt, w.y[:], w.rg[t][:], xt, ALU.mult, ALU.add).then_inc(w.x_done, 1)

            dve.wait_ge(f.x_done, MB)
            dve.wait_ge(w.rows_ps, 1)
            dve.tensor_copy(w.mean_row[:], w.rows_ps_bank[:, 0])
            dve.tensor_scalar(w.shift_row[:], w.b2[:], gates[:, 3:4], None, ALU.mult).then_inc(w.rows_done, 1)
            dve.wait_ge(w.rows_done, 1)
            dve.scalar_tensor_tensor(w.shift_row[:], w.rows_ps_bank[:, 1], w.gate[:], w.shift_row[:], ALU.mult,
                                     ALU.add).then_inc(w.rows_done, 1)

            def body(b, behind, ahead):
                for t in range(MT):
                    if t == 3 and ahead:
                        ternary_residue(dve, w, b.next())
                    stats_2(b, t)
                    if t == 0 and ahead:
                        ternary_stats(dve, w, b.next())
                    if t >= 1:
                        residue(b, t - 1)
                    elif behind:
                        residue(b.last(), MT - 1)
                    if t == 1 and ahead:
                        ternary_norm(dve, w, b.next())
                    if t >= 2:
                        residual(b, t - 2)
                    elif behind:
                        residual(b.last(), t - 2 + MT)
                    aggregate_2(b, t)
                    if t == 0 and ahead:
                        ternary_aggregate(dve, w, b.next())

            paired_blocks(dve, MB, body, w.base)
            final = Block(MB - 1, 1, (MB - 2) // 2, w.base)
            residue(final, MT - 1)
            residual(final, MT - 2)
            residual(final, MT - 1)

        def ternary_transpose(pe, w, b, k):
            if k == 0:
                pe.wait_ge(w.ln_done, b.count + 1)
            after(pe, w.x_affine, KC * b.n + k)
            for t in range(MT):
                last = pe.transpose(w.xt_bank[:, t * P:(t + 1) * P], w.xn[:, t, k * P:(k + 1) * P], ident[:])
            last.then_inc(w.xk_ps, 1)

        def ternary_on_tensor(pe, w):
            w1 = w.code[:, 0].rearrange("p (k n) -> p k n", k=KC)
            w2 = w.code[:, 1].rearrange("p (k n) -> p k n", k=HC)

            def up(b, t):
                part = slice(t * P, (t + 1) * P)
                pe.wait_ge(w.x_split, b.count + 1)
                after(pe, w.gelu_done, MT * b.n + t - 1)
                for c in range(2):
                    n = slice(c * 512, (c + 1) * 512)
                    ps = w.up_ps[:, t % 2, c]
                    pe.matmul(ps, ones_r[0:2, :], w.b1_parts[:, n], start=True, stop=False)
                    for k in range(KC):
                        pe.matmul(ps, w.x_hi[b.z][:, k, part], w1[:, k, n], start=False, stop=False)
                        last = pe.matmul(ps, w.x_lo[b.z][:, k, part], w1[:, k, n], start=False, stop=k == KC - 1)
                last.then_inc(w.up_done, 1)

            def transpose_h(b, t):
                at = MT * b.n + t
                pe.wait_ge(w.gh_done, at + 1)
                if isinstance(b.n, int) and at == 0:
                    pe.wait_ge(f.y_sum, MB)
                after(pe, w.h_split, at)
                for k in range(HC):
                    last = pe.transpose(w.ht_bank[:, k // 4, k % 4 * P:(k % 4 + 1) * P], w.gh[t % 2][:, k * P:(k + 1) * P], ident[:])
                last.then_inc(w.ht_ps, 1)

            def down(b, t):
                at = MT * b.n + t
                pe.wait_ge(w.h_split, at + 1)
                after(pe, w.x_done, at)
                for k in range(HC):
                    pe.matmul(w.y_bank, w.h_hi[t % 2][:, k], w2[:, k], start=k == 0, stop=False)
                    last = pe.matmul(w.y_bank, w.h_lo[t % 2][:, k], w2[:, k], start=False, stop=k == HC - 1)
                last.then_inc(w.y_ps, 1)

            def rows():
                pe.wait_ge(w.rows_split, 1)
                pe.wait_ge(w.x_affine, KC)
                for n in range(2):
                    for k in range(HC):
                        pe.matmul(w.rows_ps_bank[:, n], w.rows_hi[:, n, k], w2[:, k], start=k == 0, stop=False)
                        last = pe.matmul(w.rows_ps_bank[:, n], w.rows_lo[:, n, k], w2[:, k], start=False, stop=k == HC - 1)
                last.then_inc(w.rows_ps, 1)

            pe.wait_ge(w.scale_done, 1)
            pe.wait_ge(w.bias_split, 2)

            def body(b, behind, ahead):
                for t in range(MT):
                    if t == 3 and ahead:
                        ternary_transpose(pe, w, b.next(), 1)
                    up(b, t)
                    if t == 1 and not behind:
                        rows()
                    if t == 2 and ahead:
                        if not behind:
                            pe.wait_ge(w.rows_done, 2)
                        ternary_transpose(pe, w, b.next(), 0)
                    if t >= 1:
                        transpose_h(b, t - 1)
                    elif behind:
                        transpose_h(b.last(), MT - 1)
                    if t >= 2:
                        down(b, t - 2)
                    elif behind:
                        down(b.last(), t - 2 + MT)

            paired_blocks(pe, MB, body, w.base)
            final = Block(MB - 1, 1, (MB - 2) // 2, w.base)
            transpose_h(final, MT - 1)
            down(final, MT - 2)
            down(final, MT - 1)

        weight_scope = root.enter_context(ExitStack())
        moe_w = sb(weight_scope, "moe_w", [P, (EXPERTS + 1) * EXPERT_COLS], F32R)
        weight_scope.close()
        early_scope = root.enter_context(ExitStack())
        sb(early_scope, "moe_early_place", [P, EARLY_CHUNKS * 2 * MOE_CHUNK], F32R)
        zeros = sb(early_scope, "zeros", [P, DIM])
        moe_raw = [sb(early_scope, f"moe_raw{z}", [P, MOE_CHUNK]) for z in range(2)]
        a0 = Attention(0, early_scope)
        early_scope.close()
        mix_scope = root.enter_context(ExitStack())
        mix = Mixture(mix_scope)
        mix_scope.close()

        layer1_scope = root.enter_context(ExitStack())
        z_sum = sb(layer1_scope, "z_sum", [P, TILES, DIM])
        ffn_hi = sb(layer1_scope, "ffn_hi", [P, FFN_COLS], F32R)
        ffn_lo = sb(layer1_scope, "ffn_lo", [P, FFN_COLS], F32R)
        a1_w_raw = sb(layer1_scope, "a1_w_raw", [P, 4, MATRIX])
        f = FeedForward(layer1_scope, a1_w_raw)
        att1_scope = layer1_scope.enter_context(ExitStack())
        ffn_raw = [sb(att1_scope, f"ffn_raw{z}", [P, FFN_CHUNK]) for z in range(2)]
        a1 = Attention(1, att1_scope, z_sum, a1_w_raw)
        att1_scope.close()
        f.later_buffers(layer1_scope)
        w = Ternary(layer1_scope)
        layer1_scope.close()
        w.work_buffers(root)

        side_in = [sem(f"side_in{z}") for z in range(2)]
        side_round = sem("side_round")
        side_split = sem("side_split")
        zeros_out = sem("zeros_out")
        out_done = sem("out_done")
        WA_ORDER = (1, 2, 0, 3)

        block = root.enter_context(nc.Block())

        @block.sync
        def _(sp):
            def load(a, b):
                if a.stage == 0:
                    after(sp, a.x_in[b.z], 16 * b.half)
                    sp.dma_start(tiles(b), x_dram[:, bass.ds(BT * b.n, BT), :]).then_inc(a.x_in[b.z], 16)
                after(sp, a.ctx_split, b.count - 1)
                sp.dma_start(a.ctx[b.z][:], ctx_dram[bass.ds(b.n, 1)].rearrange("o p k n -> p (o k) n")).then_inc(a.ctx_in[b.z], 16)

            def spread(a, b):
                sp.wait_ge(a.x_split, b.count + 1)
                values = a.v[b.z][:].rearrange("k (m h) n -> k m h n", m=KC)
                for h, key, keys, c, row in value_pieces():
                    at = column_of(c) + (h - heads_of(c)[0]) * VW
                    sp.dma_start(a.v_diagonal[b.z][row:row + keys, :, at:at + VW],
                                 values[key:key + keys, :, h]).then_inc(a.v_spread[b.z], 16)

            def load_moe(b):
                after(sp, side_split, b.count - 1)
                sp.dma_start(moe_raw[b.z][:], d["moe_w"][:, bass.ds(b.n * MOE_CHUNK, MOE_CHUNK)]).then_inc(side_in[b.z], 16)

            for n in range(2):
                load(a0, Block(n, n, 0))
            sp.wait_ge(pool_const, 6)

            def clear(b, count=ZERO_TILES):
                sp.dma_start(d["sorted_x"].rearrange("(t p) c -> p t c", p=P)[:, bass.ds(ZERO_TILES * b.n, count), :],
                             zeros[:].unsqueeze(1).broadcast_to([P, count, DIM])).then_inc(zeros_out, 16)

            load_moe(Block(0, 0, 0))
            sp.wait_ge(a0.v_ones, 2)
            spread(a0, Block(0, 0, 0))

            def body(b, behind, ahead):
                if ahead > 1:
                    load(a0, b.next().next())
                if ahead:
                    load_moe(b.next())
                    spread(a0, b.next())
                clear(b)

            paired_blocks(sp, BATCH, body, 0, 3)
            clear(Block(BATCH, 0, BATCH // 2), SORTED - ZERO_TILES * BATCH)
            mixture_on_sync(sp, mix)
            sp.wait_ge(mix.y_done, SHARED + SORTED)
            def load_ffn(b):
                after(sp, side_split, b.count - 1)
                sp.dma_start(ffn_raw[b.z][:], d["ffn_w"][:, bass.ds(b.n * FFN_CHUNK, FFN_CHUNK)]).then_inc(side_in[b.z], 16)

            for n in range(2):
                load(a1, Block(n, n, 0, a1.base))
            load_ffn(Block(0, 0, 0, a1.base))
            sp.wait_ge(a1.v_ones, 4)
            spread(a1, Block(0, 0, 0, a1.base))

            def body(b, behind, ahead):
                if ahead > 1:
                    load(a1, b.next().next())
                if ahead:
                    load_ffn(b.next())
                    spread(a1, b.next())

            paired_blocks(sp, BATCH, body, a1.base, 3)
            sp.wait_ge(a1.y_done, 2 * BATCH + 1)
            sp.wait_ge(side_split, 2 * BATCH)
            for n, name in enumerate(("ter_w1", "ter_w2")):
                sp.dma_start(w.raw[:, n], d[name]).then_inc(w.raw_in, 16)
            for b in range(BATCH):
                sp.wait_ge(w.x_done, BT * (b + 1))
                sp.dma_start(out_dram[:, BT * b:BT * (b + 1), :], x[:, BT * b:BT * (b + 1), :]).then_inc(out_done, 16)
            sp.wait_ge(out_done, 16 * BATCH)

        @block.gpsimd
        def _(pool):
            pool.memset(ident[:], 0.0).then_inc(pool_const, 1)
            pool.memset(headmask[:], 1.0).then_inc(pool_const, 1)
            pool.memset(ones[:], 1.0).then_inc(pool_const, 1)
            pool.memset(neghalf[:], -0.5)
            pool.memset(eps_tile[:], EPS).then_inc(pool_const, 1)
            pool.memset(a0.mask_raw[:], 0.0).then_inc(pool_const, 1)
            pool.memset(zeros[:], 0.0).then_inc(pool_const, 1)
            pool.wait_ge(pool_const, 6)
            pool.affine_select(out=ident[:], in_=ident[:], compare_op=ALU.not_equal, fill=1.0, base=0,
                               pattern=[[-1, P]], channel_multiplier=1).then_inc(pool_const, 1)
            pool.affine_select(out=headmask[:], in_=headmask[:], compare_op=ALU.is_ge, fill=0.0, base=0,
                               pattern=[[-HD, HPC]], channel_multiplier=1).then_inc(pool_const, 1)
            pool.wait_ge(pool_const, 8)
            pool.affine_select(out=headmask[:], in_=headmask[:], compare_op=ALU.is_ge, fill=0.0, base=HD - 1,
                               pattern=[[HD, HPC]], channel_multiplier=-1).then_inc(pool_const, 1)
            pool.wait_ge(pool_const, 9)

            def split_moe(b):
                hi, lo = (moe_w[:, bass.ds((2 * b.n + part) * MOE_CHUNK, MOE_CHUNK)] for part in range(2))
                pool.wait_ge(side_in[b.z], 16 * (b.half + 1))
                pool.tensor_tensor(hi, moe_raw[b.z][:], one([P, MOE_CHUNK]), ALU.mult).then_inc(side_round, 1)
                pool.wait_ge(side_round, b.n + 1)
                pool.tensor_tensor(lo, moe_raw[b.z][:], hi.bitcast(F32), ALU.subtract).then_inc(side_split, 1)

            attention_on_gpsimd(pool, a0, None, split_moe)
            mixture_on_gpsimd(pool, mix)

            def split_ffn(b):
                part = bass.ds(b.n * FFN_CHUNK, FFN_CHUNK)
                pool.wait_ge(side_in[b.z], 16 * (b.half + b.base // 2 + 1))
                pool.tensor_tensor(ffn_hi[:, part], ffn_raw[b.z][:], one([P, FFN_CHUNK]), ALU.mult).then_inc(side_round, 1)
                pool.wait_ge(side_round, b.count + 1)
                pool.tensor_tensor(ffn_lo[:, part], ffn_raw[b.z][:], ffn_hi[:, part].bitcast(F32),
                                   ALU.subtract).then_inc(side_split, 1)

            pool.wait_ge(mix.y_done, SHARED + SORTED)
            for z in range(2):
                pool.wait_ge(mix.tile_out[z], 16 * GROUPS // 2)
            pool.memset(a1.mask_raw, 1.0)
            attention_on_gpsimd(pool, a1, z_sum, split_ffn)
            ffn_on_gpsimd(pool, f)
            ternary_on_gpsimd(pool, w)

        @block.scalar
        def _(act):
            act.dma_start(a0.w_raw[:, 1], d["wa0"][:, 1]).then_inc(a0.w_in[1], 16)
            act.dma_start(a0.w_raw[:, 2], d["wa0"][:, 2]).then_inc(a0.w_in[2], 16)
            act.dma_start(cols[:], d["cols"]).then_inc(consts_in, 16)
            act.dma_start(a0.bv[:], d["bv"][0].partition_broadcast(CTXP)).then_inc(a0.small_in, 16)
            act.dma_start(a0.w_raw[:, 0], d["wa0"][:, 0]).then_inc(a0.w_in[0], 16)
            act.dma_start(a0.bias_raw[:], d["bias"][0:1]).then_inc(a0.small_in, 16)
            act.dma_start(gates_raw[:], d["gates"].partition_broadcast(P)).then_inc(consts_in, 16)
            act.wait_ge(pool_const, 5)
            act.dma_start(a0.mask_raw[:, :, 0:CTX], d["mask_q"].rearrange("(t p) n -> p t n", p=P)).then_inc(a0.mask_in, 16)
            act.dma_start(a0.w_raw[:, 3], d["wa0"][:, 3]).then_inc(a0.w_in[3], 16)
            for n, i in enumerate(WA_ORDER):
                act.wait_ge(a0.w_in[i], 16)
                act.activation(a0.w_hi[:, i].rearrange("p k n -> p (k n)"), a0.w_raw[:, i], ACT.Copy).then_inc(a0.w_round, 1)
                if n == 0:
                    act.wait_ge(consts_in, 32)
                    act.wait_ge(a0.small_in, 32)
                    act.activation(a0.bias_hi[:], a0.bias_raw[:], ACT.Copy).then_inc(a0.bias_round, 1)
                    act.activation(gates[:], gates_raw[:], ACT.Tanh).then_inc(gates_done, 1)
            attention_on_scalar(act, a0)
            mixture_on_scalar(act, mix)
            act.wait_ge(mix.y_done, SHARED + SORTED)
            for i in WA_ORDER:
                act.dma_start(a1.w_raw[:, i], d["wa1"][:, i]).then_inc(a1.w_in[i], 16)
            act.dma_start(a1.bv[:], d["bv"][1].partition_broadcast(CTXP)).then_inc(a1.small_in, 16)
            act.dma_start(a1.bias_raw[:], d["bias"][1:2]).then_inc(a1.small_in, 16)
            act.dma_start(a1.mask_u8[:], d["mask_k"]).then_inc(a1.mask_in, 16)
            act.dma_start(f.norm1[:].rearrange("p r c -> p (r c)"),
                          d["norms"][0:2].rearrange("r c -> (r c)").partition_broadcast(P)).then_inc(f.small_in, 16)
            for n, i in enumerate(WA_ORDER):
                act.wait_ge(a1.w_in[i], 32)
                act.activation(a1.w_hi[:, i].rearrange("p k n -> p (k n)"), a1.w_raw[:, i], ACT.Copy).then_inc(a1.w_round, 1)
                if n == 0:
                    act.wait_ge(a1.small_in, 64)
                    act.activation(a1.bias_hi[:], a1.bias_raw[:], ACT.Copy).then_inc(a1.bias_round, 1)
            attention_on_scalar(act, a1)
            ffn_on_scalar(act, f)
            ternary_on_scalar(act, w)

        @block.vector
        def _(dve):
            dve.wait_ge(pool_const, 9)
            dve.tensor_copy(a0.ident[:], ident[:]).then_inc(a0.y_done, 1)
            dve.tensor_copy(ones_r[:], ones[:]).then_inc(consts_done, 1)
            dve.wait_ge(a0.bias_round, 1)
            dve.tensor_tensor(a0.bias_lo[:], a0.bias_raw[:], a0.bias_hi[:].bitcast(F32), ALU.subtract).then_inc(a0.bias_split, 1)
            for n, i in enumerate(WA_ORDER):
                dve.wait_ge(a0.w_round, n + 1)
                dve.tensor_tensor(a0.w_lo[:, i].rearrange("p k n -> p (k n)"), a0.w_raw[:, i],
                                  a0.w_hi[:, i].bitcast(F32).rearrange("p k n -> p (k n)"), ALU.subtract).then_inc(a0.w_split, 1)
            dve.wait_ge(a0.mask_in, 16)
            dve.tensor_scalar(a0.mask[:], a0.mask_raw[:], 0.0, MASKED, ALU.is_equal, ALU.mult).then_inc(a0.mask_done, 1)
            attention_on_vector(dve, a0, None)
            mixture_on_vector(dve, mix)
            dve.wait_ge(mix.y_done, SHARED + SORTED)
            dve.wait_ge(a1.bias_round, 2)
            dve.tensor_tensor(a1.bias_lo[:], a1.bias_raw[:], a1.bias_hi[:].bitcast(F32), ALU.subtract).then_inc(a1.bias_split, 1)
            for n, i in enumerate(WA_ORDER):
                dve.wait_ge(a1.w_round, 4 + n + 1)
                dve.tensor_tensor(a1.w_lo[:, i].rearrange("p k n -> p (k n)"), a1.w_raw[:, i],
                                  a1.w_hi[:, i].bitcast(F32).rearrange("p k n -> p (k n)"), ALU.subtract).then_inc(a1.w_split, 1)
            dve.wait_ge(a1.mask_in, 32)
            dve.wait_ge(a1.v_ones, 4)
            dve.tensor_copy(a1.mask_raw[:, :, 0:CTX], a1.mask_u8[:]).then_inc(a1.mask_cast, 1)
            dve.wait_ge(a1.mask_cast, 1)
            dve.tensor_scalar(a1.mask[:], a1.mask_raw, MASKED, None, ALU.mult).then_inc(a1.mask_done, 1)
            attention_on_vector(dve, a1, z_sum, lambda: ffn_first_stats_on_vector(dve, f), lambda: ffn_first_norm_on_vector(dve, f))
            ffn_on_vector(dve, f)
            ternary_on_vector(dve, w)

        @block.tensor
        def _(pe):
            attention_on_tensor(pe, a0)
            mixture_on_tensor(pe, mix)
            attention_on_tensor(pe, a1)
            ffn_on_tensor(pe, f)
            ternary_on_tensor(pe, w)


_SHAPE = (BATCH, SEQ, DIM)


def kernel(**inputs):
    import concourse.bacc as bacc
    from concourse.bass_utils import run_bass_kernel_spmd

    nc = bacc.Bacc("TRN2", target_bir_lowering=False, num_devices=1)
    arrays = lay_out({k: np.asarray(v) for k, v in inputs.items()})
    d = {n: nc.dram_tensor(n, a.shape, mybir.dt.from_np(a.dtype), kind="ExternalInput").ap() for n, a in arrays.items()}
    out = nc.dram_tensor("y", _SHAPE, F32, kind="ExternalOutput").ap()
    flamingo_kernel(nc, d, out)
    r = run_bass_kernel_spmd(nc, [arrays], core_ids=[0])
    return r.results[0]["y"]
```
